# Optimizing a Trainium2 kernel written in Bass

```python
import numpy as np
import jax
import jax.numpy as jnp

def _softmax(x, axis=-1):
    return jax.nn.softmax(x, axis=axis)

def _gelu(x):
    return jax.nn.gelu(x, approximate=True)

def _silu(x):
    return jax.nn.silu(x)

def _sigmoid(x):
    return jax.nn.sigmoid(x)

def _layernorm(x, axis=-1, eps=1e-05):
    m = jnp.mean(x, axis=axis, keepdims=True)
    v = jnp.var(x, axis=axis, keepdims=True)
    return (x - m) / jnp.sqrt(v + eps)

def _scatter_add(tgt, idx, src, axis=0):
    return tgt.at[idx].add(src)

def _segment_sum(src, seg, n):
    return jax.ops.segment_sum(src, seg, n)
kernel_name = 'mk_cond_seq_d2_seqx_r4_e733ab'

def setup_inputs(seed: int=0):
    np.random.seed(seed)
    _w = jnp.asarray

    def _rec_inputs():
        import jax
        import jax.numpy as jnp
        _rk = jax.random.key(seed)
        x = 1.648e-05 + 1 * jax.random.normal(jax.random.fold_in(_rk, 1), (64, 64, 288), jnp.float32)
        _lenS = 64 - jax.random.randint(jax.random.fold_in(_rk, 7), (64,), 0, max(1, 64 // 4) + 1, jnp.int32)
        _lenS2 = 64 - jax.random.randint(jax.random.fold_in(_rk, 8), (64,), 0, max(1, 64 // 4) + 1, jnp.int32)
        cond_1152 = 0.00914911 + 1.00357 * jax.random.normal(jax.random.fold_in(_rk, 11), (64, 288), jnp.float32)
        return (x, cond_1152)
    x, cond_1152 = _rec_inputs()

    def _L0_cond_setup():
        import jax, jax.numpy as jnp
        import numpy as np
        B, L, C = (8, 256, 288)
        H = 16
        D = C // H
        FF = int(C * 4.0)
        EPS = 1e-06

        def _layernorm(x):
            mu = jnp.mean(x, axis=-1, keepdims=True)
            var = jnp.mean(jnp.square(x - mu), axis=-1, keepdims=True)
            return (x - mu) * jax.lax.rsqrt(var + EPS)

        def _modulate(x, shift, scale):
            return x * (1.0 + scale) + shift

        def _attention(h, W_qkv, b_qkv, W_proj, b_proj):
            b, l, c = h.shape
            qkv = h @ W_qkv + b_qkv
            qkv = qkv.reshape(b, l, 3, H, D)
            q, k, v = (qkv[:, :, 0], qkv[:, :, 1], qkv[:, :, 2])
            scale = D ** (-0.5)
            scores = jnp.einsum('blhd,bmhd->bhlm', q * scale, k)
            attn = jax.nn.softmax(scores, axis=-1)
            o = jnp.einsum('bhlm,bmhd->blhd', attn, v).reshape(b, l, c)
            return o @ W_proj + b_proj
        key = jax.random.key(seed)
        ks = jax.random.split(key, 12)
        s = 0.02
        return {'x': jax.random.normal(ks[0], (B, L, C), jnp.float32), 'c': jax.random.normal(ks[1], (B, 1, C), jnp.float32), 'W_qkv': jax.random.normal(ks[2], (C, 3 * C), jnp.float32) * s, 'b_qkv': jnp.zeros((3 * C,), jnp.float32), 'W_proj': jax.random.normal(ks[3], (C, C), jnp.float32) * s, 'b_proj': jnp.zeros((C,), jnp.float32), 'W_fc1': jax.random.normal(ks[4], (C, FF), jnp.float32) * s, 'b_fc1': jnp.zeros((FF,), jnp.float32), 'W_fc2': jax.random.normal(ks[5], (FF, C), jnp.float32) * s, 'b_fc2': jnp.zeros((C,), jnp.float32), 'W_ada': jax.random.normal(ks[6], (C, 6 * C), jnp.float32) * s, 'b_ada': jnp.zeros((6 * C,), jnp.float32)}
    _L0_cond_all = _L0_cond_setup()
    _L0_cond_in = {k: v for k, v in _L0_cond_all.items() if k in ('W_qkv', 'b_qkv', 'W_proj', 'b_proj', 'W_fc1', 'b_fc1', 'W_fc2', 'b_fc2', 'W_ada', 'b_ada')}
    del _L0_cond_all

    def _L1_cond_setup():
        import jax, jax.numpy as jnp
        import numpy as np
        from jax.scipy.linalg import expm
        N, D, COND_DIM = (288, 64, 288)
        B, T = (16, 256)

        def _rotation(cond, W, b):
            v = jax.nn.silu(cond) @ W.T + b
            iu, ju = jnp.triu_indices(D, k=1)
            A = jnp.zeros((cond.shape[0], D, D), dtype=v.dtype)
            A = A.at[:, iu, ju].set(v).at[:, ju, iu].set(-v)
            return expm(A)
        key = jax.random.key(seed)
        k1, k2, k3, k4, k5 = jax.random.split(key, 5)
        x = jax.random.normal(k1, (B, T, N), dtype=jnp.float32)
        cond = jax.random.normal(k2, (B, COND_DIM), dtype=jnp.float32)
        P = jax.random.normal(k3, (N, D), dtype=jnp.float32)
        n_skew = D * (D - 1) // 2
        bound = 1.0 / np.sqrt(COND_DIM)
        W = jax.random.uniform(k4, (n_skew, COND_DIM), minval=-bound, maxval=bound, dtype=jnp.float32)
        b = jax.random.uniform(k5, (n_skew,), minval=-bound, maxval=bound, dtype=jnp.float32)
        return {'x': x, 'cond': cond, 'P': P, 'W': W, 'b': b}
    _L1_cond_all = _L1_cond_setup()
    _L1_cond_in = {k: v for k, v in _L1_cond_all.items() if k in ('P', 'W', 'b')}
    del _L1_cond_all
    return {'x': x, 'cond_1152': cond_1152, 'L0_cond_W_qkv': _L0_cond_in['W_qkv'], 'L0_cond_b_qkv': _L0_cond_in['b_qkv'], 'L0_cond_W_proj': _L0_cond_in['W_proj'], 'L0_cond_b_proj': _L0_cond_in['b_proj'], 'L0_cond_W_fc1': _L0_cond_in['W_fc1'], 'L0_cond_b_fc1': _L0_cond_in['b_fc1'], 'L0_cond_W_fc2': _L0_cond_in['W_fc2'], 'L0_cond_b_fc2': _L0_cond_in['b_fc2'], 'L0_cond_W_ada': _L0_cond_in['W_ada'], 'L0_cond_b_ada': _L0_cond_in['b_ada'], 'L1_cond_P': _L1_cond_in['P'], 'L1_cond_W': _L1_cond_in['W'], 'L1_cond_b': _L1_cond_in['b']}

def reference(x, cond_1152, L0_cond_W_qkv, L0_cond_b_qkv, L0_cond_W_proj, L0_cond_b_proj, L0_cond_W_fc1, L0_cond_b_fc1, L0_cond_W_fc2, L0_cond_b_fc2, L0_cond_W_ada, L0_cond_b_ada, L1_cond_P, L1_cond_W, L1_cond_b):
    import jax
    import jax.numpy as jnp

    def _L0_cond_ref(x, c, W_qkv, b_qkv, W_proj, b_proj, W_fc1, b_fc1, W_fc2, b_fc2, W_ada, b_ada):
        import jax, jax.numpy as jnp
        import numpy as np
        B, L, C = (8, 256, 288)
        H = 16
        D = C // H
        FF = int(C * 4.0)
        EPS = 1e-06

        def _layernorm(x):
            mu = jnp.mean(x, axis=-1, keepdims=True)
            var = jnp.mean(jnp.square(x - mu), axis=-1, keepdims=True)
            return (x - mu) * jax.lax.rsqrt(var + EPS)

        def _modulate(x, shift, scale):
            return x * (1.0 + scale) + shift

        def _attention(h, W_qkv, b_qkv, W_proj, b_proj):
            b, l, c = h.shape
            qkv = h @ W_qkv + b_qkv
            qkv = qkv.reshape(b, l, 3, H, D)
            q, k, v = (qkv[:, :, 0], qkv[:, :, 1], qkv[:, :, 2])
            scale = D ** (-0.5)
            scores = jnp.einsum('blhd,bmhd->bhlm', q * scale, k)
            attn = jax.nn.softmax(scores, axis=-1)
            o = jnp.einsum('bhlm,bmhd->blhd', attn, v).reshape(b, l, c)
            return o @ W_proj + b_proj
        ada = jax.nn.silu(c) @ W_ada + b_ada
        shift_msa, scale_msa, gate_msa, shift_mlp, scale_mlp, gate_mlp = jnp.split(ada, 6, axis=-1)
        h = _modulate(_layernorm(x), shift_msa, scale_msa)
        x = x + gate_msa * _attention(h, W_qkv, b_qkv, W_proj, b_proj)
        h = _modulate(_layernorm(x), shift_mlp, scale_mlp)
        mlp = jax.nn.gelu(h @ W_fc1 + b_fc1, approximate=True) @ W_fc2 + b_fc2
        x = x + gate_mlp * mlp
        return x

    def _L1_cond_ref(x, cond, P, W, b):
        import jax, jax.numpy as jnp
        import numpy as np
        from jax.scipy.linalg import expm
        N, D, COND_DIM = (288, 64, 288)
        B, T = (16, 256)

        def _rotation(cond, W, b):
            v = jax.nn.silu(cond) @ W.T + b
            iu, ju = jnp.triu_indices(D, k=1)
            A = jnp.zeros((cond.shape[0], D, D), dtype=v.dtype)
            A = A.at[:, iu, ju].set(v).at[:, ju, iu].set(-v)
            return expm(A)
        U, _ = jnp.linalg.qr(P)
        R = _rotation(cond, W, b)
        z = jnp.einsum('btn,nd->btd', x, U)
        z_rot = jnp.einsum('btd,bde->bte', z, R)
        x_rot = x + jnp.einsum('btd,nd->btn', z_rot - z, U)
        return x_rot
    x = _L0_cond_ref(x, cond_1152[:, None, :], L0_cond_W_qkv, L0_cond_b_qkv, L0_cond_W_proj, L0_cond_b_proj, L0_cond_W_fc1, L0_cond_b_fc1, L0_cond_W_fc2, L0_cond_b_fc2, L0_cond_W_ada, L0_cond_b_ada)
    x = _L1_cond_ref(x, cond_1152, L1_cond_P, L1_cond_W, L1_cond_b)
    return x

_drawn_inputs = setup_inputs


def setup_inputs(seed=0):
    import zlib

    import numpy as np

    out = dict(_drawn_inputs(seed))
    spreads = {'L0_cond_b_qkv': (0.0, 0.8),
     'L0_cond_b_proj': (0.0, 0.351),
     'L0_cond_b_fc1': (0.0, 0.8),
     'L0_cond_b_fc2': (0.0, 0.367),
     'L0_cond_b_ada': (0.0, 0.396)}
    factors = {'L0_cond_W_qkv': 7.974, 'L0_cond_W_proj': 5.311}
    for name, (base, spread) in spreads.items():
        noise = np.random.default_rng([zlib.crc32(name.encode()), seed]).standard_normal(out[name].shape)
        drawn = base * np.exp(spread * noise) if base else spread * noise
        out[name] = jnp.asarray(drawn.astype(out[name].dtype))
    for name, factor in factors.items():
        out[name] = (out[name] * factor).astype(out[name].dtype)
    return out
```

```python
from contextlib import ExitStack

import concourse.bass as bass
from concourse import mybir

ALU = mybir.AluOpType
ACT = mybir.ActivationFunctionType
AX_X = mybir.AxisListType.X
F32 = mybir.dt.float32
F32R = mybir.dt.float32r

P = 128
B, L, C = 64, 64, 288
H = 16
D = C // H
DP = 32
FF = 4 * C
FT = FF // P
RK = 64
NV = RK * (RK - 1) // 2
PAIRS = B // 2
GP = 4
GROUPS = PAIRS // GP
GB = 2 * GP
TG = GP * P
CR = C - 2 * P
CD = 2 * P + 3 * CR
KR = 3 * CR + 2
EPS = 1e-6
SCALE = float(D) ** -0.5
SQUARINGS = 8
ELIM_ATT, ELIM_MLP = 5, 3
BANK = 512


def offset_of_row(i):
    return i * (RK - 1) - i * (i - 1) // 2


class Memory:

    def __init__(self, nc, ctx):
        self.nc, self.ctx = nc, ctx

    def sb(self, name, shape, dt=F32):
        return self.ctx.enter_context(self.nc.sbuf_tensor(name, shape, dt))

    def banks(self, prefix, n):
        return [self.ctx.enter_context(self.nc.psum_tensor(f"{prefix}{i}", [P, BANK], F32)) for i in range(n)]

    def sem(self, name):
        return self.ctx.enter_context(self.nc.semaphore(name))


def setup(nc, mem, st, io):
    with ExitStack() as ctx:
        m = Memory(nc, ctx)
        ps = m.banks("setup_ps", 8)
        cond = m.sb("cond", [B, C])
        e_neg = m.sb("e_neg", [B, C])
        silu = m.sb("silu", [B, C])
        silu_t = m.sb("silu_t", [P, 2, B])
        silu_r = m.sb("silu_r", [CR + 1, B])
        w_ada = m.sb("w_ada", [P, 3, 6 * C])
        ada = m.sb("ada", [B, 6, C])
        mod = m.sb("mod", [B, 4, CD])
        NL1 = NV // 16
        w_l1 = m.sb("w_l1", [NL1, 16, C])
        w_l1t = m.sb("w_l1t", [P, 3, NV])
        vec = m.sb("vec", [B, NV])
        upper = m.sb("upper", [B, RK, RK])
        skewed = m.sb("skewed", [B, RK, RK])

        ld_c, ld_ada, ld_l1, ld_p, ld_x = m.sem("ld_c"), m.sem("ld_ada"), m.sem("ld_l1"), m.sem("ld_p"), m.sem("ld_x")
        consts = m.sem("consts")
        silu_step = m.sem("silu_step")
        pe_done = m.sem("pe_done")
        dve_done = m.sem("dve_done")
        act_done = m.sem("act_done")
        spread = m.sem("spread")
        zeroed = m.sem("zeroed")
        gates_out = m.sem("gates_out")
        skew_out = m.sem("skew_out")
        skew_in = m.sem("skew_in")
        low_done = m.sem("low_done")

        block = ctx.enter_context(nc.Block())

        @block.sync
        def _(sp):
            sp.dma_start(cond[:], io["cond_1152"]).then_inc(ld_c, 16)
            sp.dma_start(w_ada[:, 0:2, :], io["L0_cond_W_ada"][0:2 * P, :].rearrange("(t p) n -> p t n", p=P)).then_inc(ld_ada, 16)
            sp.dma_start(w_ada[0:CR, 2, :], io["L0_cond_W_ada"][2 * P:C, :]).then_inc(ld_ada, 16)
            sp.dma_start(w_ada[CR:CR + 1, 2, :], io["L0_cond_b_ada"].rearrange("(a n) -> a n", a=1)).then_inc(ld_ada, 16)
            sp.dma_start(w_l1[:], io["L1_cond_W"].rearrange("(t p) c -> p t c", p=NL1)).then_inc(ld_l1, 16)
            sp.dma_start(w_l1t[CR:CR + 1, 2, :], io["L1_cond_b"].rearrange("(a n) -> a n", a=1)).then_inc(ld_l1, 16)
            sp.dma_start(st.p_c[:], io["L1_cond_P"].rearrange("(t p) n -> p t n", p=96)).then_inc(ld_p, 16)
            sp.dma_start(st.elim[RK:P, 0:RK], io["L1_cond_P"][0:RK, :]).then_inc(ld_p, 16)
            sp.wait_ge(dve_done, 2)
            sp.dma_start(io["gates"], ada[:, 2:6:3, :]).then_inc(gates_out, 16)
            sp.wait_ge(dve_done, 4)
            sp.dma_start(io["skew"], skewed[:]).then_inc(skew_out, 16)
            sp.wait_ge(skew_out, 16)
            for b in range(2):
                sp.dma_start(st.skew[RK * b:RK * (b + 1), :, :],
                             io["skew"].rearrange("(q b) i j -> b i q j", b=2)[b]).then_inc(skew_in, 16)
            sp.wait_ge(gates_out, 16)
            sp.wait_ge(skew_in, 32)
            sp.wait_ge(ld_x, 16 * GROUPS)

        @block.gpsimd
        def _(pool):
            pool.memset(st.ident[:], 0.0).then_inc(consts, 1)
            pool.wait_ge(consts, 1)
            pool.memset(st.ident2[:], 0.0).then_inc(consts, 1)
            pool.wait_ge(consts, 2)
            pool.memset(st.below[:], -1.0).then_inc(consts, 1)
            pool.wait_ge(consts, 3)
            pool.memset(st.half1[:], 0.0).then_inc(consts, 1)
            pool.wait_ge(consts, 4)
            pool.memset(st.half2[:], 0.0).then_inc(consts, 1)
            pool.wait_ge(consts, 5)
            pool.memset(st.lowrow[:], 0.0).then_inc(consts, 1)
            pool.wait_ge(consts, 6)
            pool.affine_select(out=st.ident[:], in_=st.ident[:], compare_op=ALU.not_equal, fill=1.0, base=0,
                               pattern=[[-1, P]], channel_multiplier=1).then_inc(consts, 1)
            pool.wait_ge(consts, 7)
            pool.affine_select(out=st.ident2[:], in_=st.ident2[:], compare_op=ALU.not_equal, fill=1.0, base=0,
                               pattern=[[-1, RK]], channel_multiplier=1).then_inc(consts, 1)
            pool.wait_ge(consts, 8)
            pool.affine_select(out=st.ident2[:], in_=st.ident2[:], compare_op=ALU.not_equal, fill=1.0, base=-RK,
                               pattern=[[-1, RK]], channel_multiplier=1).then_inc(consts, 1)
            pool.wait_ge(consts, 9)
            pool.affine_select(out=st.below[0:RK, :], in_=st.below[0:RK, :], compare_op=ALU.is_gt, fill=0.0, base=0,
                               pattern=[[-1, RK]], channel_multiplier=1).then_inc(consts, 1)
            pool.wait_ge(consts, 10)
            pool.affine_select(out=st.below[RK:P, :], in_=st.below[RK:P, :], compare_op=ALU.is_gt, fill=0.0, base=0,
                               pattern=[[-1, RK]], channel_multiplier=1).then_inc(consts, 1)
            pool.wait_ge(consts, 11)
            pool.memset(st.half1[RK:P, :], 1.0).then_inc(consts, 1)
            pool.wait_ge(consts, 12)
            pool.memset(st.half2[RK:P, :], 2.0).then_inc(consts, 1)
            pool.wait_ge(consts, 13)
            pool.memset(st.lowrow[CR:2 * CR, 1:2], 1.0).then_inc(consts, 1)
            pool.wait_ge(consts, 14)
            pool.affine_select(out=st.lowrow[3 * CR:P, 1:2], in_=st.lowrow[3 * CR:P, 1:2], compare_op=ALU.not_equal,
                               fill=1.0, base=-1, pattern=[[0, 1]], channel_multiplier=1).then_inc(consts, 1)
            pool.wait_ge(consts, 15)
            pool.tensor_scalar(st.lowrow[:, 0:1], st.lowrow[:, 1:2], -1.0, 1.0, ALU.mult, ALU.add).then_inc(consts, 1)
            pool.wait_ge(consts, 16)
            pool.memset(st.ones[:], 1.0).then_inc(consts, 1)
            pool.wait_ge(consts, 17)
            pool.memset(st.ones_top[:], 0.0).then_inc(consts, 1)
            pool.wait_ge(consts, 18)
            pool.memset(st.ones_top[0:RK, :], 1.0).then_inc(consts, 1)
            pool.wait_ge(consts, 19)
            pool.memset(st.ones_low[:], 0.0).then_inc(consts, 1)
            pool.wait_ge(consts, 20)
            pool.memset(st.ones_low[RK:P, :], 1.0).then_inc(consts, 1)
            pool.wait_ge(consts, 21)
            pool.memset(st.minus_half[:], -0.5).then_inc(consts, 1)
            pool.wait_ge(consts, 22)
            pool.memset(st.powers[:, 0:1], 0.5).then_inc(consts, 1)
            pool.wait_ge(consts, 23)
            pool.memset(st.powers[:, 1:2], -1.0).then_inc(consts, 1)
            pool.wait_ge(consts, 24)
            pool.memset(silu_r[CR:CR + 1, :], 1.0).then_inc(consts, 1)
            pool.wait_ge(consts, 25)
            pool.memset(st.elim[:, RK:P], 0.0).then_inc(consts, 1)
            pool.wait_ge(consts, 26)
            pool.affine_select(out=st.elim[0:RK, RK:P], in_=st.elim[0:RK, RK:P], compare_op=ALU.not_equal, fill=1.0,
                               base=0, pattern=[[-1, RK]], channel_multiplier=1).then_inc(consts, 1)
            pool.memset(upper[:], 0.0).then_inc(zeroed, 1)
            pool.wait_ge(zeroed, 1)
            pool.wait_ge(dve_done, 3)
            for i in range(0, RK - 1, 2):
                a, n = offset_of_row(i), RK - 1 - i
                pool.tensor_copy(upper[:, i, i + 1:RK], vec[:, a:a + n]).then_inc(spread, 1)

        @block.scalar
        def _(act):
            for g in range(GROUPS):
                act.dma_start(st.x[:, g * GP:(g + 1) * GP, :],
                              io["x"].rearrange("(q b) l c -> (b l) q c", b=2)[:, g * GP:(g + 1) * GP, :]
                              ).then_inc(ld_x, 16)
            act.wait_ge(ld_c, 16)
            act.activation(e_neg[:], cond[:], ACT.Exp, scale=-1.0).then_inc(silu_step, 1)
            for n in range(12):
                if n % 2 == 0:
                    act.wait_ge(pe_done, 2 + 1 + n)
                    rows = P if n // 4 < 2 else CR
                    act.copy(w_l1t[0:rows, n // 4, (n % 4) * 4 * NL1:(n % 4 + 1) * 4 * NL1],
                             ps[n % 8][0:rows, 0:4 * NL1]).then_inc(act_done, 1)
            act.wait_ge(zeroed, 1)
            act.wait_ge(dve_done, 3)
            for i in range(1, RK - 1, 2):
                a, n = offset_of_row(i), RK - 1 - i
                act.copy(upper[:, i, i + 1:RK], vec[:, a:a + n]).then_inc(spread, 1)

        @block.vector
        def _(dve):
            dve.wait_ge(silu_step, 1)
            dve.tensor_scalar(e_neg[:], e_neg[:], 1.0, None, ALU.add).then_inc(silu_step, 1)
            dve.wait_ge(silu_step, 2)
            dve.reciprocal(silu[:], e_neg[:]).then_inc(silu_step, 1)
            dve.wait_ge(silu_step, 3)
            dve.tensor_tensor(silu[:], silu[:], cond[:], ALU.mult).then_inc(silu_step, 1)
            dve.wait_ge(pe_done, 1)
            dve.tensor_copy(silu_t[:], ps[0][:, 0:2 * B].rearrange("p (t b) -> p t b", b=B)).then_inc(dve_done, 1)
            dve.tensor_copy(silu_r[0:CR, :], ps[0][0:CR, 2 * B:3 * B]).then_inc(silu_step, 1)
            dve.wait_ge(pe_done, 2)
            ada_f = ada[:].rearrange("b s c -> b (s c)")
            for n in range(4):
                w = min(BANK, 6 * C - n * BANK)
                dve.tensor_copy(ada_f[:, n * BANK:n * BANK + w], ps[4 + n][0:B, 0:w]).then_inc(silu_step, 1)
            dve.wait_ge(silu_step, 9)
            for n, (s, plus) in enumerate(((0, 0.0), (1, 1.0), (3, 0.0), (4, 1.0))):
                dve.tensor_scalar(mod[:, n, 0:C], ada[:, s, :], plus, None, ALU.add).then_inc(silu_step, 1)
                dve.tensor_scalar(mod[:, n, C:CD].rearrange("b (r c) -> b r c", c=CR),
                                  ada[:, s, 2 * P:C].unsqueeze(1).to_broadcast([B, 2, CR]), plus, None,
                                  ALU.add).then_inc(silu_step, 1)
            dve.wait_ge(silu_step, 17)
            dve.tensor_copy(mod[0:1, 0, 0:1], mod[0:1, 0, 0:1]).then_inc(dve_done, 1)
            for n in range(12):
                if n % 2 == 1:
                    dve.wait_ge(pe_done, 2 + 1 + n)
                    rows = P if n // 4 < 2 else CR
                    dve.tensor_copy(w_l1t[0:rows, n // 4, (n % 4) * 4 * NL1:(n % 4 + 1) * 4 * NL1],
                                    ps[n % 8][0:rows, 0:4 * NL1]).then_inc(low_done, 1)
            dve.wait_ge(pe_done, 15)
            for n in range(4):
                dve.tensor_copy(st.mod_t[:, n, 0:2, :], ps[4][:, n * 2 * B:(n + 1) * 2 * B].rearrange("p (t b) -> p t b", b=B)
                                ).then_inc(silu_step, 1)
            dve.tensor_copy(st.mod_t[0:3 * CR, :, 2, :], ps[5][0:3 * CR, 0:4 * B].rearrange("p (n b) -> p n b", b=B)
                            ).then_inc(silu_step, 1)
            dve.wait_ge(pe_done, 16)
            for n in range(4):
                dve.tensor_scalar(vec[:, n * 4 * NL1:(n + 1) * 4 * NL1], ps[n][0:B, 0:4 * NL1],
                                  2.0 ** -SQUARINGS, None, ALU.mult).then_inc(silu_step, 1)
            dve.wait_ge(silu_step, 26)
            dve.tensor_copy(vec[0:1, 0:1], vec[0:1, 0:1]).then_inc(dve_done, 1)
            dve.wait_ge(spread, RK - 1)
            dve.tensor_tensor(skewed[:], upper[:], upper[:].rearrange("b i j -> b j i"), ALU.subtract).then_inc(dve_done, 1)
            dve.wait_ge(pe_done, 17)
            dve.tensor_copy(st.elim[0:RK, 0:RK], ps[6][0:RK, 0:RK]).then_inc(silu_step, 1)
            dve.tensor_copy(st.p_t[:], ps[7][0:RK, 0:C]).then_inc(silu_step, 1)

        @block.tensor
        def _(pe):
            pe.wait_ge(silu_step, 4)
            pe.wait_ge(consts, 27)
            for t in range(3):
                rows = P if t < 2 else CR
                mm = pe.transpose(ps[0][0:rows, t * B:(t + 1) * B], silu[:, t * P:t * P + rows], st.ident[0:B, 0:B])
            mm.then_inc(pe_done, 1)
            pe.wait_ge(dve_done, 1)
            pe.wait_ge(silu_step, 5)
            pe.wait_ge(ld_ada, 48)
            lhs = [silu_t[:, 0, :], silu_t[:, 1, :], silu_r[:, :]]
            for n in range(4):
                w = min(BANK, 6 * C - n * BANK)
                for t in range(3):
                    rows = P if t < 2 else CR + 1
                    mm = pe.matmul(ps[4 + n][0:B, 0:w], lhs[t], w_ada[0:rows, t, n * BANK:n * BANK + w],
                                   start=(t == 0), stop=(t == 2))
            mm.then_inc(pe_done, 1)
            pe.wait_ge(ld_l1, 32)
            pe.wait_ge(dve_done, 2)
            for n in range(12):
                t = n // 4
                rows = P if t < 2 else CR
                if n >= 8:
                    if n % 2 == 0:
                        pe.wait_ge(act_done, (n - 8) // 2 + 1)
                    else:
                        pe.wait_ge(low_done, (n - 8) // 2 + 1)
                for q in range(4):
                    r = (n % 4) * 4 + q
                    mm = pe.transpose(ps[n % 8][0:rows, q * NL1:(q + 1) * NL1], w_l1[:, r, t * P:t * P + rows],
                                      st.ident[0:NL1, 0:NL1])
                mm.then_inc(pe_done, 1)
            pe.wait_ge(act_done, 6)
            pe.wait_ge(low_done, 6)
            for n in range(4):
                for t in range(2):
                    mm = pe.transpose(ps[4][:, (2 * n + t) * B:(2 * n + t + 1) * B], mod[:, n, t * P:(t + 1) * P],
                                      st.ident[0:B, 0:B])
                mm = pe.transpose(ps[5][0:3 * CR, n * B:(n + 1) * B], mod[:, n, 2 * P:CD], st.ident[0:B, 0:B])
            mm.then_inc(pe_done, 1)
            for n in range(4):
                for t in range(3):
                    rows = P if t < 2 else CR + 1
                    mm = pe.matmul(ps[n][0:B, 0:4 * NL1], lhs[t], w_l1t[0:rows, t, n * 4 * NL1:(n + 1) * 4 * NL1],
                                   start=(t == 0), stop=(t == 2))
            mm.then_inc(pe_done, 1)
            pe.wait_ge(ld_p, 32)
            for t in range(3):
                pe.matmul(ps[6][0:RK, 0:RK], st.p_c[:, t, :], st.p_c[:, t, :], start=(t == 0), stop=(t == 2))
            for t in range(3):
                mm = pe.transpose(ps[7][0:RK, t * 96:(t + 1) * 96], st.p_c[:, t, :], st.ident[0:96, 0:96])
            mm.then_inc(pe_done, 1)


def split_weights(nc, st, io):
    with ExitStack() as ctx:
        m = Memory(nc, ctx)
        stage = m.sb("stage", [P, 3, FF])
        lows = m.sb("lows", [P, FF])
        stage2 = m.sb("stage2", [P, FT, C])
        bias2 = m.sb("bias2", [2, C])
        ld_w, hi_done, split_done = m.sem("ld_w"), m.sem("hi_done"), m.sem("split_done")
        low_done, zero_w = m.sem("low_done"), m.sem("zero_w")
        ld2, hi2, lo2 = m.sem("fc2_ld"), m.sem("fc2_hi"), m.sem("fc2_lo")

        block = ctx.enter_context(nc.Block())

        weights = [("qkv", io["L0_cond_W_qkv"], io["L0_cond_b_qkv"], 3 * C),
                   ("proj", io["L0_cond_W_proj"], io["L0_cond_b_proj"], C),
                   ("fc1", io["L0_cond_W_fc1"], io["L0_cond_b_fc1"], FF)]
        PER_W = 6 * 16

        def views(name):
            if name == "qkv":
                def heads(t, a):
                    return t[:, a:a + H * DP].rearrange("p (h d) -> p h d", d=DP)[:, :, 0:D]
                out = []
                for n in range(2):
                    a = n * H * DP
                    hi = [heads(st.wqk_hi[:, k, :], a) for k in range(2)]
                    lo = [heads(st.wqk_lo[:, k, :], a) for k in range(2)]
                    out.append((n * C, C, hi, lo, heads(st.wqk_r[:, :], a), D))
                out.append((2 * C, C, [st.wv_hi[:, k, :] for k in range(2)], [st.wv_lo[:, k, :] for k in range(2)],
                            st.wv_r[:, :], None))
                return out
            hi, lo, r = (st.wp_hi, st.wp_lo, st.wp_r) if name == "proj" else (st.w1_hi, st.w1_lo, st.w1_r)
            n = C if name == "proj" else FF
            return [(0, n, [hi[:, k, :] for k in range(2)], [lo[:, k, :] for k in range(2)], r[:, :], None)]

        @block.sync
        def _(sp):
            sp.dma_start(stage2[:], io["L0_cond_W_fc2"].rearrange("(t p) n -> p t n", p=P)).then_inc(ld2, 16)
            sp.dma_start(bias2[:], io["L0_cond_b_fc2"].rearrange("(a n) -> a n", a=1).to_broadcast([2, C])).then_inc(ld2, 16)

        @block.scalar
        def _(act):
            done = 0
            act.wait_ge(zero_w, 3)
            for w, (name, src, bias, cols) in enumerate(weights):
                if w:
                    act.wait_ge(split_done, done)
                for k in range(2):
                    act.dma_start(stage[:, k, 0:cols], src[k * P:(k + 1) * P, :]).then_inc(ld_w, 16)
                for k in range(3):
                    act.dma_start(stage[k * CR:(k + 1) * CR, 2, 0:cols], src[2 * P:C, :]).then_inc(ld_w, 16)
                act.dma_start(stage[3 * CR:KR, 2, 0:cols],
                              bias.rearrange("(a n) -> a n", a=1).to_broadcast([2, cols])).then_inc(ld_w, 16)
                act.wait_ge(ld_w, PER_W * (w + 1))
                for a, n, hi, lo, rest, d in views(name):
                    for k in range(3):
                        done += 1
                        rows = P if k < 2 else KR
                        src_v = stage[0:rows, k, a:a + n]
                        if d:
                            src_v = src_v.rearrange("p (h d) -> p h d", d=d)
                        act.copy((hi + [rest])[k], src_v).then_inc(hi_done, 1)
            act.wait_ge(ld2, 32)
            act.wait_ge(zero_w, 4)
            act.copy(st.w2_hi[:], stage2[:]).then_inc(hi2, 1)
            act.copy(st.b2[0:2, :], bias2[:]).then_inc(hi2, 1)

        @block.vector
        def _(dve):
            zero_q = [st.wqk_hi[:], st.wqk_lo[:], st.wqk_r[:], st.b2[:]]
            for t in zero_q:
                dve.memset(t.bitcast(F32), 0.0).then_inc(zero_w, 1)
            done = 0
            for w, (name, src, bias, cols) in enumerate(weights):
                for a, n, hi, lo, rest, d in views(name):
                    for k in range(3):
                        rows = P if k < 2 else KR
                        src_v = stage[0:rows, k, a:a + n]
                        low_v = lows[0:rows, 0:n]
                        if d:
                            src_v = src_v.rearrange("p (h d) -> p h d", d=d)
                            low_v = low_v.rearrange("p (h d) -> p h d", d=d)
                        done += 1
                        dve.wait_ge(hi_done, done)
                        if k < 2:
                            dve.tensor_tensor(lo[k], src_v, hi[k].bitcast(F32), ALU.subtract).then_inc(split_done, 1)
                            continue
                        dve.wait_ge(split_done, done - 1)
                        dve.tensor_tensor(low_v, src_v, rest.bitcast(F32), ALU.subtract).then_inc(low_done, 1)
                        n_low = 2 * len([1 for x in weights[:w] for _ in views(x[0])])
                        n_low += 2 * [v[0] for v in views(name)].index(a)
                        dve.wait_ge(low_done, n_low + 1)
                        dve.tensor_scalar(low_v, low_v, st.lowrow[0:rows, 1:2], None, ALU.mult).then_inc(low_done, 1)
                        dve.wait_ge(low_done, n_low + 2)
                        dve.scalar_tensor_tensor(out=rest, in0=rest.bitcast(F32), scalar=st.lowrow[0:rows, 0:1],
                                                 in1=low_v, op0=ALU.mult, op1=ALU.add).then_inc(split_done, 1)
            dve.wait_ge(hi2, 1)
            dve.tensor_tensor(st.w2_lo[:], stage2[:], st.w2_hi[:].bitcast(F32), ALU.subtract).then_inc(lo2, 1)
            dve.wait_ge(hi2, 2)
            dve.memset(st.ones2[:].bitcast(F32), 1.0).then_inc(lo2, 1)
            dve.tensor_tensor(bias2[:], bias2[:], st.b2[0:2, :].bitcast(F32), ALU.subtract).then_inc(lo2, 1)
            dve.tensor_copy(st.sel2[:], st.lowrow[3 * CR:KR, :]).then_inc(lo2, 1)
            dve.wait_ge(lo2, 4)
            dve.tensor_scalar(bias2[:], bias2[:], st.sel2[:, 1:2], None, ALU.mult).then_inc(lo2, 1)
            dve.wait_ge(lo2, 5)
            dve.scalar_tensor_tensor(out=st.b2[0:2, :], in0=st.b2[0:2, :].bitcast(F32), scalar=st.sel2[:, 0:1], in1=bias2[:],
                                     op0=ALU.mult, op1=ALU.add).then_inc(lo2, 1)


def rotations(nc, st):
    with ExitStack() as ctx:
        m = Memory(nc, ctx)
        ps = m.banks("exp_ps", GROUPS)
        sc = m.sb("sc", [P, PAIRS, 2, RK])
        diag = m.sb("diag", [P, PAIRS, P])
        twos = m.sb("twos", [P, 1])
        taylor = m.sb("taylor", [P, PAIRS, RK])
        work = m.sb("exp_work", [P, 2, GP, RK])

        prod, c_new, s_new, held_even = m.sem("prod"), m.sem("c_new"), m.sem("s_new"), m.sem("held_even")
        held_odd, zeroed = m.sem("held_odd"), m.sem("diag_zeroed")
        work_done = m.sem("work_done")

        block = ctx.enter_context(nc.Block())

        def pairs(g):
            return slice(g * GP, (g + 1) * GP)

        def product(g, n):
            return ps[g][:, 0:GP * n * RK].rearrange("p (q j) -> p q j", q=GP)

        def hold(eng, src, g, scale):
            b = 0 if eng is nc.scalar else 1
            r = slice(RK * b, RK * (b + 1))
            out = diag[r, pairs(g), RK * b:RK * (b + 1)]
            if b == 0:
                eng.mul(out, src[r], scale).then_inc(held_even, 1)
            else:
                factor = twos if scale == 2.0 else st.ones
                eng.tensor_tensor(out, src[r], factor[r, 0:1].unsqueeze(1).to_broadcast([RK, GP, RK]), ALU.mult
                                  ).then_inc(held_odd, 1)

        def wait_held(eng, n):
            eng.wait_ge(held_even, n)
            eng.wait_ge(held_odd, n)

        def holds(eng):
            for g in range(GROUPS):
                if eng is nc.scalar:
                    eng.wait_ge(zeroed, 2)
                hold(eng, st.skew[:, pairs(g), :], g, 1.0)
            for g in range(GROUPS):
                if eng is nc.scalar:
                    eng.wait_ge(prod, g + 1)
                    eng.mul(sc[:, pairs(g), 1, :], product(g, 1), -1.0).then_inc(c_new, 1)
                eng.wait_ge(c_new, g + 1)
                hold(eng, sc[:, pairs(g), 1, :], g, 1.0)
            for g in range(GROUPS):
                eng.wait_ge(prod, GROUPS + g + 1)
                hold(eng, st.skew[:, pairs(g), :], g, 1.0)
            for g in range(GROUPS):
                eng.wait_ge(s_new, g + 1)
                hold(eng, sc[:, pairs(g), 0, :], g, 2.0)

        @block.gpsimd
        def _(pool):
            pool.memset(diag[:], 0.0).then_inc(zeroed, 1)
            pool.memset(twos[:], 2.0).then_inc(zeroed, 1)
            pool.wait_ge(zeroed, 2)
            holds(pool)
            with pool.Fori(0, SQUARINGS) as step:
                for g in range(GROUPS):
                    pool.wait_ge(s_new, GROUPS * (step + 1) + g + 1)
                    hold(pool, sc[:, pairs(g), 0, :], g, 2.0)

        @block.scalar
        def _(act):
            holds(act)
            with act.Fori(0, SQUARINGS) as step:
                for g in range(GROUPS):
                    act.wait_ge(s_new, GROUPS * (step + 1) + g + 1)
                    act.mul(sc[:, pairs(g), 1, :], product(g, 2).rearrange("p q (w j) -> p q w j", w=2)[:, :, 0, :],
                            -1.0).then_inc(c_new, 1)
                    hold(act, sc[:, pairs(g), 0, :], g, 2.0)

        @block.vector
        def _(dve):
            for g in range(GROUPS):
                dve.wait_ge(prod, GROUPS + g + 1)
                dve.tensor_scalar(work[:, 0], product(g, 1), 1 / 24, None, ALU.mult).then_inc(work_done, 1)
                dve.tensor_scalar(work[:, 1], product(g, 1), 1 / 120, None, ALU.mult).then_inc(work_done, 1)
                dve.wait_ge(work_done, 4 * g + 2)
                sq = sc[:, pairs(g), 1, :]
                dve.scalar_tensor_tensor(out=taylor[:, pairs(g), :], in0=sq, scalar=1 / 6, in1=work[:, 1],
                                         op0=ALU.mult, op1=ALU.add).then_inc(work_done, 1)
                wait_held(dve, 2 * GROUPS)
                dve.wait_ge(work_done, 4 * g + 3)
                dve.scalar_tensor_tensor(out=sq, in0=sq, scalar=0.5, in1=work[:, 0],
                                         op0=ALU.mult, op1=ALU.add).then_inc(work_done, 1)
                dve.wait_ge(work_done, 4 * g + 4)
            for g in range(GROUPS):
                dve.wait_ge(prod, 2 * GROUPS + g + 1)
                dve.tensor_tensor(sc[:, pairs(g), 0, :], st.skew[:, pairs(g), :], product(g, 1), ALU.subtract
                                  ).then_inc(s_new, 1)
            with dve.Fori(0, SQUARINGS) as step:
                for g in range(GROUPS):
                    dve.wait_ge(prod, GROUPS * (step + 3) + g + 1)
                    dve.scalar_tensor_tensor(out=sc[:, pairs(g), 0, :], in0=sc[:, pairs(g), 0, :], scalar=2.0,
                                             in1=product(g, 2).rearrange("p q (w j) -> p q w j", w=2)[:, :, 1, :],
                                             op0=ALU.mult, op1=ALU.subtract).then_inc(s_new, 1)
            dve.wait_ge(s_new, GROUPS * (SQUARINGS + 1))
            dve.wait_ge(c_new, GROUPS * (SQUARINGS + 1))
            dve.tensor_tensor(st.skew[:], sc[:, :, 0, :], sc[:, :, 1, :], ALU.add).then_inc(work_done, 1)

        @block.tensor
        def _(pe):
            for g in range(GROUPS):
                wait_held(pe, g + 1)
                for q in range(GP):
                    i = g * GP + q
                    mm = pe.matmul(product(g, 1)[:, q, :], diag[:, i, :], st.skew[:, i, :], start=True, stop=True)
                mm.then_inc(prod, 1)
            for g in range(GROUPS):
                wait_held(pe, GROUPS + g + 1)
                for q in range(GP):
                    i = g * GP + q
                    mm = pe.matmul(product(g, 1)[:, q, :], diag[:, i, :], sc[:, i, 1, :], start=True, stop=True)
                mm.then_inc(prod, 1)
            for g in range(GROUPS):
                wait_held(pe, 2 * GROUPS + g + 1)
                pe.wait_ge(work_done, 4 * (g + 1))
                for q in range(GP):
                    i = g * GP + q
                    mm = pe.matmul(product(g, 1)[:, q, :], diag[:, i, :], taylor[:, i, :], start=True, stop=True)
                mm.then_inc(prod, 1)
            with pe.Fori(0, SQUARINGS) as step:
                for g in range(GROUPS):
                    wait_held(pe, GROUPS * (step + 3) + g + 1)
                    pe.wait_ge(c_new, GROUPS * step + g + 1)
                    for q in range(GP):
                        i = g * GP + q
                        mm = pe.matmul(product(g, 2)[:, q, :], diag[:, i, :], sc[:, i, :, :], start=True, stop=True)
                    mm.then_inc(prod, 1)


class Elimination:

    W = P + RK

    def __init__(self, m, st):
        self.st = st
        self.bank = m.banks("elim_ps", 1)[0]
        self.picked = m.sb("picked", [P, P])
        self.rows = m.sb("pivot_rows", [P, self.W])
        self.root = m.sb("root", [P, 1])
        self.sign2 = m.sb("sign2", [P, 1])
        self.weight = m.sb("weight", [P, 1])
        self.part = m.sb("part", [P, RK])
        self.inv = m.sb("inv", [P, 1])
        self.factor = m.sb("factor", [P, 1])
        self.update = m.sb("update", [P, P])
        self.gram_k = m.sb("gram_k", [P, 1])
        self.square_k = m.sb("square_k", [P, 1])
        self.part_k = m.sb("part_k", [P, 1])
        self.pivot = m.sb("pivot", [P, 1])
        self.below_k = m.sb("below_k", [P, 1])
        self.chosen = m.sem("pivot_chosen")
        self.spread = m.sem("pivot_spread")
        self.copied = m.sem("pivot_copied")

    def pe(self, pe, k):
        pe.wait_ge(self.chosen, k + 1)
        pe.matmul(self.bank[:, 0:P], self.st.ones_top[:], self.picked[:], start=True, stop=True)
        pe.matmul(self.bank[:, P:self.W], self.st.ones_low[:], self.picked[:, 0:RK],
                  start=True, stop=True).then_inc(self.spread, 1)

    def act(self, act, k):
        act.wait_ge(self.spread, k + 1)
        act.copy(self.rows[:], self.bank[:, 0:self.W])
        act.copy(self.gram_k[:], self.bank[:, bass.ds(k, 1)])
        act.copy(self.square_k[:], self.bank[:, bass.ds(k + P, 1)]).then_inc(self.copied, 1)

    def pool(self, pool, k):
        st, el = self.st, self.st.elim
        pool.tensor_tensor(self.picked[:], el[:], st.ident2[:, bass.ds(k, 1)].to_broadcast([P, P]), ALU.mult
                           ).then_inc(self.chosen, 1)
        pool.wait_ge(self.copied, k + 1)
        pool.tensor_tensor(self.root[:], self.gram_k[:], st.powers[:, 0:1], ALU.pow)
        pool.tensor_scalar(self.sign2[:], self.square_k[:], 0.0, st.half2[:], ALU.is_ge, ALU.mult)
        pool.tensor_tensor(self.below_k[:], el[:, bass.ds(k, 1)], st.below[:, bass.ds(k, 1)], ALU.mult)
        pool.drain()
        pool.tensor_scalar(self.weight[:], self.sign2[:], st.half1[:], self.root[:], ALU.subtract, ALU.mult)
        pool.drain()
        pool.tensor_scalar(self.part[:], self.rows[:, P:self.W], self.weight[:], None, ALU.mult)
        pool.tensor_tensor(self.part_k[:], self.square_k[:], self.weight[:], ALU.mult)
        pool.drain()
        pool.tensor_tensor(self.rows[:, 0:RK], self.rows[:, 0:RK], self.part[:], ALU.add)
        pool.tensor_tensor(self.pivot[:], self.gram_k[:], self.part_k[:], ALU.add)
        pool.drain()
        pool.tensor_tensor(self.inv[:], self.pivot[:], st.powers[:, 1:2], ALU.pow)
        pool.drain()
        pool.tensor_tensor(self.factor[:], self.below_k[:], self.inv[:], ALU.mult)
        pool.drain()
        pool.tensor_scalar(self.update[:], self.rows[:, 0:P], self.factor[:], None, ALU.mult)
        pool.drain()
        pool.tensor_tensor(el[:], el[:], self.update[:], ALU.add)
        pool.drain()


def basis(nc, st):
    with ExitStack() as ctx:
        m = Memory(nc, ctx)
        ps = m.banks("basis_ps", 5)
        prod = m.sb("diag_prod", [P, RK])
        pivots = m.sb("pivots", [P, 1])
        sign = m.sb("sign", [RK, 1])
        scale = m.sb("scale", [RK, 1])
        t_scaled = m.sb("t_scaled", [RK, RK])
        t_tr = m.sb("t_tr", [RK, RK])
        dve_step, pool_step, pe_step = m.sem("basis_dve"), m.sem("basis_pool"), m.sem("basis_pe")
        block = ctx.enter_context(nc.Block())

        @block.vector
        def _(dve):
            dve.tensor_tensor(prod[:], st.elim[:, 0:RK], st.ident2[:], ALU.mult).then_inc(dve_step, 1)
            dve.wait_ge(dve_step, 1)
            dve.reduce_sum(pivots[:], prod[:], AX_X).then_inc(dve_step, 1)
            dve.wait_ge(dve_step, 2)
            dve.tensor_scalar(sign[:], pivots[RK:P, :], 0.0, -2.0, ALU.is_ge, ALU.mult).then_inc(dve_step, 1)
            dve.wait_ge(pool_step, 1)
            dve.wait_ge(dve_step, 3)
            dve.tensor_scalar(scale[:], sign[:], 1.0, scale[:], ALU.add, ALU.mult).then_inc(dve_step, 1)
            dve.wait_ge(dve_step, 4)
            dve.tensor_scalar(t_scaled[:], st.elim[0:RK, RK:P], scale[:], None, ALU.mult).then_inc(dve_step, 1)
            dve.wait_ge(pe_step, 1)
            dve.tensor_copy(t_tr[:], ps[0][0:RK, 0:RK]).then_inc(dve_step, 1)
            dve.wait_ge(pe_step, 2)
            for t in range(3):
                rows = P if t < 2 else CR
                dve.tensor_copy(st.u[0:rows, t, :].rearrange("p (w k) -> p w k", w=2),
                                ps[1 + t][0:rows, 0:RK].unsqueeze(1).to_broadcast([rows, 2, RK])).then_inc(dve_step, 1)
            dve.tensor_copy(st.u_t[:], ps[4][0:RK, 0:C]).then_inc(dve_step, 1)

        @block.gpsimd
        def _(pool):
            pool.wait_ge(dve_step, 2)
            pool.tensor_tensor(scale[:], pivots[0:RK, :], st.minus_half[0:RK, 0:1], ALU.pow).then_inc(pool_step, 1)

        @block.tensor
        def _(pe):
            pe.wait_ge(dve_step, 5)
            pe.transpose(ps[0][0:RK, 0:RK], t_scaled[:], st.ident[0:RK, 0:RK]).then_inc(pe_step, 1)
            pe.wait_ge(dve_step, 6)
            for t in range(3):
                rows = P if t < 2 else CR
                pe.matmul(ps[1 + t][0:rows, 0:RK], st.p_t[:, t * P:t * P + rows], t_tr[:], start=True, stop=True)
            pe.matmul(ps[4][0:RK, 0:C], t_tr[:], st.p_t[:], start=True, stop=True).then_inc(pe_step, 1)


class Jobs:

    def __init__(self, mem, name, banks, jobs, ahead=()):
        self.banks = banks
        n = len(banks)
        self.steady = {job: (i % n, i // n) for i, job in enumerate(jobs)}
        left = [job for job in jobs if job not in ahead]
        self.final = {job: (i % n, i // n) for i, job in enumerate(left)}
        self.first = {job: (i, 0) for i, job in enumerate(ahead)}
        self.before = [int(b < len(ahead)) for b in range(n)]
        self.uses = [len(range(b, len(jobs), n)) for b in range(n)]
        self.full = [mem.sem(f"{name}_full{i}") for i in range(n)]
        self.free = [mem.sem(f"{name}_free{i}") for i in range(n)]

    def open(self, eng):
        for free in self.free:
            eng.sem_inc(free, 1)

    def at(self, g, job):
        if isinstance(g, int) and g < 0:
            return self.first[job]
        b, k = (self.final if isinstance(g, int) and g == GROUPS - 1 else self.steady)[job]
        return b, g * self.uses[b] + k + self.before[b]

    def bank(self, g, job):
        return self.banks[self.at(g, job)[0]]

    def full_of(self, g, job):
        return self.full[self.at(g, job)[0]]

    def free_of(self, g, job):
        return self.free[self.at(g, job)[0]]

    def wait_free(self, eng, g, job):
        b, n = self.at(g, job)
        eng.wait_ge(self.free[b], n + 1)

    def wait_full(self, eng, g, job):
        b, n = self.at(g, job)
        eng.wait_ge(self.full[b], n + 1)

    def wait_taken(self, eng, g, job):
        b, n = self.at(g, job)
        eng.wait_ge(self.free[b], n + 2)


def for_groups(eng, body):
    with eng.Fori(0, GROUPS - 1) as g:
        body(g)
    body(GROUPS - 1)


class Split:

    def __init__(self, m, name, tokens):
        self.hi = m.sb(f"{name}_hi", [P, 2, tokens], F32R)
        self.lo = m.sb(f"{name}_lo", [P, 2, tokens], F32R)
        self.rest = m.sb(f"{name}_rest", [KR, tokens], F32R)

    def ones(self, eng, sem):
        eng.memset(self.rest[3 * CR:KR, :].bitcast(F32), 1.0).then_inc(sem, 1)


def product(pe, out, acts, tokens, weights, cols, weights_held):
    w_hi, w_lo, w_r = weights
    terms = [(acts.hi[:, k, tokens], w_hi[:, k, cols]) for k in range(2)]
    terms += [(acts.hi[:, k, tokens], w_lo[:, k, cols]) for k in range(2)]
    terms += [(acts.lo[:, k, tokens], w_hi[:, k, cols]) for k in range(2)]
    terms += [(acts.rest[:, tokens], w_r[:, cols])]
    for i, (a, w) in enumerate(terms):
        held, streamed = (w, a) if weights_held else (a, w)
        mm = pe.matmul(out, held, streamed, start=(i == 0), stop=(i == len(terms) - 1))
    return mm


class Norm:

    def __init__(self, m, name, st, jobs, acts, shift, scale):
        self.st, self.jobs, self.acts, self.shift, self.scale = st, jobs, acts, shift, scale
        self.stats = m.sb(f"{name}_stats", [P, GP, 6])
        self.mv = m.sb(f"{name}_mean_var", [P, GP, 2])
        self.var = m.sb(f"{name}_var_eps", [P, GP])
        self.rstd = m.sb(f"{name}_rstd", [P, GP])
        self.xn = m.sb(f"{name}_xn", [P, GP, CD])
        self.h = m.sb(f"{name}_h", [P, 3, TG])
        self.aggr = m.sem(f"{name}_aggr_done")
        self.var_ready, self.rstd_ready = m.sem(f"{name}_var_ready"), m.sem(f"{name}_rstd_ready")
        self.xn_ready, self.scaled, self.shifted = m.sem(f"{name}_xn_ready"), m.sem(f"{name}_scaled"), m.sem(f"{name}_shifted")
        self.hi_ready, self.lo_ready = m.sem(f"{name}_hi_ready"), m.sem(f"{name}_lo_ready")

    def statistics(self, dve, g):
        x = self.st.x
        for p in range(GP):
            dve.bn_stats(self.stats[:, p, :], x[:, bass.ds(g * GP + p, 1), :].rearrange("p q c -> p (q c)"))
        dve.drain()
        for p in range(GP):
            dve.bn_aggr(self.mv[:, p, :], self.stats[:, p, :]).then_inc(self.aggr, 1)
        dve.wait_ge(self.aggr, g * GP + GP)
        dve.tensor_scalar(self.var[:], self.mv[:, :, 1], EPS, None, ALU.add).then_inc(self.var_ready, 1)

    def root(self, pool, g):
        pool.wait_ge(self.var_ready, g + 1)
        pool.tensor_tensor(self.rstd[:], self.var[:], self.st.minus_half[:], ALU.pow).then_inc(self.rstd_ready, 1)

    def normalize(self, dve, g):
        x = self.st.x
        dve.wait_ge(self.rstd_ready, g + 1)
        for p in range(GP):
            mean, rstd = self.mv[:, p, 0:1], self.rstd[:, p:p + 1]
            xg = x[:, bass.ds(g * GP + p, 1), :].rearrange("p q c -> p (q c)")
            dve.tensor_scalar(self.xn[:, p, 0:C], xg, mean, rstd, ALU.subtract, ALU.mult).then_inc(self.xn_ready, 1)
            dve.tensor_scalar(self.xn[:, p, C:CD].rearrange("p (r c) -> p r c", r=2),
                              x[:, bass.ds(g * GP + p, 1), 2 * P:C].to_broadcast([P, 2, CR]), mean, rstd,
                              ALU.subtract, ALU.mult).then_inc(self.xn_ready, 1)

    def transposes(self, pe, g, at):
        pe.wait_ge(self.xn_ready, (g + 1) * 2 * GP)
        for t in range(3):
            rows = P if t < 2 else 3 * CR
            job = ("ln", t)
            self.jobs.wait_free(pe, at, job)
            for p in range(GP):
                mm = pe.transpose(self.jobs.bank(at, job)[0:rows, p * P:(p + 1) * P],
                                  self.xn[:, p, t * P:t * P + rows], self.st.ident[:])
            mm.then_inc(self.jobs.full_of(at, job), 1)

    def modulate(self, dve, g, at):
        for t in range(3):
            rows = P if t < 2 else 3 * CR
            job = ("ln", t)
            by = lambda n: self.st.mod_t[0:rows, n, t, bass.ds(g * GB, GB)].unsqueeze(2).to_broadcast([rows, GB, L])
            h = self.h[0:rows, t, :].rearrange("p (b l) -> p b l", l=L)
            self.jobs.wait_full(dve, at, job)
            dve.tensor_tensor(h, self.jobs.bank(at, job)[0:rows, :].rearrange("p (b l) -> p b l", l=L), by(self.scale),
                              ALU.mult).then_inc(self.jobs.free_of(at, job), 1)
        for t in range(3):
            rows = P if t < 2 else 3 * CR
            by = lambda n: self.st.mod_t[0:rows, n, t, bass.ds(g * GB, GB)].unsqueeze(2).to_broadcast([rows, GB, L])
            h = self.h[0:rows, t, :].rearrange("p (b l) -> p b l", l=L)
            self.jobs.wait_taken(dve, at, ("ln", t))
            dve.tensor_tensor(h, h, by(self.shift), ALU.add).then_inc(self.shifted, 1)

    def high(self, act, g):
        for t in range(3):
            act.wait_ge(self.shifted, g * 3 + t + 1)
            out = self.acts.hi[:, t, :] if t < 2 else self.acts.rest[0:3 * CR, :]
            act.copy(out, self.h[0:P if t < 2 else 3 * CR, t, :]).then_inc(self.hi_ready, 1)

    def low(self, eng, g, drain):
        for t in range(3):
            if t == 2 and drain:
                eng.drain()
            eng.wait_ge(self.hi_ready, g * 3 + t + 1)
            if t < 2:
                out, hi, h = self.acts.lo[:, t, :], self.acts.hi[:, t, :], self.h[:, t, :]
            else:
                r = slice(2 * CR, 3 * CR)
                out, hi, h = self.acts.rest[r, :], self.acts.rest[r, :], self.h[r, t, :]
            eng.tensor_tensor(out, h, hi.bitcast(F32), ALU.subtract).then_inc(self.lo_ready, 1)
        if drain:
            eng.drain()

    def wait_acts(self, eng, g):
        eng.wait_ge(self.lo_ready, 3 * (g + 1))


def gate_loads(sp, nc, io, which, gate, loaded, used):
    src = io["gates"].rearrange("(q b) s c -> b s q c", b=2)
    with sp.Fori(0, GROUPS) as g:
        sp.wait_ge(used, g * GP + 1)
        for b in range(2):
            sp.dma_start(gate[L * b:L * (b + 1), :, :],
                         src[b, which, bass.ds(g * GP, GP), :].unsqueeze(0).to_broadcast([L, GP, C])
                         ).then_inc(loaded, 16)


def attention(nc, st, io, elim):
    with ExitStack() as ctx:
        m = Memory(nc, ctx)
        banks = m.banks("att_ps", 3)
        scores = ctx.enter_context(nc.psum_tensor("scores", [P, 4, BANK], F32))
        HP = H // 2
        HF = HP // 2
        V1 = D + 1

        names = [("qk", j) for j in range(8)] + [("v", p) for p in range(GP)]
        for p in range(GP):
            if p >= 1:
                names += [("pt", p - 1, 0), ("pt", p - 1, 1)]
                names += [("ot", p - 2)] if p >= 2 else []
                names += [("o", p - 1, 0), ("o", p - 1, 1)]
                names += [("proj", p - 2)] if p >= 2 else []
        names += [("ln", t) for t in range(3)]
        names += [("pt", 3, 0), ("pt", 3, 1), ("ot", 2), ("o", 3, 0), ("o", 3, 1), ("proj", 2), ("ot", 3), ("proj", 3)]
        jobs = Jobs(m, "att", banks, names, [("ln", t) for t in range(3)])

        acts = Split(m, "h1", TG)
        norm = Norm(m, "ln1", st, jobs, acts, 0, 1)
        q_t, k_t = m.sb("q_t", [P, 4, TG]), m.sb("k_t", [P, 4, TG])
        va = m.sb("va", [P, GP, HP, 2, 2 * V1])
        prob = m.sb("prob", [P, 2, H * L])
        row_max = m.sb("row_max", [P, 2, 4, 4])
        prob_t = m.sb("prob_t", [P, 2, 4 * P])
        rsum = m.sb("rsum", [P, 2, 2, 4])
        o = m.sb("o", [P, 2, CD])
        o_t = Split(m, "o_t", P)
        gated = m.sb("gated", [P, 2, C])
        gate = m.sb("gate", [P, GP, C])

        begun, gate_in = m.sem("att_begun"), m.sem("gate_in")
        scored, max_done, less_max = m.sem("scored"), m.sem("max_done"), m.sem("less_max")
        exp_done, inverted, o_half, o_ready = m.sem("exp_done"), m.sem("inverted"), m.sem("o_half"), m.sem("o_ready")
        o_lo = m.sem("o_lo")
        o_hi, gate_done, added = m.sem("o_hi"), m.sem("gate_done"), m.sem("added")

        def step_of(g, i):
            return g * ELIM_ATT + i

        block = ctx.enter_context(nc.Block())

        def by_head(t):
            return t.rearrange("p (q r d) -> p r q d", r=4, d=D)

        @block.sync
        def _(sp):
            gate_loads(sp, nc, io, 0, gate, gate_in, added)

        @block.gpsimd
        def _(pool):
            norm.root(pool, 0)
            norm.low(pool, 0, True)

            def body(g):
                for i in range(ELIM_ATT):
                    if i == 2 and not isinstance(g, int):
                        norm.root(pool, g + 1)
                    elim.pool(pool, step_of(g, i))
                if not isinstance(g, int):
                    norm.low(pool, g + 1, True)
            for_groups(pool, body)

        @block.scalar
        def _(act):
            norm.high(act, 0)

            def exponential(g, p):
                act.wait_ge(less_max, g * GP + p + 2)
                act.activation(prob[:, p % 2, :], prob[:, p % 2, :], ACT.Exp, scale=SCALE).then_inc(exp_done, 1)

            def take_prob_t(g, p):
                for hf in range(2):
                    job = ("pt", p, hf)
                    jobs.wait_full(act, g, job)
                    act.copy(prob_t[:, hf, :], jobs.bank(g, job)[:]).then_inc(jobs.free_of(g, job), 1)

            def repeat_rest(g, p):
                act.wait_ge(o_half, (g * GP + p) * 2 + 2)
                for hf in range(2):
                    jobs.wait_taken(act, g, ("o", p, hf))
                act.copy(o[:, p % 2, C:CD].rearrange("p (r c) -> p r c", r=2),
                         o[:, p % 2, 2 * P:C].unsqueeze(1).to_broadcast([P, 2, CR])).then_inc(o_ready, 1)

            def o_high(g, p):
                jobs.wait_full(act, g, ("ot", p))
                bank = jobs.bank(g, ("ot", p))
                act.copy(o_t.hi[:], bank[:, 0:2 * P].rearrange("p (k t) -> p k t", k=2)).then_inc(o_hi, 1)
                act.copy(o_t.rest[0:3 * CR, :], bank[0:3 * CR, 2 * P:3 * P]).then_inc(o_hi, 1)

            def body(g):
                for j in range(0, 8, 2):
                    jobs.wait_full(act, g, ("qk", j))
                    out = (q_t if j < 4 else k_t)[:, j % 4, :]
                    act.copy(out, jobs.bank(g, ("qk", j))[:]).then_inc(jobs.free_of(g, ("qk", j)), 1)
                elim.act(act, step_of(g, 0))
                for p in range(GP):
                    job = ("v", p)
                    jobs.wait_full(act, g, job)
                    src = jobs.bank(g, job)[:, 0:C].rearrange("p (j w r d) -> p w r j d", j=2, w=2, d=D)
                    for b in range(2):
                        for w in range(2):
                            out = va[RK * w:RK * (w + 1), p, :, b, w * V1:w * V1 + D].rearrange(
                                "p (r j) d -> p r j d", j=2)
                            cp = act.copy(out, src[L * b:L * (b + 1), w])
                            if b == 1 and w == 1:
                                cp.then_inc(jobs.free_of(g, job), 1)
                for p in range(GP):
                    exponential(g, p)
                    if p >= 1:
                        take_prob_t(g, p - 1)
                    if p >= 2:
                        o_high(g, p - 2)
                    if p >= 1:
                        repeat_rest(g, p - 1)
                    elim.act(act, step_of(g, p + 1))
                take_prob_t(g, 3)
                o_high(g, 2)
                repeat_rest(g, 3)
                o_high(g, 3)
                if not isinstance(g, int):
                    norm.high(act, g + 1)
            for_groups(act, body)

        @block.vector
        def _(dve):
            dve.memset(va[:], 0.0).then_inc(begun, 1)
            acts.ones(dve, begun)
            o_t.ones(dve, begun)
            dve.wait_ge(begun, 3)
            for w in range(2):
                dve.memset(va[RK * w:RK * (w + 1), :, :, :, w * V1 + D].rearrange("p g q b -> p (g q b)"), 1.0
                           ).then_inc(begun, 1)
            dve.wait_ge(begun, 5)
            jobs.open(dve)
            dve.sem_inc(less_max, 1)
            dve.sem_inc(added, 1)
            norm.statistics(dve, 0)
            norm.normalize(dve, 0)
            norm.modulate(dve, 0, -1)

            def softmax_max(g, p):
                n = g * GP + p
                s = scores[:, :, 0:4 * L].rearrange("p r (q m) -> p r q m", m=L)
                dve.wait_ge(scored, n + 1)
                dve.tensor_reduce(row_max[:, p % 2], s, AX_X, ALU.max).then_inc(max_done, 1)
                dve.wait_ge(max_done, n + 1)
                dve.tensor_tensor(prob[:, p % 2, :].rearrange("p (r q m) -> p r q m", r=4, m=L), s,
                                  row_max[:, p % 2].unsqueeze(3).to_broadcast([P, 4, 4, L]), ALU.subtract
                                  ).then_inc(less_max, 1)

            def take_o(g, p):
                for hf in range(2):
                    job = ("o", p, hf)
                    jobs.wait_full(dve, g, job)
                    src = jobs.bank(g, job)[:, 0:8 * 2 * V1].rearrange("p (b r q d) -> p b r q d", b=2, r=2, d=V1)
                    dve.reciprocal(rsum[:, hf], src[:, 0, :, :, D]).then_inc(inverted, 1)
                    dve.wait_ge(inverted, (g * GP + p) * 2 + hf + 1)
                    for b in range(2):
                        rows = slice(L * b, L * (b + 1))
                        out = by_head(o[rows, p % 2, 0:C])[:, 2 * hf:2 * hf + 2]
                        tt = dve.tensor_tensor(out, src[rows, b, :, :, 0:D],
                                               rsum[rows, hf].unsqueeze(3).to_broadcast([L, 2, 4, D]), ALU.mult)
                        tt.then_inc(jobs.free_of(g, job) if b else o_half, 1)

            def o_low(g, p):
                job = ("ot", p)
                bank = jobs.bank(g, job)
                r = slice(2 * CR, 3 * CR)
                dve.wait_ge(o_hi, (g * GP + p) * 2 + 2)
                dve.tensor_tensor(o_t.lo[:], bank[:, 0:2 * P].rearrange("p (k t) -> p k t", k=2),
                                  o_t.hi[:].bitcast(F32), ALU.subtract).then_inc(o_lo, 1)
                dve.tensor_tensor(o_t.rest[r, :], bank[r, 2 * P:3 * P], o_t.rest[r, :].bitcast(F32), ALU.subtract
                                  ).then_inc(jobs.free_of(g, job), 1)

            def residual(g, p):
                n = g * GP + p
                job = ("proj", p)
                xg = st.x[:, bass.ds(n, 1), :].rearrange("p q c -> p (q c)")
                jobs.wait_full(dve, g, job)
                if p == 0:
                    dve.wait_ge(gate_in, 32 * (g + 1))
                dve.tensor_tensor(gated[:, p % 2, :], jobs.bank(g, job)[:, 0:C], gate[:, p, :], ALU.mult
                                  ).then_inc(jobs.free_of(g, job), 1)
                jobs.wait_taken(dve, g, job)
                dve.tensor_tensor(xg, xg, gated[:, p % 2, :], ALU.add).then_inc(added, 1)

            def body(g):
                ahead = not isinstance(g, int)
                for j in range(1, 8, 2):
                    jobs.wait_full(dve, g, ("qk", j))
                    out = (q_t if j < 4 else k_t)[:, j % 4, :]
                    dve.tensor_copy(out, jobs.bank(g, ("qk", j))[:]).then_inc(jobs.free_of(g, ("qk", j)), 1)
                if ahead:
                    norm.statistics(dve, g + 1)
                for p in range(GP):
                    softmax_max(g, p)
                    if p == 2 and ahead:
                        norm.normalize(dve, g + 1)
                    if p >= 2:
                        o_low(g, p - 2)
                    if p >= 1:
                        take_o(g, p - 1)
                    if p >= 2:
                        residual(g, p - 2)
                if ahead:
                    norm.modulate(dve, g + 1, g)
                o_low(g, 2)
                take_o(g, 3)
                residual(g, 2)
                o_low(g, 3)
                residual(g, 3)
            for_groups(dve, body)

        @block.tensor
        def _(pe):
            pe.wait_ge(begun, 5)
            norm.transposes(pe, 0, -1)

            def score(g, p):
                n = g * GP + p
                if p == 0:
                    for j in range(8 - len(banks), 8):
                        jobs.wait_taken(pe, g, ("qk", j))
                pe.wait_ge(less_max, n + 1)
                for r in range(4):
                    rows = slice(DP * r, DP * (r + 1))
                    for q in range(4):
                        for b in range(2):
                            tok = slice(p * P + L * b, p * P + L * (b + 1))
                            mm = pe.matmul(scores[L * b:L * (b + 1), r, q * L:(q + 1) * L], q_t[rows, q, tok],
                                           k_t[rows, q, tok], start=True, stop=True)
                mm.then_inc(scored, 1)

            def transpose_prob(g, p):
                pe.wait_ge(exp_done, g * GP + p + 1)
                for hf in range(2):
                    job = ("pt", p, hf)
                    jobs.wait_free(pe, g, job)
                    for i in range(4):
                        mm = pe.transpose(jobs.bank(g, job)[:, i * P:(i + 1) * P],
                                          prob[:, p % 2, (hf * 4 + i) * P:(hf * 4 + i + 1) * P], st.ident[:])
                    mm.then_inc(jobs.full_of(g, job), 1)

            def weigh_v(g, p):
                for hf in range(2):
                    job = ("o", p, hf)
                    jobs.wait_taken(pe, g, ("v", p))
                    jobs.wait_taken(pe, g, ("pt", p, hf))
                    jobs.wait_free(pe, g, job)
                    out = jobs.bank(g, job)[:, 0:8 * 2 * V1].rearrange("p (b i d) -> p b i d", b=2, i=4)
                    for i in range(4):
                        mm = pe.matmul(out[:, :, i, :], prob_t[:, hf, i * P:(i + 1) * P], va[:, p, hf * 4 + i, :, :],
                                       start=True, stop=True)
                    mm.then_inc(jobs.full_of(g, job), 1)

            def transpose_o(g, p):
                job = ("ot", p)
                pe.wait_ge(o_ready, g * GP + p + 1)
                jobs.wait_free(pe, g, job)
                for t in range(3):
                    rows = P if t < 2 else 3 * CR
                    mm = pe.transpose(jobs.bank(g, job)[0:rows, t * P:(t + 1) * P], o[:, p % 2, t * P:t * P + rows],
                                      st.ident[:])
                mm.then_inc(jobs.full_of(g, job), 1)

            def project(g, p):
                job = ("proj", p)
                pe.wait_ge(o_lo, g * GP + p + 1)
                jobs.wait_taken(pe, g, ("ot", p))
                jobs.wait_free(pe, g, job)
                product(pe, jobs.bank(g, job)[:, 0:C], o_t, slice(0, P), (st.wp_hi, st.wp_lo, st.wp_r), slice(0, C),
                        False).then_inc(jobs.full_of(g, job), 1)

            def body(g):
                norm.wait_acts(pe, g)
                for j in range(8):
                    jobs.wait_free(pe, g, ("qk", j))
                    product(pe, jobs.bank(g, ("qk", j))[:], acts, slice(0, TG), (st.wqk_hi, st.wqk_lo, st.wqk_r),
                            slice(j * P, (j + 1) * P), True).then_inc(jobs.full_of(g, ("qk", j)), 1)
                    if j == 6:
                        elim.pe(pe, step_of(g, 0))
                for p in range(GP):
                    jobs.wait_free(pe, g, ("v", p))
                    product(pe, jobs.bank(g, ("v", p))[:, 0:C], acts, slice(p * P, (p + 1) * P),
                            (st.wv_hi, st.wv_lo, st.wv_r), slice(0, C), False).then_inc(jobs.full_of(g, ("v", p)), 1)
                for p in range(GP):
                    score(g, p)
                    if p >= 1:
                        transpose_prob(g, p - 1)
                    if p >= 2:
                        transpose_o(g, p - 2)
                    if p >= 1:
                        weigh_v(g, p - 1)
                    if p >= 2:
                        project(g, p - 2)
                    elim.pe(pe, step_of(g, p + 1))
                if not isinstance(g, int):
                    norm.transposes(pe, g + 1, g)
                transpose_prob(g, 3)
                transpose_o(g, 2)
                weigh_v(g, 3)
                project(g, 2)
                transpose_o(g, 3)
                project(g, 3)
            for_groups(pe, body)


def mlp(nc, st, io, elim):
    with ExitStack() as ctx:
        m = Memory(nc, ctx)
        ln = [("ln", t) for t in range(3)]
        jobs = Jobs(m, "mlp", m.banks("mlp_ps", 7), [("fc1", f) for f in range(FT)] + ln + [("fc2", p) for p in range(GP)], ln)
        acts = Split(m, "h2", TG)
        norm = Norm(m, "ln2", st, jobs, acts, 2, 3)
        NG = 3
        g32 = m.sb("g32", [P, NG, TG])
        g_hi, g_lo = m.sb("g_hi", [P, FT, TG], F32R), m.sb("g_lo", [P, FT, TG], F32R)
        gated = m.sb("gated2", [P, 2, C])
        gate = m.sb("gate2", [P, GP, C])
        begun, gate_in, added = m.sem("mlp_begun"), m.sem("gate2_in"), m.sem("added2")
        g_lo_done = m.sem("g_lo_done")

        def step_of(g, i):
            return ELIM_ATT * GROUPS + g * ELIM_MLP + i

        def elim_after(f):
            return f // 3 if f % 3 == 1 else None

        block = ctx.enter_context(nc.Block())

        @block.sync
        def _(sp):
            gate_loads(sp, nc, io, 1, gate, gate_in, added)

        @block.gpsimd
        def _(pool):
            norm.root(pool, 0)
            norm.low(pool, 0, True)

            def body(g):
                for i in range(ELIM_MLP):
                    if i == 1 and not isinstance(g, int):
                        norm.root(pool, g + 1)
                    elim.pool(pool, step_of(g, i))
                if not isinstance(g, int):
                    norm.low(pool, g + 1, True)
            for_groups(pool, body)

        @block.scalar
        def _(act):
            norm.high(act, 0)

            def body(g):
                for f in range(FT):
                    job = ("fc1", f)
                    bank = jobs.bank(g, job)
                    jobs.wait_full(act, g, job)
                    act.wait_ge(g_lo_done, g * FT + f + 1)
                    act.activation(g32[:, f % NG, :], bank[:], ACT.Gelu_apprx_tanh)
                    act.activation(g_hi[:, f, :], bank[:], ACT.Gelu_apprx_tanh
                                   ).then_inc(jobs.free_of(g, job), 1)
                    if elim_after(f) is not None:
                        elim.act(act, step_of(g, elim_after(f)))
                if not isinstance(g, int):
                    norm.high(act, g + 1)
            for_groups(act, body)

        @block.vector
        def _(dve):
            acts.ones(dve, begun)
            jobs.open(dve)
            dve.sem_inc(added, 1)
            dve.sem_inc(g_lo_done, NG)
            norm.statistics(dve, 0)
            norm.normalize(dve, 0)
            norm.modulate(dve, 0, -1)

            def low(g, f):
                jobs.wait_taken(dve, g, ("fc1", f))
                dve.tensor_tensor(g_lo[:, f, :], g32[:, f % NG, :], g_hi[:, f, :].bitcast(F32), ALU.subtract
                                  ).then_inc(g_lo_done, 1)

            def residual(g, p):
                n = g * GP + p
                job = ("fc2", p)
                xg = st.x[:, bass.ds(n, 1), :].rearrange("p q c -> p (q c)")
                jobs.wait_full(dve, g, job)
                if p == 0:
                    dve.wait_ge(gate_in, 32 * (g + 1))
                dve.tensor_tensor(gated[:, p % 2, :], jobs.bank(g, job)[:, 0:C], gate[:, p, :], ALU.mult
                                  ).then_inc(jobs.free_of(g, job), 1)
                jobs.wait_taken(dve, g, job)
                dve.tensor_tensor(xg, xg, gated[:, p % 2, :], ALU.add).then_inc(added, 1)

            def body(g):
                ahead = not isinstance(g, int)
                for f in range(FT):
                    low(g, f)
                    if f == 1 and ahead:
                        norm.statistics(dve, g + 1)
                    if f == 5 and ahead:
                        norm.normalize(dve, g + 1)
                if ahead:
                    norm.modulate(dve, g + 1, g)
                for p in range(GP):
                    residual(g, p)
            for_groups(dve, body)

        @block.tensor
        def _(pe):
            pe.wait_ge(begun, 1)
            norm.transposes(pe, 0, -1)

            def down(g, p):
                job, tok = ("fc2", p), slice(p * P, (p + 1) * P)
                jobs.wait_free(pe, g, job)
                if p == 0:
                    pe.wait_ge(g_lo_done, (g + 1) * FT + NG)
                out = jobs.bank(g, job)[:, 0:C]
                pe.matmul(out, st.ones2[:], st.b2[:], start=True, stop=False)
                for f in range(FT):
                    pe.matmul(out, g_hi[:, f, tok], st.w2_hi[:, f, :], start=False, stop=False)
                    pe.matmul(out, g_hi[:, f, tok], st.w2_lo[:, f, :], start=False, stop=False)
                    mm = pe.matmul(out, g_lo[:, f, tok], st.w2_hi[:, f, :], start=False, stop=(f == FT - 1))
                mm.then_inc(jobs.full_of(g, job), 1)

            def body(g):
                norm.wait_acts(pe, g)
                for f in range(FT):
                    job = ("fc1", f)
                    jobs.wait_free(pe, g, job)
                    product(pe, jobs.bank(g, job)[:], acts, slice(0, TG), (st.w1_hi, st.w1_lo, st.w1_r),
                            slice(f * P, (f + 1) * P), True).then_inc(jobs.full_of(g, job), 1)
                    if elim_after(f) is not None:
                        elim.pe(pe, step_of(g, elim_after(f)))
                if not isinstance(g, int):
                    norm.transposes(pe, g + 1, g)
                for p in range(GP):
                    down(g, p)
            for_groups(pe, body)


def rotate(nc, st, io):
    with ExitStack() as ctx:
        m = Memory(nc, ctx)
        banks = m.banks("rot_ps", 8)
        names = [("x", t) for t in range(3)] + [("z",), ("dz", 0), ("dz", 1)] + [("out", p) for p in range(GP)]
        jobs = Jobs(m, "rot", banks, names)
        x_s = m.sb("x_s", [P, GP, C])
        e_s = m.sb("e_s", [P, GP, 2, RK])
        x_t = m.sb("x_t", [P, 3, TG])
        z_t = m.sb("z_t", [P, TG])
        dz_t = m.sb("dz_t", [RK, TG])
        copied, e_copied, begun, done, stored = m.sem("x_copied"), m.sem("e_copied"), m.sem("rot_begun"), m.sem("rot_done"), m.sem("stored")
        block = ctx.enter_context(nc.Block())

        @block.sync
        def _(sp):
            out = io["out"].rearrange("(q b) l c -> (b l) q c", b=2)
            with sp.Fori(0, GROUPS) as g:
                sp.wait_ge(done, (g + 1) * GP)
                sp.dma_start(out[:, bass.ds(g * GP, GP), :], st.x[:, bass.ds(g * GP, GP), :]).then_inc(stored, 16)
            sp.wait_ge(stored, 16 * GROUPS)

        @block.scalar
        def _(act):
            def stage(g):
                act.copy(x_s[:], st.x[:, bass.ds(g * GP, GP), :]).then_inc(copied, 1)
                act.copy(e_s[:], st.skew[:, bass.ds(g * GP, GP), :].unsqueeze(2).to_broadcast([P, GP, 2, RK])
                         ).then_inc(e_copied, 1)

            with act.Fori(0, GROUPS) as g:
                act.wait_ge(done, g * GP + 1)
                stage(g)
                for t in (0, 2):
                    rows = P if t < 2 else CR
                    jobs.wait_full(act, g, ("x", t))
                    act.copy(x_t[0:rows, t, :], jobs.bank(g, ("x", t))[0:rows, :]).then_inc(jobs.free_of(g, ("x", t)), 1)

        @block.vector
        def _(dve):
            jobs.open(dve)
            dve.sem_inc(done, 1)
            with dve.Fori(0, GROUPS) as g:
                jobs.wait_full(dve, g, ("x", 1))
                dve.tensor_copy(x_t[:, 1, :], jobs.bank(g, ("x", 1))[:]).then_inc(jobs.free_of(g, ("x", 1)), 1)
                jobs.wait_full(dve, g, ("z",))
                dve.tensor_copy(z_t[:], jobs.bank(g, ("z",))[:]).then_inc(jobs.free_of(g, ("z",)), 1)
                for b in range(2):
                    jobs.wait_full(dve, g, ("dz", b))
                    dve.tensor_copy(dz_t[:].rearrange("k (q b l) -> k q b l", b=2, l=L)[:, :, b, :],
                                    jobs.bank(g, ("dz", b))[0:RK, 0:GP * L].rearrange("k (q l) -> k q l", l=L)
                                    ).then_inc(jobs.free_of(g, ("dz", b)), 1)
                for p in range(GP):
                    job = ("out", p)
                    xg = st.x[:, bass.ds(g * GP + p, 1), :].rearrange("p q c -> p (q c)")
                    jobs.wait_full(dve, g, job)
                    dve.tensor_tensor(xg, xg, jobs.bank(g, job)[:, 0:C], ALU.add).then_inc(jobs.free_of(g, job), 1)
                jobs.wait_taken(dve, g, ("out", GP - 1))
                dve.sem_inc(done, GP)

        @block.tensor
        def _(pe):
            with pe.Fori(0, GROUPS) as g:
                pe.wait_ge(copied, g + 1)
                for t in range(3):
                    rows = P if t < 2 else CR
                    jobs.wait_free(pe, g, ("x", t))
                    for p in range(GP):
                        mm = pe.transpose(jobs.bank(g, ("x", t))[0:rows, p * P:(p + 1) * P],
                                          x_s[:, p, t * P:t * P + rows], st.ident[:])
                    mm.then_inc(jobs.full_of(g, ("x", t)), 1)
                jobs.wait_free(pe, g, ("z",))
                for t in range(3):
                    rows = P if t < 2 else CR
                    jobs.wait_taken(pe, g, ("x", t))
                    mm = pe.matmul(jobs.bank(g, ("z",))[:], st.u[0:rows, t, :], x_t[0:rows, t, :],
                                   start=(t == 0), stop=(t == 2))
                mm.then_inc(jobs.full_of(g, ("z",)), 1)
                jobs.wait_taken(pe, g, ("z",))
                pe.wait_ge(e_copied, g + 1)
                for b in range(2):
                    rows = slice(L * b, L * (b + 1))
                    jobs.wait_free(pe, g, ("dz", b))
                    for p in range(GP):
                        tok = slice(p * P + L * b, p * P + L * (b + 1))
                        mm = pe.matmul(jobs.bank(g, ("dz", b))[:, p * L:(p + 1) * L], e_s[rows, p, :, :],
                                       z_t[rows, tok], start=True, stop=True)
                    mm.then_inc(jobs.full_of(g, ("dz", b)), 1)
                for b in range(2):
                    jobs.wait_taken(pe, g, ("dz", b))
                for p in range(GP):
                    job = ("out", p)
                    jobs.wait_free(pe, g, job)
                    pe.matmul(jobs.bank(g, job)[:, 0:C], dz_t[:, p * P:(p + 1) * P], st.u_t[:], start=True, stop=True
                              ).then_inc(jobs.full_of(g, job), 1)


class State:
    pass


def state(nc, ctx):
    m, st = Memory(nc, ctx), State()
    st.x = m.sb("x", [P, PAIRS, C])
    st.ident = m.sb("ident", [P, P])
    st.ident2 = m.sb("ident2", [P, RK])
    st.below = m.sb("below", [P, RK])
    st.half1, st.half2 = m.sb("half1", [P, 1]), m.sb("half2", [P, 1])
    st.lowrow = m.sb("lowrow", [P, 2])
    st.sel2 = m.sb("sel2", [2, 2])
    st.ones = m.sb("ones", [P, 1])
    st.ones_top, st.ones_low = m.sb("ones_top", [P, P]), m.sb("ones_low", [P, P])
    st.minus_half = m.sb("minus_half", [P, GP])
    st.powers = m.sb("powers", [P, 2])
    st.elim = m.sb("elim", [P, P])
    st.p_c = m.sb("p_c", [96, 3, RK])
    st.p_t = m.sb("p_t", [RK, C])
    st.u = m.sb("u", [P, 3, 2 * RK])
    st.u_t = m.sb("u_t", [RK, C])
    st.skew = m.sb("skew", [P, PAIRS, RK])
    st.mod_t = m.sb("mod_t", [P, 4, 3, B])
    return st


def weight_state(nc, ctx, st):
    m = Memory(nc, ctx)
    st.wqk_hi, st.wqk_lo = m.sb("wqk_hi", [P, 2, 2 * H * DP], F32R), m.sb("wqk_lo", [P, 2, 2 * H * DP], F32R)
    st.wqk_r = m.sb("wqk_r", [KR, 2 * H * DP], F32R)
    st.wv_hi, st.wv_lo, st.wv_r = m.sb("wv_hi", [P, 2, C], F32R), m.sb("wv_lo", [P, 2, C], F32R), m.sb("wv_r", [KR, C], F32R)
    st.wp_hi, st.wp_lo, st.wp_r = m.sb("wp_hi", [P, 2, C], F32R), m.sb("wp_lo", [P, 2, C], F32R), m.sb("wp_r", [KR, C], F32R)
    st.w1_hi, st.w1_lo, st.w1_r = m.sb("w1_hi", [P, 2, FF], F32R), m.sb("w1_lo", [P, 2, FF], F32R), m.sb("w1_r", [KR, FF], F32R)
    st.w2_hi, st.w2_lo = m.sb("w2_hi", [P, FT, C], F32R), m.sb("w2_lo", [P, FT, C], F32R)
    st.b2, st.ones2 = m.sb("b2", [P, C], F32R), m.sb("ones2", [P, P], F32R)


def program(nc, io):
    io["gates"] = nc.dram_tensor("gates", (B, 2, C), F32, kind="Internal").ap()
    io["skew"] = nc.dram_tensor("skew_dram", (B, RK, RK), F32, kind="Internal").ap()
    with ExitStack() as ctx:
        st = state(nc, ctx)
        setup(nc, Memory(nc, ctx), st, io)
        weight_state(nc, ctx, st)
        split_weights(nc, st, io)
        rotations(nc, st)
        with ExitStack() as inner:
            elim = Elimination(Memory(nc, inner), st)
            attention(nc, st, io, elim)
            mlp(nc, st, io, elim)
        basis(nc, st)
        rotate(nc, st, io)


_INS = ["x", "cond_1152", "L0_cond_W_qkv", "L0_cond_b_qkv", "L0_cond_W_proj", "L0_cond_b_proj", "L0_cond_W_fc1",
        "L0_cond_b_fc1", "L0_cond_W_fc2", "L0_cond_b_fc2", "L0_cond_W_ada", "L0_cond_b_ada", "L1_cond_P",
        "L1_cond_W", "L1_cond_b"]


def kernel(**inputs):
    import numpy as _np
    import concourse.bacc as _bacc
    from concourse import mybir as _mybir
    from concourse.bass_utils import run_bass_kernel_spmd as _run

    nc = _bacc.Bacc("TRN2", target_bir_lowering=False, num_devices=1)
    arrays, io = {}, {}
    for name in _INS:
        a = _np.ascontiguousarray(inputs[name])
        arrays[f"in_{name}_dram"] = a
        io[name] = nc.dram_tensor(f"in_{name}_dram", a.shape, _mybir.dt.from_np(a.dtype), kind="ExternalInput").ap()
    io["out"] = nc.dram_tensor("out_0_dram", (64, 64, 288), _mybir.dt.float32, kind="ExternalOutput").ap()
    program(nc, io)
    r = _run(nc, [arrays], core_ids=[0])
    return r.results[0]["out_0_dram"]
```

```python
from contextlib import ExitStack

import concourse.bass as bass
from concourse import mybir

ALU = mybir.AluOpType
ACT = mybir.ActivationFunctionType
AX_X = mybir.AxisListType.X
F32 = mybir.dt.float32
F32R = mybir.dt.float32r

P = 128
B, L, C = 64, 64, 288
H = 16
D = C // H
DP = 32
FF = 4 * C
FT = FF // P
RK = 64
NV = RK * (RK - 1) // 2
PAIRS = B // 2
GP = 4
GROUPS = PAIRS // GP
GB = 2 * GP
TG = GP * P
CR = C - 2 * P
CD = 2 * P + 3 * CR
KR = 3 * CR + 2
EPS = 1e-6
SCALE = float(D) ** -0.5
SQUARINGS = 8
ELIM_ATT, ELIM_MLP = 4, 4
BANK = 512


def offset_of_row(i):
    return i * (RK - 1) - i * (i - 1) // 2


class Memory:

    def __init__(self, nc, ctx):
        self.nc, self.ctx = nc, ctx

    def sb(self, name, shape, dt=F32):
        return self.ctx.enter_context(self.nc.sbuf_tensor(name, shape, dt))

    def banks(self, prefix, n):
        return [self.ctx.enter_context(self.nc.psum_tensor(f"{prefix}{i}", [P, BANK], F32)) for i in range(n)]

    def sem(self, name):
        return self.ctx.enter_context(self.nc.semaphore(name))


def setup(nc, mem, st, io):
    with ExitStack() as ctx:
        m = Memory(nc, ctx)
        ps = m.banks("setup_ps", 8)
        cond = m.sb("cond", [B, C])
        p_c = m.sb("p_c", [96, 3, RK])
        e_neg = m.sb("e_neg", [B, C])
        silu = m.sb("silu", [B, C])
        silu_t = m.sb("silu_t", [P, 2, B])
        silu_r = m.sb("silu_r", [CR + 1, B])
        w_ada = m.sb("w_ada", [P, 3, 6 * C])
        ada = m.sb("ada", [B, 6, C])
        mod = m.sb("mod", [B, 4, CD])
        NL1 = NV // 16
        w_l1 = m.sb("w_l1", [NL1, 16, C])
        w_l1t = m.sb("w_l1t", [P, 3, NV])
        vec = m.sb("vec", [B, NV])
        upper = m.sb("upper", [B, RK, RK])
        skewed = m.sb("skewed", [B, RK, RK])

        ld_c, ld_ada, ld_l1, ld_p, ld_x = m.sem("ld_c"), m.sem("ld_ada"), m.sem("ld_l1"), m.sem("ld_p"), m.sem("ld_x")
        consts = m.sem("consts")
        silu_step = m.sem("silu_step")
        pe_done = m.sem("pe_done")
        dve_done = m.sem("dve_done")
        act_done = m.sem("act_done")
        spread = m.sem("spread")
        zeroed = m.sem("zeroed")
        gates_out = m.sem("gates_out")
        skew_out = m.sem("skew_out")
        low_done = m.sem("low_done")

        block = ctx.enter_context(nc.Block())

        @block.sync
        def _(sp):
            sp.dma_start(cond[:], io["cond_1152"]).then_inc(ld_c, 16)
            sp.dma_start(w_ada[:, 0:2, :], io["L0_cond_W_ada"][0:2 * P, :].rearrange("(t p) n -> p t n", p=P)).then_inc(ld_ada, 16)
            sp.dma_start(w_ada[0:CR, 2, :], io["L0_cond_W_ada"][2 * P:C, :]).then_inc(ld_ada, 16)
            sp.dma_start(w_ada[CR:CR + 1, 2, :], io["L0_cond_b_ada"].rearrange("(a n) -> a n", a=1)).then_inc(ld_ada, 16)
            sp.dma_start(w_l1[:], io["L1_cond_W"].rearrange("(t p) c -> p t c", p=NL1)).then_inc(ld_l1, 16)
            sp.dma_start(w_l1t[CR:CR + 1, 2, :], io["L1_cond_b"].rearrange("(a n) -> a n", a=1)).then_inc(ld_l1, 16)
            sp.dma_start(p_c[:], io["L1_cond_P"].rearrange("(t p) n -> p t n", p=96)).then_inc(ld_p, 16)
            sp.dma_start(st.elim[RK:P, 0:RK], io["L1_cond_P"][0:RK, :]).then_inc(ld_p, 16)
            sp.wait_ge(dve_done, 2)
            sp.dma_start(io["gates"], ada[:, 2:6:3, :]).then_inc(gates_out, 16)
            sp.wait_ge(dve_done, 4)
            sp.dma_start(io["skew"], skewed[:]).then_inc(skew_out, 16)
            sp.wait_ge(skew_out, 16)
            sp.wait_ge(gates_out, 16)
            sp.wait_ge(ld_x, 16 * GROUPS)

        @block.gpsimd
        def _(pool):
            pool.memset(st.ident[:], 0.0).then_inc(consts, 1)
            pool.wait_ge(consts, 1)
            pool.memset(st.ident2[:], 0.0).then_inc(consts, 1)
            pool.wait_ge(consts, 2)
            pool.memset(st.below[:], -1.0).then_inc(consts, 1)
            pool.wait_ge(consts, 3)
            pool.memset(st.half1[:], 0.0).then_inc(consts, 1)
            pool.wait_ge(consts, 4)
            pool.memset(st.half2[:], 0.0).then_inc(consts, 1)
            pool.wait_ge(consts, 5)
            pool.memset(st.lowrow[:], 0.0).then_inc(consts, 1)
            pool.wait_ge(consts, 6)
            pool.affine_select(out=st.ident[:], in_=st.ident[:], compare_op=ALU.not_equal, fill=1.0, base=0,
                               pattern=[[-1, P]], channel_multiplier=1).then_inc(consts, 1)
            pool.wait_ge(consts, 7)
            pool.affine_select(out=st.ident2[:], in_=st.ident2[:], compare_op=ALU.not_equal, fill=1.0, base=0,
                               pattern=[[-1, RK]], channel_multiplier=1).then_inc(consts, 1)
            pool.wait_ge(consts, 8)
            pool.affine_select(out=st.ident2[:], in_=st.ident2[:], compare_op=ALU.not_equal, fill=1.0, base=-RK,
                               pattern=[[-1, RK]], channel_multiplier=1).then_inc(consts, 1)
            pool.wait_ge(consts, 9)
            pool.affine_select(out=st.below[0:RK, :], in_=st.below[0:RK, :], compare_op=ALU.is_gt, fill=0.0, base=0,
                               pattern=[[-1, RK]], channel_multiplier=1).then_inc(consts, 1)
            pool.wait_ge(consts, 10)
            pool.affine_select(out=st.below[RK:P, :], in_=st.below[RK:P, :], compare_op=ALU.is_gt, fill=0.0, base=0,
                               pattern=[[-1, RK]], channel_multiplier=1).then_inc(consts, 1)
            pool.wait_ge(consts, 11)
            pool.memset(st.half1[RK:P, :], 1.0).then_inc(consts, 1)
            pool.wait_ge(consts, 12)
            pool.memset(st.half2[RK:P, :], 2.0).then_inc(consts, 1)
            pool.wait_ge(consts, 13)
            pool.memset(st.lowrow[CR:2 * CR, 1:2], 1.0).then_inc(consts, 1)
            pool.wait_ge(consts, 14)
            pool.affine_select(out=st.lowrow[3 * CR:P, 1:2], in_=st.lowrow[3 * CR:P, 1:2], compare_op=ALU.not_equal,
                               fill=1.0, base=-1, pattern=[[0, 1]], channel_multiplier=1).then_inc(consts, 1)
            pool.wait_ge(consts, 15)
            pool.tensor_scalar(st.lowrow[:, 0:1], st.lowrow[:, 1:2], -1.0, 1.0, ALU.mult, ALU.add).then_inc(consts, 1)
            pool.wait_ge(consts, 16)
            pool.memset(st.ones[:], 1.0).then_inc(consts, 1)
            pool.wait_ge(consts, 17)
            pool.memset(st.ones_top[:], 0.0).then_inc(consts, 1)
            pool.wait_ge(consts, 18)
            pool.memset(st.ones_top[0:RK, :], 1.0).then_inc(consts, 1)
            pool.wait_ge(consts, 19)
            pool.memset(st.ones_low[:], 0.0).then_inc(consts, 1)
            pool.wait_ge(consts, 20)
            pool.memset(st.ones_low[RK:P, :], 1.0).then_inc(consts, 1)
            pool.wait_ge(consts, 21)
            pool.memset(st.minus_half[:], -0.5).then_inc(consts, 1)
            pool.wait_ge(consts, 22)
            pool.memset(st.powers[:, 0:1], 0.5).then_inc(consts, 1)
            pool.wait_ge(consts, 23)
            pool.memset(st.powers[:, 1:2], -1.0).then_inc(consts, 1)
            pool.wait_ge(consts, 24)
            pool.memset(silu_r[CR:CR + 1, :], 1.0).then_inc(consts, 1)
            pool.wait_ge(consts, 25)
            pool.memset(st.elim[:, RK:P], 0.0).then_inc(consts, 1)
            pool.wait_ge(consts, 26)
            pool.affine_select(out=st.elim[0:RK, RK:P], in_=st.elim[0:RK, RK:P], compare_op=ALU.not_equal, fill=1.0,
                               base=0, pattern=[[-1, RK]], channel_multiplier=1).then_inc(consts, 1)
            pool.memset(upper[:], 0.0).then_inc(zeroed, 1)
            pool.wait_ge(zeroed, 1)
            pool.wait_ge(dve_done, 3)
            for i in range(0, RK - 1, 2):
                a, n = offset_of_row(i), RK - 1 - i
                pool.tensor_copy(upper[:, i, i + 1:RK], vec[:, a:a + n]).then_inc(spread, 1)

        @block.scalar
        def _(act):
            for g in range(GROUPS):
                act.dma_start(st.x[:, g * GP:(g + 1) * GP, :],
                              io["x"].rearrange("(q b) l c -> (b l) q c", b=2)[:, g * GP:(g + 1) * GP, :]
                              ).then_inc(ld_x, 16)
            act.wait_ge(ld_c, 16)
            act.activation(e_neg[:], cond[:], ACT.Exp, scale=-1.0).then_inc(silu_step, 1)
            for n in range(12):
                if n % 2 == 0:
                    act.wait_ge(pe_done, 2 + 1 + n)
                    rows = P if n // 4 < 2 else CR
                    act.copy(w_l1t[0:rows, n // 4, (n % 4) * 4 * NL1:(n % 4 + 1) * 4 * NL1],
                             ps[n % 8][0:rows, 0:4 * NL1]).then_inc(act_done, 1)
            act.wait_ge(zeroed, 1)
            act.wait_ge(dve_done, 3)
            for i in range(1, RK - 1, 2):
                a, n = offset_of_row(i), RK - 1 - i
                act.copy(upper[:, i, i + 1:RK], vec[:, a:a + n]).then_inc(spread, 1)

        @block.vector
        def _(dve):
            dve.wait_ge(silu_step, 1)
            dve.tensor_scalar(e_neg[:], e_neg[:], 1.0, None, ALU.add).then_inc(silu_step, 1)
            dve.wait_ge(silu_step, 2)
            dve.reciprocal(silu[:], e_neg[:]).then_inc(silu_step, 1)
            dve.wait_ge(silu_step, 3)
            dve.tensor_tensor(silu[:], silu[:], cond[:], ALU.mult).then_inc(silu_step, 1)
            dve.wait_ge(pe_done, 1)
            dve.tensor_copy(silu_t[:], ps[0][:, 0:2 * B].rearrange("p (t b) -> p t b", b=B)).then_inc(dve_done, 1)
            dve.tensor_copy(silu_r[0:CR, :], ps[0][0:CR, 2 * B:3 * B]).then_inc(silu_step, 1)
            dve.wait_ge(pe_done, 2)
            ada_f = ada[:].rearrange("b s c -> b (s c)")
            for n in range(4):
                w = min(BANK, 6 * C - n * BANK)
                dve.tensor_copy(ada_f[:, n * BANK:n * BANK + w], ps[4 + n][0:B, 0:w]).then_inc(silu_step, 1)
            dve.wait_ge(silu_step, 9)
            for n, (s, plus) in enumerate(((0, 0.0), (1, 1.0), (3, 0.0), (4, 1.0))):
                dve.tensor_scalar(mod[:, n, 0:C], ada[:, s, :], plus, None, ALU.add).then_inc(silu_step, 1)
                dve.tensor_scalar(mod[:, n, C:CD].rearrange("b (r c) -> b r c", c=CR),
                                  ada[:, s, 2 * P:C].unsqueeze(1).to_broadcast([B, 2, CR]), plus, None,
                                  ALU.add).then_inc(silu_step, 1)
            dve.wait_ge(silu_step, 17)
            dve.tensor_copy(mod[0:1, 0, 0:1], mod[0:1, 0, 0:1]).then_inc(dve_done, 1)
            for n in range(12):
                if n % 2 == 1:
                    dve.wait_ge(pe_done, 2 + 1 + n)
                    rows = P if n // 4 < 2 else CR
                    dve.tensor_copy(w_l1t[0:rows, n // 4, (n % 4) * 4 * NL1:(n % 4 + 1) * 4 * NL1],
                                    ps[n % 8][0:rows, 0:4 * NL1]).then_inc(low_done, 1)
            dve.wait_ge(pe_done, 15)
            for n in range(4):
                dve.tensor_copy(st.mod_t[:, n, 0:2, :], ps[4][:, n * 2 * B:(n + 1) * 2 * B].rearrange("p (t b) -> p t b", b=B)
                                ).then_inc(silu_step, 1)
            dve.tensor_copy(st.mod_t[0:3 * CR, :, 2, :], ps[5][0:3 * CR, 0:4 * B].rearrange("p (n b) -> p n b", b=B)
                            ).then_inc(silu_step, 1)
            dve.wait_ge(pe_done, 16)
            for n in range(4):
                dve.tensor_scalar(vec[:, n * 4 * NL1:(n + 1) * 4 * NL1], ps[n][0:B, 0:4 * NL1],
                                  2.0 ** -SQUARINGS, None, ALU.mult).then_inc(silu_step, 1)
            dve.wait_ge(silu_step, 26)
            dve.tensor_copy(vec[0:1, 0:1], vec[0:1, 0:1]).then_inc(dve_done, 1)
            dve.wait_ge(spread, RK - 1)
            dve.tensor_tensor(skewed[:], upper[:], upper[:].rearrange("b i j -> b j i"), ALU.subtract).then_inc(dve_done, 1)
            dve.wait_ge(pe_done, 17)
            dve.tensor_copy(st.elim[0:RK, 0:RK], ps[6][0:RK, 0:RK]).then_inc(silu_step, 1)
            dve.tensor_copy(st.p_t[:], ps[7][0:RK, 0:C]).then_inc(silu_step, 1)

        @block.tensor
        def _(pe):
            pe.wait_ge(silu_step, 4)
            pe.wait_ge(consts, 27)
            for t in range(3):
                rows = P if t < 2 else CR
                mm = pe.transpose(ps[0][0:rows, t * B:(t + 1) * B], silu[:, t * P:t * P + rows], st.ident[0:B, 0:B])
            mm.then_inc(pe_done, 1)
            pe.wait_ge(dve_done, 1)
            pe.wait_ge(silu_step, 5)
            pe.wait_ge(ld_ada, 48)
            lhs = [silu_t[:, 0, :], silu_t[:, 1, :], silu_r[:, :]]
            for n in range(4):
                w = min(BANK, 6 * C - n * BANK)
                for t in range(3):
                    rows = P if t < 2 else CR + 1
                    mm = pe.matmul(ps[4 + n][0:B, 0:w], lhs[t], w_ada[0:rows, t, n * BANK:n * BANK + w],
                                   start=(t == 0), stop=(t == 2))
            mm.then_inc(pe_done, 1)
            pe.wait_ge(ld_l1, 32)
            pe.wait_ge(dve_done, 2)
            for n in range(12):
                t = n // 4
                rows = P if t < 2 else CR
                if n >= 8:
                    if n % 2 == 0:
                        pe.wait_ge(act_done, (n - 8) // 2 + 1)
                    else:
                        pe.wait_ge(low_done, (n - 8) // 2 + 1)
                for q in range(4):
                    r = (n % 4) * 4 + q
                    mm = pe.transpose(ps[n % 8][0:rows, q * NL1:(q + 1) * NL1], w_l1[:, r, t * P:t * P + rows],
                                      st.ident[0:NL1, 0:NL1])
                mm.then_inc(pe_done, 1)
            pe.wait_ge(act_done, 6)
            pe.wait_ge(low_done, 6)
            for n in range(4):
                for t in range(2):
                    mm = pe.transpose(ps[4][:, (2 * n + t) * B:(2 * n + t + 1) * B], mod[:, n, t * P:(t + 1) * P],
                                      st.ident[0:B, 0:B])
                mm = pe.transpose(ps[5][0:3 * CR, n * B:(n + 1) * B], mod[:, n, 2 * P:CD], st.ident[0:B, 0:B])
            mm.then_inc(pe_done, 1)
            for n in range(4):
                for t in range(3):
                    rows = P if t < 2 else CR + 1
                    mm = pe.matmul(ps[n][0:B, 0:4 * NL1], lhs[t], w_l1t[0:rows, t, n * 4 * NL1:(n + 1) * 4 * NL1],
                                   start=(t == 0), stop=(t == 2))
            mm.then_inc(pe_done, 1)
            pe.wait_ge(ld_p, 32)
            for t in range(3):
                pe.matmul(ps[6][0:RK, 0:RK], p_c[:, t, :], p_c[:, t, :], start=(t == 0), stop=(t == 2))
            for t in range(3):
                mm = pe.transpose(ps[7][0:RK, t * 96:(t + 1) * 96], p_c[:, t, :], st.ident[0:96, 0:96])
            mm.then_inc(pe_done, 1)


def skew_moves(sp, st, io, moved, to_dram):
    for b in range(2):
        sbuf = st.skew[RK * b:RK * (b + 1), :, :]
        dram = io["skew"].rearrange("(q b) i j -> b i q j", b=2)[b]
        sp.dma_start(*((dram, sbuf) if to_dram else (sbuf, dram))).then_inc(moved, 16)


def split_weights(nc, st, io):
    with ExitStack() as ctx:
        m = Memory(nc, ctx)
        stage = m.sb("stage", [P, 3, FF])
        lows = m.sb("lows", [P, FF])
        stage2 = m.sb("stage2", [P, FT, C])
        bias2 = m.sb("bias2", [2, C])
        ld_w, hi_done, split_done = m.sem("ld_w"), m.sem("hi_done"), m.sem("split_done")
        low_done, zero_w = m.sem("low_done"), m.sem("zero_w")
        ld2, hi2, lo2 = m.sem("fc2_ld"), m.sem("fc2_hi"), m.sem("fc2_lo")

        block = ctx.enter_context(nc.Block())

        weights = [("qkv", io["L0_cond_W_qkv"], io["L0_cond_b_qkv"], 3 * C),
                   ("proj", io["L0_cond_W_proj"], io["L0_cond_b_proj"], C),
                   ("fc1", io["L0_cond_W_fc1"], io["L0_cond_b_fc1"], FF)]
        PER_W = 6 * 16
        skew_in = m.sem("skew_in")

        def views(name):
            if name == "qkv":
                def heads(t, a):
                    return t[:, a:a + H * DP].rearrange("p (h d) -> p h d", d=DP)[:, :, 0:D]
                out = []
                for n in range(2):
                    a = n * H * DP
                    hi = [heads(st.wqk_hi[:, k, :], a) for k in range(2)]
                    lo = [heads(st.wqk_lo[:, k, :], a) for k in range(2)]
                    out.append((n * C, C, hi, lo, heads(st.wqk_r[:, :], a), D))
                out.append((2 * C, C, [st.wv_hi[:, k, :] for k in range(2)], [st.wv_lo[:, k, :] for k in range(2)],
                            st.wv_r[:, :], None))
                return out
            hi, lo, r = (st.wp_hi, st.wp_lo, st.wp_r) if name == "proj" else (st.w1_hi, st.w1_lo, st.w1_r)
            n = C if name == "proj" else FF
            return [(0, n, [hi[:, k, :] for k in range(2)], [lo[:, k, :] for k in range(2)], r[:, :], None)]

        @block.sync
        def _(sp):
            skew_moves(sp, st, io, skew_in, to_dram=False)
            sp.dma_start(stage2[:], io["L0_cond_W_fc2"].rearrange("(t p) n -> p t n", p=P)).then_inc(ld2, 16)
            sp.dma_start(bias2[:], io["L0_cond_b_fc2"].rearrange("(a n) -> a n", a=1).to_broadcast([2, C])).then_inc(ld2, 16)
            sp.wait_ge(skew_in, 32)

        @block.scalar
        def _(act):
            done = 0
            act.wait_ge(zero_w, 3)
            for w, (name, src, bias, cols) in enumerate(weights):
                if w:
                    act.wait_ge(split_done, done)
                for k in range(2):
                    act.dma_start(stage[:, k, 0:cols], src[k * P:(k + 1) * P, :]).then_inc(ld_w, 16)
                for k in range(3):
                    act.dma_start(stage[k * CR:(k + 1) * CR, 2, 0:cols], src[2 * P:C, :]).then_inc(ld_w, 16)
                act.dma_start(stage[3 * CR:KR, 2, 0:cols],
                              bias.rearrange("(a n) -> a n", a=1).to_broadcast([2, cols])).then_inc(ld_w, 16)
                act.wait_ge(ld_w, PER_W * (w + 1))
                for a, n, hi, lo, rest, d in views(name):
                    for k in range(3):
                        done += 1
                        rows = P if k < 2 else KR
                        src_v = stage[0:rows, k, a:a + n]
                        if d:
                            src_v = src_v.rearrange("p (h d) -> p h d", d=d)
                        act.copy((hi + [rest])[k], src_v).then_inc(hi_done, 1)
            act.wait_ge(ld2, 32)
            act.wait_ge(zero_w, 4)
            act.copy(st.w2_hi[:], stage2[:]).then_inc(hi2, 1)
            act.copy(st.b2[0:2, :], bias2[:]).then_inc(hi2, 1)

        @block.vector
        def _(dve):
            zero_q = [st.wqk_hi[:], st.wqk_lo[:], st.wqk_r[:], st.b2[:]]
            for t in zero_q:
                dve.memset(t.bitcast(F32), 0.0).then_inc(zero_w, 1)
            done = 0
            for w, (name, src, bias, cols) in enumerate(weights):
                for a, n, hi, lo, rest, d in views(name):
                    for k in range(3):
                        rows = P if k < 2 else KR
                        src_v = stage[0:rows, k, a:a + n]
                        low_v = lows[0:rows, 0:n]
                        if d:
                            src_v = src_v.rearrange("p (h d) -> p h d", d=d)
                            low_v = low_v.rearrange("p (h d) -> p h d", d=d)
                        done += 1
                        dve.wait_ge(hi_done, done)
                        if k < 2:
                            dve.tensor_tensor(lo[k], src_v, hi[k].bitcast(F32), ALU.subtract).then_inc(split_done, 1)
                            continue
                        dve.wait_ge(split_done, done - 1)
                        dve.tensor_tensor(low_v, src_v, rest.bitcast(F32), ALU.subtract).then_inc(low_done, 1)
                        n_low = 2 * len([1 for x in weights[:w] for _ in views(x[0])])
                        n_low += 2 * [v[0] for v in views(name)].index(a)
                        dve.wait_ge(low_done, n_low + 1)
                        dve.tensor_scalar(low_v, low_v, st.lowrow[0:rows, 1:2], None, ALU.mult).then_inc(low_done, 1)
                        dve.wait_ge(low_done, n_low + 2)
                        dve.scalar_tensor_tensor(out=rest, in0=rest.bitcast(F32), scalar=st.lowrow[0:rows, 0:1],
                                                 in1=low_v, op0=ALU.mult, op1=ALU.add).then_inc(split_done, 1)
            dve.wait_ge(hi2, 1)
            dve.tensor_tensor(st.w2_lo[:], stage2[:], st.w2_hi[:].bitcast(F32), ALU.subtract).then_inc(lo2, 1)
            dve.wait_ge(hi2, 2)
            dve.memset(st.ones2[:].bitcast(F32), 1.0).then_inc(lo2, 1)
            dve.tensor_tensor(bias2[:], bias2[:], st.b2[0:2, :].bitcast(F32), ALU.subtract).then_inc(lo2, 1)
            dve.tensor_copy(st.sel2[:], st.lowrow[3 * CR:KR, :]).then_inc(lo2, 1)
            dve.wait_ge(lo2, 4)
            dve.tensor_scalar(bias2[:], bias2[:], st.sel2[:, 1:2], None, ALU.mult).then_inc(lo2, 1)
            dve.wait_ge(lo2, 5)
            dve.scalar_tensor_tensor(out=st.b2[0:2, :], in0=st.b2[0:2, :].bitcast(F32), scalar=st.sel2[:, 0:1], in1=bias2[:],
                                     op0=ALU.mult, op1=ALU.add).then_inc(lo2, 1)


def rotations(nc, st, io):
    with ExitStack() as ctx:
        m = Memory(nc, ctx)
        ps = m.banks("exp_ps", GROUPS)
        sc = m.sb("sc", [P, PAIRS, 2, RK])
        diag = m.sb("diag", [P, PAIRS, P])
        twos = m.sb("twos", [P, 1])
        taylor = m.sb("taylor", [P, PAIRS, RK])
        work = m.sb("exp_work", [P, 2, GP, RK])

        prod, c_new, s_new, held_even = m.sem("prod"), m.sem("c_new"), m.sem("s_new"), m.sem("held_even")
        held_odd, zeroed = m.sem("held_odd"), m.sem("diag_zeroed")
        work_done = m.sem("work_done")
        rotation_done, kept = m.sem("rotation_done"), m.sem("rotation_kept")

        block = ctx.enter_context(nc.Block())

        def pairs(g):
            return slice(g * GP, (g + 1) * GP)

        def product(g, n):
            return ps[g][:, 0:GP * n * RK].rearrange("p (q j) -> p q j", q=GP)

        def hold(eng, src, g, scale):
            b = 0 if eng is nc.scalar else 1
            r = slice(RK * b, RK * (b + 1))
            out = diag[r, pairs(g), RK * b:RK * (b + 1)]
            if b == 0:
                eng.mul(out, src[r], scale).then_inc(held_even, 1)
            else:
                factor = twos if scale == 2.0 else st.ones
                eng.tensor_tensor(out, src[r], factor[r, 0:1].unsqueeze(1).to_broadcast([RK, GP, RK]), ALU.mult
                                  ).then_inc(held_odd, 1)

        def wait_held(eng, n):
            eng.wait_ge(held_even, n)
            eng.wait_ge(held_odd, n)

        def holds(eng):
            for g in range(GROUPS):
                if eng is nc.scalar:
                    eng.wait_ge(zeroed, 2)
                hold(eng, st.skew[:, pairs(g), :], g, 1.0)
            for g in range(GROUPS):
                if eng is nc.scalar:
                    eng.wait_ge(prod, g + 1)
                    eng.mul(sc[:, pairs(g), 1, :], product(g, 1), -1.0).then_inc(c_new, 1)
                eng.wait_ge(c_new, g + 1)
                hold(eng, sc[:, pairs(g), 1, :], g, 1.0)
            for g in range(GROUPS):
                eng.wait_ge(prod, GROUPS + g + 1)
                hold(eng, st.skew[:, pairs(g), :], g, 1.0)
            for g in range(GROUPS):
                eng.wait_ge(s_new, g + 1)
                hold(eng, sc[:, pairs(g), 0, :], g, 2.0)

        @block.sync
        def _(sp):
            sp.wait_ge(rotation_done, 1)
            skew_moves(sp, st, io, kept, to_dram=True)
            sp.wait_ge(kept, 32)

        @block.gpsimd
        def _(pool):
            pool.memset(diag[:], 0.0).then_inc(zeroed, 1)
            pool.memset(twos[:], 2.0).then_inc(zeroed, 1)
            pool.wait_ge(zeroed, 2)
            holds(pool)
            with pool.Fori(0, SQUARINGS) as step:
                for g in range(GROUPS):
                    pool.wait_ge(s_new, GROUPS * (step + 1) + g + 1)
                    hold(pool, sc[:, pairs(g), 0, :], g, 2.0)

        @block.scalar
        def _(act):
            holds(act)
            with act.Fori(0, SQUARINGS) as step:
                for g in range(GROUPS):
                    act.wait_ge(s_new, GROUPS * (step + 1) + g + 1)
                    act.mul(sc[:, pairs(g), 1, :], product(g, 2).rearrange("p q (w j) -> p q w j", w=2)[:, :, 0, :],
                            -1.0).then_inc(c_new, 1)
                    hold(act, sc[:, pairs(g), 0, :], g, 2.0)

        @block.vector
        def _(dve):
            for g in range(GROUPS):
                dve.wait_ge(prod, GROUPS + g + 1)
                dve.tensor_scalar(work[:, 0], product(g, 1), 1 / 24, None, ALU.mult).then_inc(work_done, 1)
                dve.tensor_scalar(work[:, 1], product(g, 1), 1 / 120, None, ALU.mult).then_inc(work_done, 1)
                dve.wait_ge(work_done, 4 * g + 2)
                sq = sc[:, pairs(g), 1, :]
                dve.scalar_tensor_tensor(out=taylor[:, pairs(g), :], in0=sq, scalar=1 / 6, in1=work[:, 1],
                                         op0=ALU.mult, op1=ALU.add).then_inc(work_done, 1)
                wait_held(dve, 2 * GROUPS)
                dve.wait_ge(work_done, 4 * g + 3)
                dve.scalar_tensor_tensor(out=sq, in0=sq, scalar=0.5, in1=work[:, 0],
                                         op0=ALU.mult, op1=ALU.add).then_inc(work_done, 1)
                dve.wait_ge(work_done, 4 * g + 4)
            for g in range(GROUPS):
                dve.wait_ge(prod, 2 * GROUPS + g + 1)
                dve.tensor_tensor(sc[:, pairs(g), 0, :], st.skew[:, pairs(g), :], product(g, 1), ALU.subtract
                                  ).then_inc(s_new, 1)
            with dve.Fori(0, SQUARINGS) as step:
                for g in range(GROUPS):
                    dve.wait_ge(prod, GROUPS * (step + 3) + g + 1)
                    dve.scalar_tensor_tensor(out=sc[:, pairs(g), 0, :], in0=sc[:, pairs(g), 0, :], scalar=2.0,
                                             in1=product(g, 2).rearrange("p q (w j) -> p q w j", w=2)[:, :, 1, :],
                                             op0=ALU.mult, op1=ALU.subtract).then_inc(s_new, 1)
            dve.wait_ge(s_new, GROUPS * (SQUARINGS + 1))
            dve.wait_ge(c_new, GROUPS * (SQUARINGS + 1))
            dve.tensor_tensor(st.skew[:], sc[:, :, 0, :], sc[:, :, 1, :], ALU.add).then_inc(rotation_done, 1)

        @block.tensor
        def _(pe):
            for g in range(GROUPS):
                wait_held(pe, g + 1)
                for q in range(GP):
                    i = g * GP + q
                    mm = pe.matmul(product(g, 1)[:, q, :], diag[:, i, :], st.skew[:, i, :], start=True, stop=True)
                mm.then_inc(prod, 1)
            for g in range(GROUPS):
                wait_held(pe, GROUPS + g + 1)
                for q in range(GP):
                    i = g * GP + q
                    mm = pe.matmul(product(g, 1)[:, q, :], diag[:, i, :], sc[:, i, 1, :], start=True, stop=True)
                mm.then_inc(prod, 1)
            for g in range(GROUPS):
                wait_held(pe, 2 * GROUPS + g + 1)
                pe.wait_ge(work_done, 4 * (g + 1))
                for q in range(GP):
                    i = g * GP + q
                    mm = pe.matmul(product(g, 1)[:, q, :], diag[:, i, :], taylor[:, i, :], start=True, stop=True)
                mm.then_inc(prod, 1)
            with pe.Fori(0, SQUARINGS) as step:
                for g in range(GROUPS):
                    wait_held(pe, GROUPS * (step + 3) + g + 1)
                    pe.wait_ge(c_new, GROUPS * step + g + 1)
                    for q in range(GP):
                        i = g * GP + q
                        mm = pe.matmul(product(g, 2)[:, q, :], diag[:, i, :], sc[:, i, :, :], start=True, stop=True)
                    mm.then_inc(prod, 1)


class Elimination:

    W = P + RK

    def __init__(self, m, st):
        self.st = st
        self.bank = m.banks("elim_ps", 1)[0]
        self.picked = m.sb("picked", [P, P])
        self.rows = m.sb("pivot_rows", [P, self.W])
        self.root = m.sb("root", [P, 1])
        self.sign2 = m.sb("sign2", [P, 1])
        self.weight = m.sb("weight", [P, 1])
        self.part = m.sb("part", [P, RK])
        self.inv = m.sb("inv", [P, 1])
        self.factor = m.sb("factor", [P, 1])
        self.update = m.sb("update", [P, P])
        self.gram_k = m.sb("gram_k", [P, 1])
        self.square_k = m.sb("square_k", [P, 1])
        self.part_k = m.sb("part_k", [P, 1])
        self.pivot = m.sb("pivot", [P, 1])
        self.below_k = m.sb("below_k", [P, 1])
        self.chosen = m.sem("pivot_chosen")
        self.spread = m.sem("pivot_spread")
        self.copied = m.sem("pivot_copied")

    def pe(self, pe, k):
        pe.wait_ge(self.chosen, k + 1)
        pe.matmul(self.bank[:, 0:P], self.st.ones_top[:], self.picked[:], start=True, stop=True)
        pe.matmul(self.bank[:, P:self.W], self.st.ones_low[:], self.picked[:, 0:RK],
                  start=True, stop=True).then_inc(self.spread, 1)

    def act(self, act, k):
        act.wait_ge(self.spread, k + 1)
        act.copy(self.rows[:], self.bank[:, 0:self.W])
        act.copy(self.gram_k[:], self.bank[:, bass.ds(k, 1)])
        act.copy(self.square_k[:], self.bank[:, bass.ds(k + P, 1)]).then_inc(self.copied, 1)

    def pool(self, pool, k):
        st, el = self.st, self.st.elim
        pool.tensor_tensor(self.picked[:], el[:], st.ident2[:, bass.ds(k, 1)].to_broadcast([P, P]), ALU.mult
                           ).then_inc(self.chosen, 1)
        pool.wait_ge(self.copied, k + 1)
        pool.tensor_tensor(self.root[:], self.gram_k[:], st.powers[:, 0:1], ALU.pow)
        pool.tensor_scalar(self.sign2[:], self.square_k[:], 0.0, st.half2[:], ALU.is_ge, ALU.mult)
        pool.tensor_tensor(self.below_k[:], el[:, bass.ds(k, 1)], st.below[:, bass.ds(k, 1)], ALU.mult)
        pool.drain()
        pool.tensor_scalar(self.weight[:], self.sign2[:], st.half1[:], self.root[:], ALU.subtract, ALU.mult)
        pool.drain()
        pool.tensor_scalar(self.part[:], self.rows[:, P:self.W], self.weight[:], None, ALU.mult)
        pool.tensor_tensor(self.part_k[:], self.square_k[:], self.weight[:], ALU.mult)
        pool.drain()
        pool.tensor_tensor(self.rows[:, 0:RK], self.rows[:, 0:RK], self.part[:], ALU.add)
        pool.tensor_tensor(self.pivot[:], self.gram_k[:], self.part_k[:], ALU.add)
        pool.drain()
        pool.tensor_tensor(self.inv[:], self.pivot[:], st.powers[:, 1:2], ALU.pow)
        pool.drain()
        pool.tensor_tensor(self.factor[:], self.below_k[:], self.inv[:], ALU.mult)
        pool.drain()
        pool.tensor_scalar(self.update[:], self.rows[:, 0:P], self.factor[:], None, ALU.mult)
        pool.drain()
        pool.tensor_tensor(el[:], el[:], self.update[:], ALU.add)
        pool.drain()


def basis(nc, st, io):
    with ExitStack() as ctx:
        m = Memory(nc, ctx)
        ps = m.banks("basis_ps", 5)
        prod = m.sb("diag_prod", [P, RK])
        pivots = m.sb("pivots", [P, 1])
        sign = m.sb("sign", [RK, 1])
        scale = m.sb("scale", [RK, 1])
        t_scaled = m.sb("t_scaled", [RK, RK])
        t_tr = m.sb("t_tr", [RK, RK])
        dve_step, pool_step, pe_step = m.sem("basis_dve"), m.sem("basis_pool"), m.sem("basis_pe")
        rotation_in = m.sem("rotation_in")
        block = ctx.enter_context(nc.Block())

        @block.sync
        def _(sp):
            skew_moves(sp, st, io, rotation_in, to_dram=False)
            sp.wait_ge(rotation_in, 32)

        @block.vector
        def _(dve):
            dve.tensor_tensor(prod[:], st.elim[:, 0:RK], st.ident2[:], ALU.mult).then_inc(dve_step, 1)
            dve.wait_ge(dve_step, 1)
            dve.reduce_sum(pivots[:], prod[:], AX_X).then_inc(dve_step, 1)
            dve.wait_ge(dve_step, 2)
            dve.tensor_scalar(sign[:], pivots[RK:P, :], 0.0, -2.0, ALU.is_ge, ALU.mult).then_inc(dve_step, 1)
            dve.wait_ge(pool_step, 1)
            dve.wait_ge(dve_step, 3)
            dve.tensor_scalar(scale[:], sign[:], 1.0, scale[:], ALU.add, ALU.mult).then_inc(dve_step, 1)
            dve.wait_ge(dve_step, 4)
            dve.tensor_scalar(t_scaled[:], st.elim[0:RK, RK:P], scale[:], None, ALU.mult).then_inc(dve_step, 1)
            dve.wait_ge(pe_step, 1)
            dve.tensor_copy(t_tr[:], ps[0][0:RK, 0:RK]).then_inc(dve_step, 1)
            dve.wait_ge(pe_step, 2)
            for t in range(3):
                rows = P if t < 2 else CR
                dve.tensor_copy(st.u[0:rows, t, :].rearrange("p (w k) -> p w k", w=2),
                                ps[1 + t][0:rows, 0:RK].unsqueeze(1).to_broadcast([rows, 2, RK])).then_inc(dve_step, 1)
            dve.tensor_copy(st.u_t[:], ps[4][0:RK, 0:C]).then_inc(dve_step, 1)

        @block.gpsimd
        def _(pool):
            pool.wait_ge(dve_step, 2)
            pool.tensor_tensor(scale[:], pivots[0:RK, :], st.minus_half[0:RK, 0:1], ALU.pow).then_inc(pool_step, 1)

        @block.tensor
        def _(pe):
            pe.wait_ge(dve_step, 5)
            pe.transpose(ps[0][0:RK, 0:RK], t_scaled[:], st.ident[0:RK, 0:RK]).then_inc(pe_step, 1)
            pe.wait_ge(dve_step, 6)
            for t in range(3):
                rows = P if t < 2 else CR
                pe.matmul(ps[1 + t][0:rows, 0:RK], st.p_t[:, t * P:t * P + rows], t_tr[:], start=True, stop=True)
            pe.matmul(ps[4][0:RK, 0:C], t_tr[:], st.p_t[:], start=True, stop=True).then_inc(pe_step, 1)


def is_last(g):
    return isinstance(g, int) and g == GROUPS - 1


class Jobs:

    def __init__(self, mem, name, banks, jobs, ahead=()):
        self.banks = banks
        n = len(banks)
        self.steady = {job: (i % n, i // n) for i, job in enumerate(jobs)}
        left = [job for job in jobs if job not in ahead]
        self.final = {job: (i % n, i // n) for i, job in enumerate(left)}
        self.first = {job: (i % n, i // n) for i, job in enumerate(ahead)}
        self.before = [len(range(b, len(ahead), n)) for b in range(n)]
        self.uses = [len(range(b, len(jobs), n)) for b in range(n)]
        self.full = [mem.sem(f"{name}_full{i}") for i in range(n)]
        self.free = [mem.sem(f"{name}_free{i}") for i in range(n)]

    def open(self, eng):
        for free in self.free:
            eng.sem_inc(free, 1)

    def at(self, g, job):
        if isinstance(g, int) and g < 0:
            return self.first[job]
        b, k = (self.final if is_last(g) else self.steady)[job]
        return b, g * self.uses[b] + k + self.before[b]

    def bank(self, g, job):
        return self.banks[self.at(g, job)[0]]

    def full_of(self, g, job):
        return self.full[self.at(g, job)[0]]

    def free_of(self, g, job):
        return self.free[self.at(g, job)[0]]

    def wait_free(self, eng, g, job):
        b, n = self.at(g, job)
        eng.wait_ge(self.free[b], n + 1)

    def wait_full(self, eng, g, job):
        b, n = self.at(g, job)
        eng.wait_ge(self.full[b], n + 1)

    def wait_taken(self, eng, g, job):
        b, n = self.at(g, job)
        eng.wait_ge(self.free[b], n + 2)


def for_groups(eng, body, first=0):
    for g in range(first):
        body(g)
    with eng.Fori(first, GROUPS - 1) as g:
        body(g)
    body(GROUPS - 1)


class Split:

    def __init__(self, m, name, tokens):
        self.hi = m.sb(f"{name}_hi", [P, 2, tokens], F32R)
        self.lo = m.sb(f"{name}_lo", [P, 2, tokens], F32R)
        self.rest = m.sb(f"{name}_rest", [KR, tokens], F32R)

    def ones(self, eng, sem):
        eng.memset(self.rest[3 * CR:KR, :].bitcast(F32), 1.0).then_inc(sem, 1)


def product(pe, out, acts, tokens, weights, cols, weights_held):
    w_hi, w_lo, w_r = weights
    terms = [(acts.hi[:, k, tokens], w_hi[:, k, cols]) for k in range(2)]
    terms += [(acts.hi[:, k, tokens], w_lo[:, k, cols]) for k in range(2)]
    terms += [(acts.lo[:, k, tokens], w_hi[:, k, cols]) for k in range(2)]
    terms += [(acts.rest[:, tokens], w_r[:, cols])]
    for i, (a, w) in enumerate(terms):
        held, streamed = (w, a) if weights_held else (a, w)
        mm = pe.matmul(out, held, streamed, start=(i == 0), stop=(i == len(terms) - 1))
    return mm


class Norm:

    def __init__(self, m, name, st, jobs, acts, shift, scale):
        self.st, self.jobs, self.acts, self.shift, self.scale = st, jobs, acts, shift, scale
        self.stats = m.sb(f"{name}_stats", [P, GP, 6])
        self.mv = m.sb(f"{name}_mean_var", [P, GP, 2])
        self.var = m.sb(f"{name}_var_eps", [P, GP])
        self.rstd = m.sb(f"{name}_rstd", [P, GP])
        self.xn = m.sb(f"{name}_xn", [P, GP, CD])
        self.h = m.sb(f"{name}_h", [P, 3, TG])
        self.aggr = m.sem(f"{name}_aggr_done")
        self.var_ready, self.rstd_ready = m.sem(f"{name}_var_ready"), m.sem(f"{name}_rstd_ready")
        self.xn_ready, self.scaled, self.shifted = m.sem(f"{name}_xn_ready"), m.sem(f"{name}_scaled"), m.sem(f"{name}_shifted")
        self.hi_ready, self.lo_ready = m.sem(f"{name}_hi_ready"), m.sem(f"{name}_lo_ready")

    def statistics(self, dve, g):
        x = self.st.x
        for p in range(GP):
            dve.bn_stats(self.stats[:, p, :], x[:, bass.ds(g * GP + p, 1), :].rearrange("p q c -> p (q c)"))
        dve.drain()
        for p in range(GP):
            dve.bn_aggr(self.mv[:, p, :], self.stats[:, p, :]).then_inc(self.aggr, 1)
        dve.wait_ge(self.aggr, g * GP + GP)
        dve.tensor_scalar(self.var[:], self.mv[:, :, 1], EPS, None, ALU.add).then_inc(self.var_ready, 1)

    def root(self, pool, g):
        pool.wait_ge(self.var_ready, g + 1)
        pool.tensor_tensor(self.rstd[:], self.var[:], self.st.minus_half[:], ALU.pow).then_inc(self.rstd_ready, 1)

    def normalize(self, dve, g):
        x = self.st.x
        dve.wait_ge(self.rstd_ready, g + 1)
        for p in range(GP):
            mean, rstd = self.mv[:, p, 0:1], self.rstd[:, p:p + 1]
            xg = x[:, bass.ds(g * GP + p, 1), :].rearrange("p q c -> p (q c)")
            dve.tensor_scalar(self.xn[:, p, 0:C], xg, mean, rstd, ALU.subtract, ALU.mult).then_inc(self.xn_ready, 1)
            dve.tensor_scalar(self.xn[:, p, C:CD].rearrange("p (r c) -> p r c", r=2),
                              x[:, bass.ds(g * GP + p, 1), 2 * P:C].to_broadcast([P, 2, CR]), mean, rstd,
                              ALU.subtract, ALU.mult).then_inc(self.xn_ready, 1)

    def transposes(self, pe, g, at):
        pe.wait_ge(self.xn_ready, (g + 1) * 2 * GP)
        for t in range(3):
            rows = P if t < 2 else 3 * CR
            job = ("ln", t)
            self.jobs.wait_free(pe, at, job)
            for p in range(GP):
                mm = pe.transpose(self.jobs.bank(at, job)[0:rows, p * P:(p + 1) * P],
                                  self.xn[:, p, t * P:t * P + rows], self.st.ident[:])
            mm.then_inc(self.jobs.full_of(at, job), 1)

    def rows(self, t):
        return P if t < 2 else 3 * CR

    def by(self, n, g, t):
        return self.st.mod_t[0:self.rows(t), n, t, bass.ds(g * GB, GB)].unsqueeze(2).to_broadcast([self.rows(t), GB, L])

    def scale_up(self, dve, g, at):
        for t in range(3):
            job = ("ln", t)
            self.jobs.wait_full(dve, at, job)
            dve.tensor_tensor(self.h[0:self.rows(t), t, :].rearrange("p (b l) -> p b l", l=L),
                              self.jobs.bank(at, job)[0:self.rows(t), :].rearrange("p (b l) -> p b l", l=L),
                              self.by(self.scale, g, t), ALU.mult).then_inc(self.jobs.free_of(at, job), 1)

    def shift_by(self, dve, g, at):
        for t in range(3):
            h = self.h[0:self.rows(t), t, :].rearrange("p (b l) -> p b l", l=L)
            self.jobs.wait_taken(dve, at, ("ln", t))
            dve.tensor_tensor(h, h, self.by(self.shift, g, t), ALU.add).then_inc(self.shifted, 1)

    def high(self, act, g):
        for t in range(3):
            act.wait_ge(self.shifted, g * 3 + t + 1)
            out = self.acts.hi[:, t, :] if t < 2 else self.acts.rest[0:3 * CR, :]
            act.copy(out, self.h[0:P if t < 2 else 3 * CR, t, :]).then_inc(self.hi_ready, 1)

    def low(self, eng, g, drain=False):
        for t in range(3):
            if t == 2 and drain:
                eng.drain()
            eng.wait_ge(self.hi_ready, g * 3 + t + 1)
            if t < 2:
                out, hi, h = self.acts.lo[:, t, :], self.acts.hi[:, t, :], self.h[:, t, :]
            else:
                r = slice(2 * CR, 3 * CR)
                out, hi, h = self.acts.rest[r, :], self.acts.rest[r, :], self.h[r, t, :]
            eng.tensor_tensor(out, h, hi.bitcast(F32), ALU.subtract).then_inc(self.lo_ready, 1)
        if drain:
            eng.drain()

    def wait_acts(self, eng, g):
        eng.wait_ge(self.lo_ready, 3 * (g + 1))


def gate_loads(sp, nc, io, which, gate, loaded, used):
    src = io["gates"].rearrange("(q b) s c -> b s q c", b=2)
    with sp.Fori(0, GROUPS) as g:
        sp.wait_ge(used, g * GP + 1)
        for b in range(2):
            sp.dma_start(gate[L * b:L * (b + 1), :, :],
                         src[b, which, bass.ds(g * GP, GP), :].unsqueeze(0).to_broadcast([L, GP, C])
                         ).then_inc(loaded, 16)


def attention(nc, st, io, elim):
    with ExitStack() as ctx:
        m = Memory(nc, ctx)
        banks = m.banks("att_ps", 5)
        scores = ctx.enter_context(nc.psum_tensor("scores", [P, 2, BANK], F32))
        HP = H // 2
        T = H // 4
        VW = 2 * D + 1

        qk = lambda t: [("q", t), ("k", t)]
        weigh = lambda t: [("pt", t, 0), ("pt", t, 1), ("o", t, 0), ("o", t, 1)]
        ln, v = [("ln", t) for t in range(3)], [("v", p) for p in range(GP)]
        names = qk(2) + weigh(0) + ln + qk(3) + weigh(1) + weigh(2) + qk(0) + weigh(3) + v
        names += [("ot", t) for t in range(3)] + qk(1) + [("proj", p) for p in range(GP)]
        jobs = Jobs(m, "att", banks, names, ln + qk(0) + v + qk(1))

        acts = Split(m, "h1", TG)
        norm = Norm(m, "ln1", st, jobs, acts, 0, 1)
        q_diag = m.sb("q_diag", [P, 2, 2, GB, 2, L])
        k_t = m.sb("k_t", [P, 2, TG])
        va = m.sb("va", [P, GP, HP, 2, VW])
        prob = m.sb("prob", [P, 2, 2, TG])
        row_max = m.sb("row_max", [P, 2, 2, GB])
        prob_t = m.sb("prob_t", [P, 2, TG])
        rsum = m.sb("rsum", [P, 2, GP, 2])
        o = m.sb("o", [P, GP, CD])
        o_t = Split(m, "o_t", TG)
        gated = m.sb("gated", [P, 2, C])
        gate = m.sb("gate", [P, GP, C])

        begun, zeroed, gate_in = m.sem("att_begun"), m.sem("att_zeroed"), m.sem("gate_in")
        scored, max_done, less_max = m.sem("scored"), m.sem("max_done"), m.sem("less_max")
        exp_done, inverted, o_ready = m.sem("exp_done"), m.sem("inverted"), m.sem("o_ready")
        o_hi, o_lo, added = m.sem("o_hi"), m.sem("o_lo"), m.sem("added")

        def turn(g, t):
            return g * T + t

        def before(g, t):
            return g - 1 if t < 2 else g

        def rows_of(t):
            return P if t < 2 else 3 * CR

        def step_of(g, i):
            return g * ELIM_ATT + i

        block = ctx.enter_context(nc.Block())

        @block.sync
        def _(sp):
            gate_loads(sp, nc, io, 0, gate, gate_in, added)

        @block.gpsimd
        def _(pool):
            pool.memset(va[:], 0.0).then_inc(zeroed, 1)
            pool.drain()
            norm.root(pool, 0)

            def body(g):
                if not is_last(g):
                    norm.root(pool, g + 1)
                for i in range(ELIM_ATT):
                    elim.pool(pool, step_of(g, i))
            for_groups(pool, body)

        @block.scalar
        def _(act):
            def take_qk(g, t, at):
                jobs.wait_full(act, at, ("q", t))
                for r in range(4):
                    rows = slice(DP * r, DP * (r + 1))
                    cp = act.copy(q_diag[rows, t % 2, r // 2, :, r % 2, :],
                                  jobs.bank(at, ("q", t))[rows, :].rearrange("p (s l) -> p s l", l=L))
                cp.then_inc(jobs.free_of(at, ("q", t)), 1)
                jobs.wait_full(act, at, ("k", t))
                act.copy(k_t[:, t % 2, :], jobs.bank(at, ("k", t))[:]).then_inc(jobs.free_of(at, ("k", t)), 1)

            def take_v(at, p):
                job = ("v", p)
                jobs.wait_full(act, at, job)
                for b in range(2):
                    rows = slice(L * b, L * (b + 1))
                    cp = act.copy(va[rows, p, :, b, 0:2 * D],
                                  jobs.bank(at, job)[rows, 0:C].rearrange("p (i d) -> p i d", d=2 * D))
                cp.then_inc(jobs.free_of(at, job), 1)

            def exponential(g, t):
                n = turn(g, t)
                act.wait_ge(less_max, n + 2)
                act.activation(prob[:, t % 2], prob[:, t % 2], ACT.Exp, scale=SCALE).then_inc(exp_done, 1)

            def take_prob_t(g, t):
                for i in range(2):
                    job = ("pt", t, i)
                    jobs.wait_full(act, g, job)
                    act.copy(prob_t[:, i, :], jobs.bank(g, job)[:]).then_inc(jobs.free_of(g, job), 1)

            def repeat_rest(g):
                jobs.wait_taken(act, g, ("o", T - 1, 1))
                act.copy(o[:, :, C:CD].rearrange("p g (r c) -> p g r c", r=2),
                         o[:, :, 2 * P:C].unsqueeze(2).to_broadcast([P, GP, 2, CR])).then_inc(o_ready, 1)

            def o_high(g):
                for t in range(3):
                    jobs.wait_full(act, g, ("ot", t))
                    out = o_t.hi[:, t, :] if t < 2 else o_t.rest[0:3 * CR, :]
                    act.copy(out, jobs.bank(g, ("ot", t))[0:rows_of(t), :]).then_inc(o_hi, 1)

            act.wait_ge(begun, 1)
            norm.high(act, 0)
            take_qk(0, 0, -1)
            act.wait_ge(zeroed, 1)
            for p in range(GP):
                take_v(-1, p)
            exponential(0, 0)
            take_qk(0, 1, -1)

            def body(g):
                ahead = not is_last(g)
                take_qk(g, 2, g)
                take_prob_t(g, 0)
                exponential(g, 1)
                elim.act(act, step_of(g, 0))
                take_qk(g, 3, g)
                take_prob_t(g, 1)
                exponential(g, 2)
                elim.act(act, step_of(g, 1))
                if ahead:
                    norm.high(act, g + 1)
                take_prob_t(g, 2)
                exponential(g, 3)
                if ahead:
                    take_qk(g + 1, 0, g)
                take_prob_t(g, 3)
                elim.act(act, step_of(g, 2))
                repeat_rest(g)
                if ahead:
                    take_v(g, 0)
                    exponential(g + 1, 0)
                    for p in range(1, GP):
                        take_v(g, p)
                o_high(g)
                if ahead:
                    take_qk(g + 1, 1, g)
                elim.act(act, step_of(g, 3))
            for_groups(act, body)

        @block.vector
        def _(dve):
            dve.memset(q_diag[:], 0.0).then_inc(begun, 1)
            acts.ones(dve, begun)
            o_t.ones(dve, begun)
            jobs.open(dve)
            dve.sem_inc(less_max, 1)
            dve.sem_inc(added, 1)
            norm.statistics(dve, 0)
            norm.normalize(dve, 0)
            dve.wait_ge(zeroed, 1)
            for b in range(2):
                dve.memset(va[L * b:L * (b + 1), :, :, b, 2 * D].rearrange("p g q -> p (g q)"), 1.0).then_inc(begun, 1)
            norm.scale_up(dve, 0, -1)
            norm.shift_by(dve, 0, -1)
            norm.low(dve, 0)

            def softmax_max(g, t):
                n = turn(g, t)
                s = scores[:].rearrange("p i (s m) -> p i s m", m=L)
                dve.wait_ge(scored, n + 1)
                dve.tensor_reduce(row_max[:, t % 2], s, AX_X, ALU.max).then_inc(max_done, 1)
                dve.wait_ge(max_done, n + 1)
                dve.tensor_tensor(prob[:, t % 2].rearrange("p i (s m) -> p i s m", m=L), s,
                                  row_max[:, t % 2].unsqueeze(3).to_broadcast([P, 2, GB, L]), ALU.subtract
                                  ).then_inc(less_max, 1)

            def take_o(g, t):
                for i in range(2):
                    job = ("o", t, i)
                    jobs.wait_full(dve, g, job)
                    src = jobs.bank(g, job)[:, 0:GP * 2 * VW].rearrange("p (g b d) -> p g b d", b=2, d=VW)
                    dve.reciprocal(rsum[:, i], src[:, :, :, 2 * D]).then_inc(inverted, 1)
                    dve.wait_ge(inverted, turn(g, t) * 2 + i + 1)
                    for w in range(2):
                        rows = slice(L * w, L * (w + 1))
                        h = 4 * t + 2 * i + w
                        for b in range(2):
                            tt = dve.tensor_tensor(o[L * b:L * (b + 1), :, h * D:(h + 1) * D],
                                                   src[rows, :, b, w * D:(w + 1) * D],
                                                   rsum[rows, i, :, b:b + 1].to_broadcast([L, GP, D]), ALU.mult)
                    tt.then_inc(jobs.free_of(g, job), 1)

            def o_low(g):
                for t in range(3):
                    bank = jobs.bank(g, ("ot", t))
                    dve.wait_ge(o_hi, g * 3 + t + 1)
                    r = slice(0, P) if t < 2 else slice(2 * CR, 3 * CR)
                    out, hi = (o_t.lo[:, t, :], o_t.hi[:, t, :]) if t < 2 else (o_t.rest[r, :], o_t.rest[r, :])
                    dve.tensor_tensor(out, bank[r, :], hi.bitcast(F32), ALU.subtract
                                      ).then_inc(jobs.free_of(g, ("ot", t)), 1)

            def residual(g, p):
                n = g * GP + p
                job = ("proj", p)
                xg = st.x[:, bass.ds(n, 1), :].rearrange("p q c -> p (q c)")
                jobs.wait_full(dve, g, job)
                if p == 0:
                    dve.wait_ge(gate_in, 32 * (g + 1))
                dve.tensor_tensor(gated[:, p % 2, :], jobs.bank(g, job)[:, 0:C], gate[:, p, :], ALU.mult
                                  ).then_inc(jobs.free_of(g, job), 1)
                jobs.wait_taken(dve, g, job)
                dve.tensor_tensor(xg, xg, gated[:, p % 2, :], ALU.add).then_inc(added, 1)

            softmax_max(0, 0)

            def body(g):
                ahead = not is_last(g)
                if ahead:
                    norm.statistics(dve, g + 1)
                softmax_max(g, 1)
                if ahead:
                    norm.normalize(dve, g + 1)
                take_o(g, 0)
                if ahead:
                    norm.scale_up(dve, g + 1, g)
                softmax_max(g, 2)
                if ahead:
                    norm.shift_by(dve, g + 1, g)
                take_o(g, 1)
                softmax_max(g, 3)
                if ahead:
                    norm.low(dve, g + 1)
                take_o(g, 2)
                take_o(g, 3)
                if ahead:
                    softmax_max(g + 1, 0)
                o_low(g)
                for p in range(GP):
                    residual(g, p)
            for_groups(dve, body)

        @block.tensor
        def _(pe):
            def project_qk(g, t, at):
                for w in range(2):
                    job = ("qk"[w], t)
                    jobs.wait_free(pe, at, job)
                    c = (w * T + t) * P
                    product(pe, jobs.bank(at, job)[:], acts, slice(0, TG), (st.wqk_hi, st.wqk_lo, st.wqk_r),
                            slice(c, c + P), True).then_inc(jobs.full_of(at, job), 1)

            def project_v(g, at):
                for p in range(GP):
                    job = ("v", p)
                    jobs.wait_free(pe, at, job)
                    product(pe, jobs.bank(at, job)[:, 0:C], acts, slice(p * P, (p + 1) * P),
                            (st.wv_hi, st.wv_lo, st.wv_r), slice(0, C), False).then_inc(jobs.full_of(at, job), 1)

            def score(g, t, at):
                jobs.wait_taken(pe, at, ("q", t))
                jobs.wait_taken(pe, at, ("k", t))
                pe.wait_ge(less_max, turn(g, t) + 1)
                for i in range(2):
                    for s in range(GB):
                        tok = slice(s * L, (s + 1) * L)
                        mm = pe.matmul(scores[:, i, tok], q_diag[:, t % 2, i, s, :, :], k_t[:, t % 2, tok],
                                       start=True, stop=True)
                mm.then_inc(scored, 1)

            def transpose_prob(g, t):
                pe.wait_ge(exp_done, turn(g, t) + 1)
                for i in range(2):
                    job = ("pt", t, i)
                    jobs.wait_free(pe, g, job)
                    for p in range(GP):
                        mm = pe.transpose(jobs.bank(g, job)[:, p * P:(p + 1) * P],
                                          prob[:, t % 2, i, p * P:(p + 1) * P], st.ident[:])
                    mm.then_inc(jobs.full_of(g, job), 1)

            def weigh_v(g, t):
                if t == 0:
                    jobs.wait_taken(pe, g - 1, ("v", GP - 1))
                for i in range(2):
                    job = ("o", t, i)
                    jobs.wait_taken(pe, g, ("pt", t, i))
                    jobs.wait_free(pe, g, job)
                    for p in range(GP):
                        mm = pe.matmul(jobs.bank(g, job)[:, p * 2 * VW:(p + 1) * 2 * VW],
                                       prob_t[:, i, p * P:(p + 1) * P], va[:, p, 2 * t + i, :, :],
                                       start=True, stop=True)
                    mm.then_inc(jobs.full_of(g, job), 1)

            def transpose_o(g):
                pe.wait_ge(o_ready, g + 1)
                for t in range(3):
                    jobs.wait_free(pe, g, ("ot", t))
                    for p in range(GP):
                        mm = pe.transpose(jobs.bank(g, ("ot", t))[0:rows_of(t), p * P:(p + 1) * P],
                                          o[:, p, t * P:t * P + rows_of(t)], st.ident[:])
                    mm.then_inc(jobs.full_of(g, ("ot", t)), 1)

            def project(g):
                for t in range(3):
                    jobs.wait_taken(pe, g, ("ot", t))
                for p in range(GP):
                    job = ("proj", p)
                    jobs.wait_free(pe, g, job)
                    product(pe, jobs.bank(g, job)[:, 0:C], o_t, slice(p * P, (p + 1) * P),
                            (st.wp_hi, st.wp_lo, st.wp_r), slice(0, C), False).then_inc(jobs.full_of(g, job), 1)

            pe.wait_ge(begun, 5)
            norm.transposes(pe, 0, -1)
            norm.wait_acts(pe, 0)
            project_qk(0, 0, -1)
            score(0, 0, -1)
            project_v(0, -1)
            project_qk(0, 1, -1)

            def body(g):
                ahead = not is_last(g)
                score(g, 1, g - 1)
                project_qk(g, 2, g)
                transpose_prob(g, 0)
                elim.pe(pe, step_of(g, 0))
                weigh_v(g, 0)
                if ahead:
                    norm.transposes(pe, g + 1, g)
                score(g, 2, g)
                project_qk(g, 3, g)
                transpose_prob(g, 1)
                elim.pe(pe, step_of(g, 1))
                weigh_v(g, 1)
                score(g, 3, g)
                transpose_prob(g, 2)
                weigh_v(g, 2)
                if ahead:
                    norm.wait_acts(pe, g + 1)
                    project_qk(g + 1, 0, g)
                transpose_prob(g, 3)
                elim.pe(pe, step_of(g, 2))
                weigh_v(g, 3)
                if ahead:
                    score(g + 1, 0, g)
                    project_v(g + 1, g)
                transpose_o(g)
                if ahead:
                    project_qk(g + 1, 1, g)
                elim.pe(pe, step_of(g, 3))
                project(g)
            for_groups(pe, body, 1)


def mlp(nc, st, io, elim):
    with ExitStack() as ctx:
        m = Memory(nc, ctx)
        ln = [("ln", t) for t in range(3)]
        jobs = Jobs(m, "mlp", m.banks("mlp_ps", 7), [("fc1", f) for f in range(FT)] + ln + [("fc2", p) for p in range(GP)], ln)
        acts = Split(m, "h2", TG)
        norm = Norm(m, "ln2", st, jobs, acts, 2, 3)
        NG = 3
        g32 = m.sb("g32", [P, NG, TG])
        g_hi, g_lo = m.sb("g_hi", [P, FT, TG], F32R), m.sb("g_lo", [P, FT, TG], F32R)
        gated = m.sb("gated2", [P, 2, C])
        gate = m.sb("gate2", [P, GP, C])
        begun, gate_in, added = m.sem("mlp_begun"), m.sem("gate2_in"), m.sem("added2")
        g_lo_done = m.sem("g_lo_done")

        def step_of(g, i):
            return ELIM_ATT * GROUPS + g * ELIM_MLP + i


        block = ctx.enter_context(nc.Block())

        @block.sync
        def _(sp):
            gate_loads(sp, nc, io, 1, gate, gate_in, added)

        @block.gpsimd
        def _(pool):
            norm.root(pool, 0)

            def body(g):
                for i in range(ELIM_MLP):
                    if i == 1 and not isinstance(g, int):
                        norm.root(pool, g + 1)
                    elim.pool(pool, step_of(g, i))
            for_groups(pool, body)

        @block.scalar
        def _(act):
            norm.high(act, 0)

            def body(g):
                for f in range(FT):
                    job = ("fc1", f)
                    bank = jobs.bank(g, job)
                    jobs.wait_full(act, g, job)
                    act.wait_ge(g_lo_done, g * FT + f + 1)
                    act.activation(g32[:, f % NG, :], bank[:], ACT.Gelu_apprx_tanh)
                    act.activation(g_hi[:, f, :], bank[:], ACT.Gelu_apprx_tanh
                                   ).then_inc(jobs.free_of(g, job), 1)
                    if f in (1, 6):
                        elim.act(act, step_of(g, f // 6))
                elim.act(act, step_of(g, 2))
                if not is_last(g):
                    norm.high(act, g + 1)
                elim.act(act, step_of(g, 3))
            for_groups(act, body)

        @block.vector
        def _(dve):
            acts.ones(dve, begun)
            jobs.open(dve)
            dve.sem_inc(added, 1)
            dve.sem_inc(g_lo_done, NG)
            norm.statistics(dve, 0)
            norm.normalize(dve, 0)
            norm.scale_up(dve, 0, -1)
            norm.shift_by(dve, 0, -1)
            norm.low(dve, 0)

            def low(g, f):
                jobs.wait_taken(dve, g, ("fc1", f))
                dve.tensor_tensor(g_lo[:, f, :], g32[:, f % NG, :], g_hi[:, f, :].bitcast(F32), ALU.subtract
                                  ).then_inc(g_lo_done, 1)

            def residual(g, p):
                n = g * GP + p
                job = ("fc2", p)
                xg = st.x[:, bass.ds(n, 1), :].rearrange("p q c -> p (q c)")
                jobs.wait_full(dve, g, job)
                if p == 0:
                    dve.wait_ge(gate_in, 32 * (g + 1))
                dve.tensor_tensor(gated[:, p % 2, :], jobs.bank(g, job)[:, 0:C], gate[:, p, :], ALU.mult
                                  ).then_inc(jobs.free_of(g, job), 1)
                jobs.wait_taken(dve, g, job)
                dve.tensor_tensor(xg, xg, gated[:, p % 2, :], ALU.add).then_inc(added, 1)

            def body(g):
                ahead = not is_last(g)
                for f in range(FT):
                    low(g, f)
                    if f == 1 and ahead:
                        norm.statistics(dve, g + 1)
                    if f == 5 and ahead:
                        norm.normalize(dve, g + 1)
                if ahead:
                    norm.scale_up(dve, g + 1, g)
                    norm.shift_by(dve, g + 1, g)
                for p in range(GP):
                    if p == 1 and ahead:
                        norm.low(dve, g + 1)
                    residual(g, p)
            for_groups(dve, body)

        @block.tensor
        def _(pe):
            pe.wait_ge(begun, 1)
            norm.transposes(pe, 0, -1)

            def down(g, p):
                job, tok = ("fc2", p), slice(p * P, (p + 1) * P)
                jobs.wait_free(pe, g, job)
                if p == 0:
                    pe.wait_ge(g_lo_done, (g + 1) * FT + NG)
                out = jobs.bank(g, job)[:, 0:C]
                pe.matmul(out, st.ones2[:], st.b2[:], start=True, stop=False)
                for f in range(FT):
                    pe.matmul(out, g_hi[:, f, tok], st.w2_hi[:, f, :], start=False, stop=False)
                    pe.matmul(out, g_hi[:, f, tok], st.w2_lo[:, f, :], start=False, stop=False)
                    mm = pe.matmul(out, g_lo[:, f, tok], st.w2_hi[:, f, :], start=False, stop=(f == FT - 1))
                mm.then_inc(jobs.full_of(g, job), 1)

            def body(g):
                norm.wait_acts(pe, g)
                for f in range(FT):
                    job = ("fc1", f)
                    jobs.wait_free(pe, g, job)
                    product(pe, jobs.bank(g, job)[:], acts, slice(0, TG), (st.w1_hi, st.w1_lo, st.w1_r),
                            slice(f * P, (f + 1) * P), True).then_inc(jobs.full_of(g, job), 1)
                    if f in (1, 6):
                        elim.pe(pe, step_of(g, f // 6))
                if not is_last(g):
                    norm.transposes(pe, g + 1, g)
                for p in range(GP):
                    down(g, p)
                    if p in (0, 2):
                        elim.pe(pe, step_of(g, 2 + p // 2))
            for_groups(pe, body)


def rotate(nc, st, io):
    with ExitStack() as ctx:
        m = Memory(nc, ctx)
        xs, dz, out = [("x", t) for t in range(3)], [("dz", 0), ("dz", 1)], [("out", p) for p in range(GP)]
        jobs = Jobs(m, "rot", m.banks("rot_ps", 8), xs + dz + [("z",)] + out, xs + [("z",)])
        x_s = m.sb("x_s", [P, GP, C])
        e_s = m.sb("e_s", [P, GP, 2, RK])
        x_t = m.sb("x_t", [P, 3, TG])
        z_t = m.sb("z_t", [P, TG])
        dz_t = m.sb("dz_t", [RK, TG])
        copied, e_copied, done, stored = m.sem("x_copied"), m.sem("e_copied"), m.sem("rot_done"), m.sem("stored")
        block = ctx.enter_context(nc.Block())

        def rows_of(t):
            return P if t < 2 else CR

        @block.sync
        def _(sp):
            dst = io["out"].rearrange("(q b) l c -> (b l) q c", b=2)
            with sp.Fori(0, GROUPS) as g:
                sp.wait_ge(done, g + 1)
                sp.dma_start(dst[:, bass.ds(g * GP, GP), :], st.x[:, bass.ds(g * GP, GP), :]).then_inc(stored, 16)
            sp.wait_ge(stored, 16 * GROUPS)

        @block.scalar
        def _(act):
            def stage_x(g):
                act.copy(x_s[:], st.x[:, bass.ds(g * GP, GP), :]).then_inc(copied, 1)

            def stage_e(g):
                act.copy(e_s[:], st.skew[:, bass.ds(g * GP, GP), :].unsqueeze(2).to_broadcast([P, GP, 2, RK])
                         ).then_inc(e_copied, 1)

            def take_x(at):
                for t in (0, 2):
                    jobs.wait_full(act, at, ("x", t))
                    act.copy(x_t[0:rows_of(t), t, :], jobs.bank(at, ("x", t))[0:rows_of(t), :]
                             ).then_inc(jobs.free_of(at, ("x", t)), 1)

            stage_x(0)
            stage_e(0)
            take_x(-1)

            def body(g):
                if not is_last(g):
                    stage_x(g + 1)
                    take_x(g)
                    jobs.wait_full(act, g, ("dz", 1))
                    stage_e(g + 1)
            for_groups(act, body)

        @block.vector
        def _(dve):
            def take_x(at):
                jobs.wait_full(dve, at, ("x", 1))
                dve.tensor_copy(x_t[:, 1, :], jobs.bank(at, ("x", 1))[:]).then_inc(jobs.free_of(at, ("x", 1)), 1)

            def take_z(at):
                jobs.wait_full(dve, at, ("z",))
                dve.tensor_copy(z_t[:], jobs.bank(at, ("z",))[:]).then_inc(jobs.free_of(at, ("z",)), 1)

            jobs.open(dve)
            take_x(-1)
            take_z(-1)

            def body(g):
                if not is_last(g):
                    take_x(g)
                for b in range(2):
                    jobs.wait_full(dve, g, ("dz", b))
                    dve.tensor_copy(dz_t[:].rearrange("k (q b l) -> k q b l", b=2, l=L)[:, :, b, :],
                                    jobs.bank(g, ("dz", b))[0:RK, 0:GP * L].rearrange("k (q l) -> k q l", l=L)
                                    ).then_inc(jobs.free_of(g, ("dz", b)), 1)
                if not is_last(g):
                    take_z(g)
                for p in range(GP):
                    job = ("out", p)
                    xg = st.x[:, bass.ds(g * GP + p, 1), :].rearrange("p q c -> p (q c)")
                    jobs.wait_full(dve, g, job)
                    dve.tensor_tensor(xg, xg, jobs.bank(g, job)[:, 0:C], ALU.add).then_inc(jobs.free_of(g, job), 1)
                jobs.wait_taken(dve, g, ("out", GP - 1))
                dve.sem_inc(done, 1)
            for_groups(dve, body)

        @block.tensor
        def _(pe):
            def transpose_x(g, at):
                pe.wait_ge(copied, g + 1)
                for t in range(3):
                    jobs.wait_free(pe, at, ("x", t))
                    for p in range(GP):
                        mm = pe.transpose(jobs.bank(at, ("x", t))[0:rows_of(t), p * P:(p + 1) * P],
                                          x_s[:, p, t * P:t * P + rows_of(t)], st.ident[:])
                    mm.then_inc(jobs.full_of(at, ("x", t)), 1)

            def into_subspace(at):
                jobs.wait_free(pe, at, ("z",))
                for t in range(3):
                    jobs.wait_taken(pe, at, ("x", t))
                    mm = pe.matmul(jobs.bank(at, ("z",))[:], st.u[0:rows_of(t), t, :], x_t[0:rows_of(t), t, :],
                                   start=(t == 0), stop=(t == 2))
                mm.then_inc(jobs.full_of(at, ("z",)), 1)

            def rotation(g):
                jobs.wait_taken(pe, g - 1, ("z",))
                pe.wait_ge(e_copied, g + 1)
                for b in range(2):
                    rows = slice(L * b, L * (b + 1))
                    jobs.wait_free(pe, g, ("dz", b))
                    for p in range(GP):
                        tok = slice(p * P + L * b, p * P + L * (b + 1))
                        mm = pe.matmul(jobs.bank(g, ("dz", b))[:, p * L:(p + 1) * L], e_s[rows, p, :, :],
                                       z_t[rows, tok], start=True, stop=True)
                    mm.then_inc(jobs.full_of(g, ("dz", b)), 1)

            def out_of_subspace(g):
                for b in range(2):
                    jobs.wait_taken(pe, g, ("dz", b))
                for p in range(GP):
                    job = ("out", p)
                    jobs.wait_free(pe, g, job)
                    pe.matmul(jobs.bank(g, job)[:, 0:C], dz_t[:, p * P:(p + 1) * P], st.u_t[:], start=True, stop=True
                              ).then_inc(jobs.full_of(g, job), 1)

            transpose_x(0, -1)
            into_subspace(-1)

            def body(g):
                if not is_last(g):
                    transpose_x(g + 1, g)
                rotation(g)
                if not is_last(g):
                    into_subspace(g)
                out_of_subspace(g)
            for_groups(pe, body, 1)


class State:
    pass


def state(nc, ctx):
    m, st = Memory(nc, ctx), State()
    st.x = m.sb("x", [P, PAIRS, C])
    st.ident = m.sb("ident", [P, P])
    st.ident2 = m.sb("ident2", [P, RK])
    st.below = m.sb("below", [P, RK])
    st.half1, st.half2 = m.sb("half1", [P, 1]), m.sb("half2", [P, 1])
    st.lowrow = m.sb("lowrow", [P, 2])
    st.sel2 = m.sb("sel2", [2, 2])
    st.ones = m.sb("ones", [P, 1])
    st.ones_top, st.ones_low = m.sb("ones_top", [P, P]), m.sb("ones_low", [P, P])
    st.minus_half = m.sb("minus_half", [P, GP])
    st.powers = m.sb("powers", [P, 2])
    st.elim = m.sb("elim", [P, P])
    st.p_t = m.sb("p_t", [RK, C])
    st.mod_t = m.sb("mod_t", [P, 4, 3, B])
    return st


def weight_state(nc, ctx, st):
    m = Memory(nc, ctx)
    st.wqk_hi, st.wqk_lo = m.sb("wqk_hi", [P, 2, 2 * H * DP], F32R), m.sb("wqk_lo", [P, 2, 2 * H * DP], F32R)
    st.wqk_r = m.sb("wqk_r", [KR, 2 * H * DP], F32R)
    st.wv_hi, st.wv_lo, st.wv_r = m.sb("wv_hi", [P, 2, C], F32R), m.sb("wv_lo", [P, 2, C], F32R), m.sb("wv_r", [KR, C], F32R)
    st.wp_hi, st.wp_lo, st.wp_r = m.sb("wp_hi", [P, 2, C], F32R), m.sb("wp_lo", [P, 2, C], F32R), m.sb("wp_r", [KR, C], F32R)
    st.w1_hi, st.w1_lo, st.w1_r = m.sb("w1_hi", [P, 2, FF], F32R), m.sb("w1_lo", [P, 2, FF], F32R), m.sb("w1_r", [KR, FF], F32R)
    st.w2_hi, st.w2_lo = m.sb("w2_hi", [P, FT, C], F32R), m.sb("w2_lo", [P, FT, C], F32R)
    st.b2, st.ones2 = m.sb("b2", [P, C], F32R), m.sb("ones2", [P, P], F32R)


def skew_state(nc, ctx, st):
    st.skew = Memory(nc, ctx).sb("skew", [P, PAIRS, RK])


def basis_state(nc, ctx, st):
    m = Memory(nc, ctx)
    st.skew = m.sb("rotation", [P, PAIRS, RK])
    st.u = m.sb("u", [P, 3, 2 * RK])
    st.u_t = m.sb("u_t", [RK, C])


def program(nc, io):
    io["gates"] = nc.dram_tensor("gates", (B, 2, C), F32, kind="Internal").ap()
    io["skew"] = nc.dram_tensor("skew_dram", (B, RK, RK), F32, kind="Internal").ap()
    with ExitStack() as ctx:
        st = state(nc, ctx)
        setup(nc, Memory(nc, ctx), st, io)
        weight_state(nc, ctx, st)
        with ExitStack() as inner:
            skew_state(nc, inner, st)
            split_weights(nc, st, io)
            rotations(nc, st, io)
        with ExitStack() as inner:
            elim = Elimination(Memory(nc, inner), st)
            attention(nc, st, io, elim)
            mlp(nc, st, io, elim)
        basis_state(nc, ctx, st)
        basis(nc, st, io)
        rotate(nc, st, io)


_INS = ["x", "cond_1152", "L0_cond_W_qkv", "L0_cond_b_qkv", "L0_cond_W_proj", "L0_cond_b_proj", "L0_cond_W_fc1",
        "L0_cond_b_fc1", "L0_cond_W_fc2", "L0_cond_b_fc2", "L0_cond_W_ada", "L0_cond_b_ada", "L1_cond_P",
        "L1_cond_W", "L1_cond_b"]


def kernel(**inputs):
    import numpy as _np
    import concourse.bacc as _bacc
    from concourse import mybir as _mybir
    from concourse.bass_utils import run_bass_kernel_spmd as _run

    nc = _bacc.Bacc("TRN2", target_bir_lowering=False, num_devices=1)
    arrays, io = {}, {}
    for name in _INS:
        a = _np.ascontiguousarray(inputs[name])
        arrays[f"in_{name}_dram"] = a
        io[name] = nc.dram_tensor(f"in_{name}_dram", a.shape, _mybir.dt.from_np(a.dtype), kind="ExternalInput").ap()
    io["out"] = nc.dram_tensor("out_0_dram", (64, 64, 288), _mybir.dt.float32, kind="ExternalOutput").ap()
    program(nc, io)
    r = _run(nc, [arrays], core_ids=[0])
    return r.results[0]["out_0_dram"]
```

```python
from contextlib import ExitStack

import concourse.bass as bass
from concourse import mybir

ALU = mybir.AluOpType
ACT = mybir.ActivationFunctionType
AX_X = mybir.AxisListType.X
F32 = mybir.dt.float32
F32R = mybir.dt.float32r

P = 128
B, L, C = 64, 64, 288
H = 16
D = C // H
DP = 32
FF = 4 * C
FT = FF // P
RK = 64
NV = RK * (RK - 1) // 2
PAIRS = B // 2
GP = 4
GROUPS = PAIRS // GP
HP = H // 2
VW = 2 * D + 1
GB = 2 * GP
TG = GP * P
CR = C - 2 * P
CD = 2 * P + 3 * CR
KR = 3 * CR + 2
EPS = 1e-6
SCALE = float(D) ** -0.5
SQUARINGS = 7
ELIM_ATT, ELIM_MLP = 5, 3
BANK = 512


def offset_of_row(i):
    return i * (RK - 1) - i * (i - 1) // 2


class Memory:

    def __init__(self, nc, ctx):
        self.nc, self.ctx = nc, ctx

    def sb(self, name, shape, dt=F32):
        return self.ctx.enter_context(self.nc.sbuf_tensor(name, shape, dt))

    def banks(self, prefix, n):
        return [self.ctx.enter_context(self.nc.psum_tensor(f"{prefix}{i}", [P, BANK], F32)) for i in range(n)]

    def sem(self, name):
        return self.ctx.enter_context(self.nc.semaphore(name))


def rotation_moves(sp, sbuf_all, io, moved, to_dram):
    for b in range(2):
        sbuf = sbuf_all[RK * b:RK * (b + 1), :, :]
        dram = io["skew"].rearrange("(q b) i j -> b i q j", b=2)[b]
        sp.dma_start(*((dram, sbuf) if to_dram else (sbuf, dram))).then_inc(moved, 16)


class WeightSplit:

    def __init__(self, m, st, io, stage, lows, bias2):
        self.st, self.stage, self.lows, self.bias2 = st, stage, lows, bias2
        self.weights = {"qkv": (io["L0_cond_W_qkv"], io["L0_cond_b_qkv"], 3 * C, 0),
                        "proj": (io["L0_cond_W_proj"], io["L0_cond_b_proj"], C, 3 * C),
                        "fc1": (io["L0_cond_W_fc1"], io["L0_cond_b_fc1"], FF, 0)}
        self.fc2 = (io["L0_cond_W_fc2"], io["L0_cond_b_fc2"])
        self.stage2 = m.sb("stage2", [P, FT, C])
        self.loaded = {name: m.sem(f"ld_{name}") for name in self.weights}
        self.zero_w, self.high_done, self.low_done, self.rest_step = m.sem("zero_w"), m.sem("w_high"), m.sem("w_low"), m.sem("rest_step")
        self.ld2, self.hi2, self.w2_low, self.lo2 = m.sem("fc2_ld"), m.sem("fc2_hi"), m.sem("w2_low"), m.sem("b2_low")

    def pieces(self, name):
        st = self.st
        if name == "qkv":
            def heads(t, a):
                return t[:, a:a + H * DP].rearrange("p (h d) -> p h d", d=DP)[:, :, 0:D]
            out = []
            for n in range(2):
                a = n * H * DP
                out.append((n * C, C, [heads(st.wqk_hi[:, k, :], a) for k in range(2)],
                            [heads(st.wqk_lo[:, k, :], a) for k in range(2)], heads(st.wqk_r[:, :], a), D))
            out.append((2 * C, C, [st.wv_hi[:, k, :] for k in range(2)], [st.wv_lo[:, k, :] for k in range(2)],
                        st.wv_r[:, :], None))
            return out
        hi, lo, r = (st.wp_hi, st.wp_lo, st.wp_r) if name == "proj" else (st.w1_hi, st.w1_lo, st.w1_r)
        n, a = self.weights[name][2:]
        return [(a, n, [hi[:, k, :] for k in range(2)], [lo[:, k, :] for k in range(2)], r[:, :], None)]

    def before(self, name):
        names = list(self.weights)
        return sum(len(self.pieces(x)) for x in names[:names.index(name)])

    def after(self, name):
        return 3 * (self.before(name) + len(self.pieces(name)))

    def load(self, q, name):
        src, bias, n, a = self.weights[name]
        for k in range(2):
            q.dma_start(self.stage[:, k, a:a + n], src[k * P:(k + 1) * P, :]).then_inc(self.loaded[name], 16)
        for k in range(3):
            q.dma_start(self.stage[k * CR:(k + 1) * CR, 2, a:a + n], src[2 * P:C, :]).then_inc(self.loaded[name], 16)
        q.dma_start(self.stage[3 * CR:KR, 2, a:a + n],
                    bias.rearrange("(a n) -> a n", a=1).to_broadcast([2, n])).then_inc(self.loaded[name], 16)

    def load_fc2(self, q):
        w, bias = self.fc2
        q.dma_start(self.stage2[:], w.rearrange("(t p) n -> p t n", p=P)).then_inc(self.ld2, 16)
        q.dma_start(self.bias2, bias.rearrange("(a n) -> a n", a=1).to_broadcast([2, C])).then_inc(self.ld2, 16)

    def zero(self, dve):
        for t in (self.st.wqk_hi, self.st.wqk_lo, self.st.wqk_r, self.st.b2):
            dve.memset(t[:].bitcast(F32), 0.0).then_inc(self.zero_w, 1)

    def source(self, piece, k):
        a, n, d = piece[0], piece[1], piece[5]
        src = self.stage[0:P if k < 2 else KR, k, a:a + n]
        return src.rearrange("p (h d) -> p h d", d=d) if d else src

    def high(self, act, name):
        act.wait_ge(self.zero_w, 4)
        act.wait_ge(self.loaded[name], 6 * 16)
        for piece in self.pieces(name):
            for k in range(3):
                act.copy((piece[2] + [piece[4]])[k], self.source(piece, k)).then_inc(self.high_done, 1)

    def low(self, dve, name):
        for i, piece in enumerate(self.pieces(name)):
            n_piece = self.before(name) + i
            _, n, hi, lo, rest, d = piece
            for k in range(2):
                dve.wait_ge(self.high_done, 3 * n_piece + k + 1)
                dve.tensor_tensor(lo[k], self.source(piece, k), hi[k].bitcast(F32), ALU.subtract
                                  ).then_inc(self.low_done, 1)
            low_v = self.lows[0:KR, 0:n]
            if d:
                low_v = low_v.rearrange("p (h d) -> p h d", d=d)
            dve.wait_ge(self.high_done, 3 * n_piece + 3)
            dve.wait_ge(self.low_done, 3 * n_piece + 2)
            dve.tensor_tensor(low_v, self.source(piece, 2), rest.bitcast(F32), ALU.subtract).then_inc(self.rest_step, 1)
            dve.wait_ge(self.rest_step, 2 * n_piece + 1)
            dve.tensor_scalar(low_v, low_v, self.st.lowrow[0:KR, 1:2], None, ALU.mult).then_inc(self.rest_step, 1)
            dve.wait_ge(self.rest_step, 2 * n_piece + 2)
            dve.scalar_tensor_tensor(out=rest, in0=rest.bitcast(F32), scalar=self.st.lowrow[0:KR, 0:1],
                                     in1=low_v, op0=ALU.mult, op1=ALU.add).then_inc(self.low_done, 1)

    def high_fc2(self, act):
        act.wait_ge(self.ld2, 32)
        act.copy(self.st.w2_hi[:], self.stage2[:]).then_inc(self.hi2, 1)
        act.copy(self.st.b2[0:2, :], self.bias2).then_inc(self.hi2, 1)

    def low_fc2(self, pool):
        pool.wait_ge(self.hi2, 1)
        pool.tensor_tensor(self.st.w2_lo[:], self.stage2[:], self.st.w2_hi[:].bitcast(F32), ALU.subtract
                           ).then_inc(self.w2_low, 1)

    def low_b2(self, dve):
        st, bias2 = self.st, self.bias2
        dve.wait_ge(self.hi2, 2)
        dve.memset(st.ones2[:].bitcast(F32), 1.0).then_inc(self.lo2, 1)
        dve.tensor_tensor(bias2, bias2, st.b2[0:2, :].bitcast(F32), ALU.subtract).then_inc(self.lo2, 1)
        dve.tensor_copy(st.sel2[:], st.lowrow[3 * CR:KR, :]).then_inc(self.lo2, 1)
        dve.wait_ge(self.lo2, 3)
        dve.tensor_scalar(bias2, bias2, st.sel2[:, 1:2], None, ALU.mult).then_inc(self.lo2, 1)
        dve.wait_ge(self.lo2, 4)
        dve.scalar_tensor_tensor(out=st.b2[0:2, :], in0=st.b2[0:2, :].bitcast(F32), scalar=st.sel2[:, 0:1], in1=bias2,
                                 op0=ALU.mult, op1=ALU.add).then_inc(self.lo2, 1)


def setup(nc, mem, st, io):
    with ExitStack() as ctx:
        m = Memory(nc, ctx)
        ps = m.banks("setup_ps", 8)
        cond = m.sb("cond", [B, C])
        p_c = m.sb("p_c", [96, 3, RK])
        silu = m.sb("silu", [B, C])
        silu_t = m.sb("silu_t", [P, 2, B])
        silu_r = m.sb("silu_r", [CR + 1, B])
        ada_room = m.sb("ada_room", [P, 3 * 6 * C])
        w_ada = ada_room[:].rearrange("p (t n) -> p t n", t=3)
        mod_room = m.sb("mod_room", [B, NV + 4 * CD])
        ada = mod_room[:, 0:6 * C].rearrange("b (s c) -> b s c", c=C)
        mod = mod_room[:, NV:].rearrange("b (n c) -> b n c", c=CD)
        vec = mod_room[:, 0:NV]
        NL1 = NV // 16
        l1_room = m.sb("l1_room", [NL1, 16 * C])
        w_l1 = l1_room[:].rearrange("p (r c) -> p r c", c=C)
        l1t_room = m.sb("l1t_room", [P, 3 * NV])
        w_l1t = l1t_room[:].rearrange("p (t n) -> p t n", t=3)
        upper = l1_room[0:B, 0:RK * RK].rearrange("b (i j) -> b i j", j=RK)
        skewed = l1t_room[0:B, 0:RK * RK].rearrange("b (i j) -> b i j", j=RK)
        split = WeightSplit(m, st, io, ada_room[:, 0:3 * FF].rearrange("p (k n) -> p k n", k=3),
                            ada_room[:, 3 * FF:4 * FF], ada_room[0:2, 4 * FF:4 * FF + C])

        ld_c, ld_ada, ld_l1, ld_p, ld_x = m.sem("ld_c"), m.sem("ld_ada"), m.sem("ld_l1"), m.sem("ld_p"), m.sem("ld_x")
        consts = m.sem("consts")
        silu_step, silu_t_done = m.sem("silu_step"), m.sem("silu_t_done")
        pe_done = m.sem("pe_done")
        ada_done, mod_done, mod_t_done = m.sem("ada_done"), m.sem("mod_done"), m.sem("mod_t_done")
        l1t_even, l1t_odd = m.sem("l1t_even"), m.sem("l1t_odd")
        vec_done, zeroed, spread, skewed_done = m.sem("vec_done"), m.sem("zeroed"), m.sem("spread"), m.sem("skewed_done")
        p_done, gates_out, skew_out = m.sem("p_done"), m.sem("gates_out"), m.sem("skew_out")

        def spread_rows(eng, copy, rows):
            eng.wait_ge(zeroed, 1)
            eng.wait_ge(vec_done, 4)
            for i in rows:
                a, n = offset_of_row(i), RK - 1 - i
                copy(upper[:, i, i + 1:RK], vec[:, a:a + n]).then_inc(spread, 1)

        block = ctx.enter_context(nc.Block())

        @block.sync
        def _(sp):
            sp.dma_start(cond[:], io["cond_1152"]).then_inc(ld_c, 16)
            sp.dma_start(w_ada[:, 0:2, :], io["L0_cond_W_ada"][0:2 * P, :].rearrange("(t p) n -> p t n", p=P)).then_inc(ld_ada, 16)
            sp.dma_start(w_ada[0:CR, 2, :], io["L0_cond_W_ada"][2 * P:C, :]).then_inc(ld_ada, 16)
            sp.dma_start(w_ada[CR:CR + 1, 2, :], io["L0_cond_b_ada"].rearrange("(a n) -> a n", a=1)).then_inc(ld_ada, 16)
            sp.dma_start(w_l1, io["L1_cond_W"].rearrange("(t p) c -> p t c", p=NL1)).then_inc(ld_l1, 16)
            sp.dma_start(w_l1t[CR:CR + 1, 2, :], io["L1_cond_b"].rearrange("(a n) -> a n", a=1)).then_inc(ld_l1, 16)
            sp.dma_start(p_c[:], io["L1_cond_P"].rearrange("(t p) n -> p t n", p=96)).then_inc(ld_p, 16)
            sp.dma_start(st.elim[RK:P, 0:RK], io["L1_cond_P"][0:RK, :]).then_inc(ld_p, 16)
            sp.wait_ge(pe_done, 2)
            split.load(sp, "qkv")
            split.load(sp, "proj")
            split.load_fc2(sp)
            sp.wait_ge(ada_done, 4)
            sp.dma_start(io["gates"], ada[:, 2:6:3, :]).then_inc(gates_out, 16)
            sp.wait_ge(split.low_done, split.after("proj"))
            split.load(sp, "fc1")
            sp.wait_ge(skewed_done, 1)
            sp.dma_start(io["skew"], skewed).then_inc(skew_out, 16)
            sp.wait_ge(skew_out, 16)
            sp.wait_ge(gates_out, 16)
            sp.wait_ge(ld_x, 16 * GROUPS)

        @block.gpsimd
        def _(pool):
            pool.memset(st.ident[:], 0.0).then_inc(consts, 1)
            pool.wait_ge(consts, 1)
            pool.memset(st.ident2[:], 0.0).then_inc(consts, 1)
            pool.wait_ge(consts, 2)
            pool.memset(st.below[:], -1.0).then_inc(consts, 1)
            pool.wait_ge(consts, 3)
            pool.memset(st.half1[:], 0.0).then_inc(consts, 1)
            pool.wait_ge(consts, 4)
            pool.memset(st.half2[:], 0.0).then_inc(consts, 1)
            pool.wait_ge(consts, 5)
            pool.memset(st.lowrow[:], 0.0).then_inc(consts, 1)
            pool.wait_ge(consts, 6)
            pool.affine_select(out=st.ident[:], in_=st.ident[:], compare_op=ALU.not_equal, fill=1.0, base=0,
                               pattern=[[-1, P]], channel_multiplier=1).then_inc(consts, 1)
            pool.wait_ge(consts, 7)
            pool.affine_select(out=st.ident2[:], in_=st.ident2[:], compare_op=ALU.not_equal, fill=1.0, base=0,
                               pattern=[[-1, RK]], channel_multiplier=1).then_inc(consts, 1)
            pool.wait_ge(consts, 8)
            pool.affine_select(out=st.ident2[:], in_=st.ident2[:], compare_op=ALU.not_equal, fill=1.0, base=-RK,
                               pattern=[[-1, RK]], channel_multiplier=1).then_inc(consts, 1)
            pool.wait_ge(consts, 9)
            pool.affine_select(out=st.below[0:RK, :], in_=st.below[0:RK, :], compare_op=ALU.is_gt, fill=0.0, base=0,
                               pattern=[[-1, RK]], channel_multiplier=1).then_inc(consts, 1)
            pool.wait_ge(consts, 10)
            pool.affine_select(out=st.below[RK:P, :], in_=st.below[RK:P, :], compare_op=ALU.is_gt, fill=0.0, base=0,
                               pattern=[[-1, RK]], channel_multiplier=1).then_inc(consts, 1)
            pool.wait_ge(consts, 11)
            pool.memset(st.half1[RK:P, :], 1.0).then_inc(consts, 1)
            pool.wait_ge(consts, 12)
            pool.memset(st.half2[RK:P, :], 2.0).then_inc(consts, 1)
            pool.wait_ge(consts, 13)
            pool.memset(st.lowrow[CR:2 * CR, 1:2], 1.0).then_inc(consts, 1)
            pool.wait_ge(consts, 14)
            pool.affine_select(out=st.lowrow[3 * CR:P, 1:2], in_=st.lowrow[3 * CR:P, 1:2], compare_op=ALU.not_equal,
                               fill=1.0, base=-1, pattern=[[0, 1]], channel_multiplier=1).then_inc(consts, 1)
            pool.wait_ge(consts, 15)
            pool.tensor_scalar(st.lowrow[:, 0:1], st.lowrow[:, 1:2], -1.0, 1.0, ALU.mult, ALU.add).then_inc(consts, 1)
            pool.wait_ge(consts, 16)
            pool.memset(st.ones[:], 1.0).then_inc(consts, 1)
            pool.wait_ge(consts, 17)
            pool.memset(st.ones_top[:], 0.0).then_inc(consts, 1)
            pool.wait_ge(consts, 18)
            pool.memset(st.ones_top[0:RK, :], 1.0).then_inc(consts, 1)
            pool.wait_ge(consts, 19)
            pool.memset(st.ones_low[:], 0.0).then_inc(consts, 1)
            pool.wait_ge(consts, 20)
            pool.memset(st.ones_low[RK:P, :], 1.0).then_inc(consts, 1)
            pool.wait_ge(consts, 21)
            pool.memset(st.minus_half[:], -0.5).then_inc(consts, 1)
            pool.wait_ge(consts, 22)
            pool.memset(st.powers[:, 0:1], 0.5).then_inc(consts, 1)
            pool.wait_ge(consts, 23)
            pool.memset(st.powers[:, 1:2], -1.0).then_inc(consts, 1)
            pool.wait_ge(consts, 24)
            pool.memset(silu_r[CR:CR + 1, :], 1.0).then_inc(consts, 1)
            pool.wait_ge(consts, 25)
            pool.memset(st.elim[:, RK:P], 0.0).then_inc(consts, 1)
            pool.wait_ge(consts, 26)
            pool.affine_select(out=st.elim[0:RK, RK:P], in_=st.elim[0:RK, RK:P], compare_op=ALU.not_equal, fill=1.0,
                               base=0, pattern=[[-1, RK]], channel_multiplier=1).then_inc(consts, 1)
            pool.wait_ge(pe_done, 14)
            pool.memset(upper, 0.0).then_inc(zeroed, 1)
            split.low_fc2(pool)
            pool.drain()
            spread_rows(pool, pool.tensor_copy, range(0, RK - 1, 4))

        @block.scalar
        def _(act):
            act.wait_ge(ld_c, 16)
            act.activation(silu[:], cond[:], ACT.Exp, scale=-1.0).then_inc(silu_step, 1)
            for n in range(12):
                if n % 2 == 0:
                    act.wait_ge(pe_done, 2 + 1 + n)
                    rows = P if n // 4 < 2 else CR
                    act.copy(w_l1t[0:rows, n // 4, (n % 4) * 4 * NL1:(n % 4 + 1) * 4 * NL1],
                             ps[n % 8][0:rows, 0:4 * NL1]).then_inc(l1t_even, 1)
            split.high(act, "qkv")
            split.high(act, "proj")
            for g in range(GROUPS):
                act.dma_start(st.x[:, g * GP:(g + 1) * GP, :],
                              io["x"].rearrange("(q b) l c -> (b l) q c", b=2)[:, g * GP:(g + 1) * GP, :]
                              ).then_inc(ld_x, 16)
            split.high_fc2(act)
            spread_rows(act, act.copy, range(1, RK - 1, 2))
            split.high(act, "fc1")

        @block.vector
        def _(dve):
            split.zero(dve)
            dve.wait_ge(silu_step, 1)
            dve.tensor_scalar(silu[:], silu[:], 1.0, None, ALU.add).then_inc(silu_step, 1)
            dve.wait_ge(silu_step, 2)
            dve.reciprocal(silu[:], silu[:]).then_inc(silu_step, 1)
            dve.wait_ge(silu_step, 3)
            dve.tensor_tensor(silu[:], silu[:], cond[:], ALU.mult).then_inc(silu_step, 1)
            dve.wait_ge(pe_done, 1)
            dve.tensor_copy(silu_t[:], ps[0][:, 0:2 * B].rearrange("p (t b) -> p t b", b=B)).then_inc(silu_t_done, 1)
            dve.tensor_copy(silu_r[0:CR, :], ps[0][0:CR, 2 * B:3 * B]).then_inc(silu_t_done, 1)
            dve.wait_ge(pe_done, 2)
            ada_f = mod_room[:, 0:6 * C]
            for n in range(4):
                w = min(BANK, 6 * C - n * BANK)
                dve.tensor_copy(ada_f[:, n * BANK:n * BANK + w], ps[4 + n][0:B, 0:w]).then_inc(ada_done, 1)
            dve.wait_ge(ada_done, 4)
            for n, (s, plus) in enumerate(((0, 0.0), (1, 1.0), (3, 0.0), (4, 1.0))):
                dve.tensor_scalar(mod[:, n, 0:C], ada[:, s, :], plus, None, ALU.add).then_inc(mod_done, 1)
                dve.tensor_scalar(mod[:, n, C:CD].rearrange("b (r c) -> b r c", c=CR),
                                  ada[:, s, 2 * P:C].unsqueeze(1).to_broadcast([B, 2, CR]), plus, None,
                                  ALU.add).then_inc(mod_done, 1)
            for n in range(1, 12, 2):
                dve.wait_ge(pe_done, 2 + 1 + n)
                rows = P if n // 4 < 2 else CR
                dve.tensor_copy(w_l1t[0:rows, n // 4, (n % 4) * 4 * NL1:(n % 4 + 1) * 4 * NL1],
                                ps[n % 8][0:rows, 0:4 * NL1]).then_inc(l1t_odd, 1)
            dve.wait_ge(consts, 16)
            split.low(dve, "qkv")
            split.low(dve, "proj")
            dve.wait_ge(pe_done, 15)
            dve.wait_ge(gates_out, 16)
            for n in range(4):
                dve.tensor_scalar(vec[:, n * 4 * NL1:(n + 1) * 4 * NL1], ps[n][0:B, 0:4 * NL1],
                                  2.0 ** -SQUARINGS, None, ALU.mult).then_inc(vec_done, 1)
            spread_rows(dve, dve.tensor_copy, range(2, RK - 1, 4))
            dve.wait_ge(pe_done, 16)
            for n in range(4):
                dve.tensor_copy(st.mod_t[:, n, 0:2, :], ps[4][:, n * 2 * B:(n + 1) * 2 * B].rearrange("p (t b) -> p t b", b=B)
                                ).then_inc(mod_t_done, 1)
            dve.tensor_copy(st.mod_t[0:3 * CR, :, 2, :], ps[5][0:3 * CR, 0:4 * B].rearrange("p (n b) -> p n b", b=B)
                            ).then_inc(mod_t_done, 1)
            split.low_b2(dve)
            dve.wait_ge(pe_done, 17)
            dve.tensor_copy(st.elim[0:RK, 0:RK], ps[6][0:RK, 0:RK]).then_inc(p_done, 1)
            dve.tensor_copy(st.p_t[:], ps[7][0:RK, 0:C]).then_inc(p_done, 1)
            dve.wait_ge(spread, RK - 1)
            dve.tensor_tensor(skewed, upper, upper.rearrange("b i j -> b j i"), ALU.subtract).then_inc(skewed_done, 1)
            split.low(dve, "fc1")

        @block.tensor
        def _(pe):
            pe.wait_ge(silu_step, 4)
            pe.wait_ge(consts, 27)
            for t in range(3):
                rows = P if t < 2 else CR
                mm = pe.transpose(ps[0][0:rows, t * B:(t + 1) * B], silu[:, t * P:t * P + rows], st.ident[0:B, 0:B])
            mm.then_inc(pe_done, 1)
            pe.wait_ge(silu_t_done, 2)
            pe.wait_ge(ld_ada, 48)
            lhs = [silu_t[:, 0, :], silu_t[:, 1, :], silu_r[:, :]]
            for n in range(4):
                w = min(BANK, 6 * C - n * BANK)
                for t in range(3):
                    rows = P if t < 2 else CR + 1
                    mm = pe.matmul(ps[4 + n][0:B, 0:w], lhs[t], w_ada[0:rows, t, n * BANK:n * BANK + w],
                                   start=(t == 0), stop=(t == 2))
            mm.then_inc(pe_done, 1)
            pe.wait_ge(ld_l1, 32)
            pe.wait_ge(ada_done, 4)
            for n in range(12):
                t = n // 4
                rows = P if t < 2 else CR
                if n >= 8:
                    if n % 2 == 0:
                        pe.wait_ge(l1t_even, (n - 8) // 2 + 1)
                    else:
                        pe.wait_ge(l1t_odd, (n - 8) // 2 + 1)
                for q in range(4):
                    r = (n % 4) * 4 + q
                    mm = pe.transpose(ps[n % 8][0:rows, q * NL1:(q + 1) * NL1], w_l1[:, r, t * P:t * P + rows],
                                      st.ident[0:NL1, 0:NL1])
                mm.then_inc(pe_done, 1)
            pe.wait_ge(l1t_even, 6)
            pe.wait_ge(l1t_odd, 6)
            for n in range(4):
                for t in range(3):
                    rows = P if t < 2 else CR + 1
                    mm = pe.matmul(ps[n][0:B, 0:4 * NL1], lhs[t], w_l1t[0:rows, t, n * 4 * NL1:(n + 1) * 4 * NL1],
                                   start=(t == 0), stop=(t == 2))
            mm.then_inc(pe_done, 1)
            pe.wait_ge(mod_done, 8)
            for n in range(4):
                for t in range(2):
                    mm = pe.transpose(ps[4][:, (2 * n + t) * B:(2 * n + t + 1) * B], mod[:, n, t * P:(t + 1) * P],
                                      st.ident[0:B, 0:B])
                mm = pe.transpose(ps[5][0:3 * CR, n * B:(n + 1) * B], mod[:, n, 2 * P:CD], st.ident[0:B, 0:B])
            mm.then_inc(pe_done, 1)
            pe.wait_ge(ld_p, 32)
            for t in range(3):
                pe.matmul(ps[6][0:RK, 0:RK], p_c[:, t, :], p_c[:, t, :], start=(t == 0), stop=(t == 2))
            for t in range(3):
                mm = pe.transpose(ps[7][0:RK, t * 96:(t + 1) * 96], p_c[:, t, :], st.ident[0:96, 0:96])
            mm.then_inc(pe_done, 1)


def rotations(nc, st, io):
    with ExitStack() as ctx:
        m = Memory(nc, ctx)
        a34_room = m.sb("a34_room", [P, PAIRS * 2 * RK])
        a34 = a34_room[:].rearrange("p (q w j) -> p q w j", w=2, j=RK)
        result = a34_room[:, 0:PAIRS * RK].rearrange("p (q j) -> p q j", j=RK)
        ps = m.banks("exp_ps", GROUPS)
        sc = m.sb("sc", [P, PAIRS, 2, RK])
        diag = m.sb("diag", [P, PAIRS, P])
        twos = m.sb("twos", [P, 1])

        prod, c_new, s_new, held_even = m.sem("prod"), m.sem("c_new"), m.sem("s_new"), m.sem("held_even")
        held_odd, zeroed = m.sem("held_odd"), m.sem("diag_zeroed")
        moved, halved, summed = m.sem("a34_moved"), m.sem("a2_halved"), m.sem("terms_summed")
        skew_in = m.sem("skew_in")
        rotation_done, prepared = m.sem("rotation_done"), m.sem("att_prepared")

        block = ctx.enter_context(nc.Block())

        def pairs(g):
            return slice(g * GP, (g + 1) * GP)

        def product(g, n):
            return ps[g][:, 0:GP * n * RK].rearrange("p (q j) -> p q j", q=GP)

        def hold(eng, src, g, scale):
            b = 0 if eng is nc.scalar else 1
            r = slice(RK * b, RK * (b + 1))
            out = diag[r, pairs(g), RK * b:RK * (b + 1)]
            if b == 0:
                eng.mul(out, src[r], scale).then_inc(held_even, 1)
            else:
                factor = twos if scale == 2.0 else st.ones
                eng.tensor_tensor(out, src[r], factor[r, 0:1].unsqueeze(1).to_broadcast([RK, GP, RK]), ALU.mult
                                  ).then_inc(held_odd, 1)

        def wait_held(eng, n):
            eng.wait_ge(held_even, n)
            eng.wait_ge(held_odd, n)

        def holds(eng):
            for g in range(GROUPS):
                if g == 0:
                    eng.wait_ge(zeroed, 2)
                    eng.wait_ge(skew_in, 32)
                hold(eng, sc[:, pairs(g), 0, :], g, 1.0)
            for g in range(GROUPS):
                if eng is nc.scalar:
                    eng.wait_ge(prod, g + 1)
                    eng.mul(sc[:, pairs(g), 1, :], product(g, 1), -1.0).then_inc(c_new, 1)
                eng.wait_ge(c_new, g + 1)
                hold(eng, sc[:, pairs(g), 1, :], g, 1.0)
            if eng is nc.scalar:
                for g in range(GROUPS):
                    eng.wait_ge(prod, GROUPS + g + 1)
                    eng.copy(a34[:, pairs(g)], product(g, 2).rearrange("p q (w j) -> p q w j", w=2)).then_inc(moved, 1)
                    eng.mul(sc[:, pairs(g), 1, :], sc[:, pairs(g), 1, :], 0.5).then_inc(halved, 1)
            for g in range(GROUPS):
                eng.wait_ge(s_new, g + 1)
                hold(eng, sc[:, pairs(g), 0, :], g, 2.0)

        @block.sync
        def _(sp):
            rotation_moves(sp, sc[:, :, 0, :], io, skew_in, to_dram=False)
            sp.wait_ge(rotation_done, GROUPS)
            rotation_moves(sp, result, io, st.rotation_kept, to_dram=True)

        @block.gpsimd
        def _(pool):
            pool.memset(diag[:], 0.0).then_inc(zeroed, 1)
            pool.memset(twos[:], 2.0).then_inc(zeroed, 1)
            st.norm.root(pool, (0, ATTENTION))
            pool.drain()
            holds(pool)
            with pool.Fori(0, SQUARINGS) as step:
                for g in range(GROUPS):
                    pool.wait_ge(s_new, GROUPS * (step + 1) + g + 1)
                    hold(pool, sc[:, pairs(g), 0, :], g, 2.0)

        @block.scalar
        def _(act):
            holds(act)
            with act.Fori(0, SQUARINGS) as step:
                for g in range(GROUPS):
                    act.wait_ge(s_new, GROUPS * (step + 1) + g + 1)
                    act.mul(sc[:, pairs(g), 1, :], product(g, 2).rearrange("p q (w j) -> p q w j", w=2)[:, :, 0, :],
                            -1.0).then_inc(c_new, 1)
                    hold(act, sc[:, pairs(g), 0, :], g, 2.0)

        @block.vector
        def _(dve):
            st.norm.statistics(dve, (0, ATTENTION))
            dve.memset(st.q_diag[:], 0.0).then_inc(prepared, 1)
            st.norm.normalize(dve, (0, ATTENTION))
            s_of, c_of = lambda g: sc[:, pairs(g), 0, :], lambda g: sc[:, pairs(g), 1, :]

            def add_a34(g):
                dve.wait_ge(moved, g + 1)
                dve.scalar_tensor_tensor(out=s_of(g), in0=a34[:, pairs(g), 0, :], scalar=1 / 6, in1=s_of(g),
                                         op0=ALU.mult, op1=ALU.add).then_inc(summed, 1)
                dve.wait_ge(halved, g + 1)
                dve.scalar_tensor_tensor(out=c_of(g), in0=a34[:, pairs(g), 1, :], scalar=1 / 24, in1=c_of(g),
                                         op0=ALU.mult, op1=ALU.add).then_inc(summed, 1)

            def add_a56(g):
                a56 = product(g, 2).rearrange("p q (w j) -> p q w j", w=2)
                dve.wait_ge(prod, 2 * GROUPS + g + 1)
                dve.wait_ge(summed, 2 * g + 2)
                dve.scalar_tensor_tensor(out=s_of(g), in0=a56[:, :, 0, :], scalar=1 / 120, in1=s_of(g),
                                         op0=ALU.mult, op1=ALU.add).then_inc(s_new, 1)
                dve.scalar_tensor_tensor(out=c_of(g), in0=a56[:, :, 1, :], scalar=1 / 720, in1=c_of(g),
                                         op0=ALU.mult, op1=ALU.add).then_inc(c_new, 1)

            add_a34(0)
            for g in range(GROUPS):
                if g + 1 < GROUPS:
                    add_a34(g + 1)
                add_a56(g)
            def double_s(step, g):
                dve.wait_ge(prod, GROUPS * (step + 3) + g + 1)
                dve.scalar_tensor_tensor(out=s_of(g), in0=s_of(g), scalar=2.0,
                                         in1=product(g, 2).rearrange("p q (w j) -> p q w j", w=2)[:, :, 1, :],
                                         op0=ALU.mult, op1=ALU.subtract).then_inc(s_new, 1)

            with dve.Fori(0, SQUARINGS - 1) as step:
                for g in range(GROUPS):
                    double_s(step, g)
            last = SQUARINGS - 1
            for g in range(GROUPS + 1):
                if g < GROUPS:
                    double_s(last, g)
                if g > 0:
                    dve.wait_ge(s_new, GROUPS * (last + 1) + g)
                    dve.wait_ge(c_new, GROUPS * (last + 2) + g)
                    dve.tensor_tensor(result[:, pairs(g - 1), :], s_of(g - 1), c_of(g - 1), ALU.add
                                      ).then_inc(rotation_done, 1)

        @block.tensor
        def _(pe):
            for g in range(GROUPS):
                wait_held(pe, g + 1)
                for q in range(GP):
                    i = g * GP + q
                    mm = pe.matmul(product(g, 1)[:, q, :], diag[:, i, :], sc[:, i, 0, :], start=True, stop=True)
                mm.then_inc(prod, 1)
            for g in range(GROUPS):
                wait_held(pe, GROUPS + g + 1)
                for q in range(GP):
                    i = g * GP + q
                    mm = pe.matmul(product(g, 2)[:, q, :], diag[:, i, :], sc[:, i, :, :], start=True, stop=True)
                mm.then_inc(prod, 1)
            for g in range(GROUPS):
                pe.wait_ge(moved, g + 1)
                for q in range(GP):
                    i = g * GP + q
                    mm = pe.matmul(product(g, 2)[:, q, :], diag[:, i, :], a34[:, i, :, :], start=True, stop=True)
                mm.then_inc(prod, 1)
            with pe.Fori(0, SQUARINGS) as step:
                for g in range(GROUPS):
                    wait_held(pe, GROUPS * (step + 2) + g + 1)
                    pe.wait_ge(c_new, GROUPS * (step + 1) + g + 1)
                    for q in range(GP):
                        i = g * GP + q
                        mm = pe.matmul(product(g, 2)[:, q, :], diag[:, i, :], sc[:, i, :, :], start=True, stop=True)
                    mm.then_inc(prod, 1)


class Elimination:

    W = P + RK

    def __init__(self, m, st):
        self.st = st
        self.picked = m.sb("picked", [P, P])
        self.rows = m.sb("pivot_rows", [P, self.W])
        self.root = m.sb("root", [P, 1])
        self.sign2 = m.sb("sign2", [P, 1])
        self.weight = m.sb("weight", [P, 1])
        self.part = m.sb("part", [P, RK])
        self.inv = m.sb("inv", [P, 1])
        self.factor = m.sb("factor", [P, 1])
        self.update = m.sb("update", [P, P])
        self.gram_k = m.sb("gram_k", [P, 1])
        self.square_k = m.sb("square_k", [P, 1])
        self.part_k = m.sb("part_k", [P, 1])
        self.pivot = m.sb("pivot", [P, 1])
        self.below_k = m.sb("below_k", [P, 1])
        self.chosen = m.sem("pivot_chosen")
        self.spread = m.sem("pivot_spread")
        self.copied = m.sem("pivot_copied")

    def use(self, bank):
        self.bank = bank

    def pe(self, pe, k):
        pe.wait_ge(self.chosen, k + 1)
        pe.matmul(self.bank[:, 0:P], self.st.ones_top[:], self.picked[:], start=True, stop=True)
        pe.matmul(self.bank[:, P:self.W], self.st.ones_low[:], self.picked[:, 0:RK],
                  start=True, stop=True).then_inc(self.spread, 1)

    def act(self, act, k):
        act.wait_ge(self.spread, k + 1)
        act.copy(self.gram_k[:], self.bank[:, bass.ds(k, 1)])
        act.copy(self.square_k[:], self.bank[:, bass.ds(k + P, 1)]).then_inc(self.copied, 1)
        act.copy(self.rows[:], self.bank[:, 0:self.W]).then_inc(self.copied, 1)

    def pool(self, pool, k):
        st, el = self.st, self.st.elim
        pool.tensor_tensor(self.picked[:], el[:], st.ident2[:, bass.ds(k, 1)].to_broadcast([P, P]), ALU.mult
                           ).then_inc(self.chosen, 1)
        pool.wait_ge(self.copied, 2 * k + 1)
        pool.tensor_tensor(self.root[:], self.gram_k[:], st.powers[:, 0:1], ALU.pow)
        pool.tensor_scalar(self.sign2[:], self.square_k[:], 0.0, st.half2[:], ALU.is_ge, ALU.mult)
        pool.tensor_tensor(self.below_k[:], el[:, bass.ds(k, 1)], st.below[:, bass.ds(k, 1)], ALU.mult)
        pool.drain()
        pool.tensor_scalar(self.weight[:], self.sign2[:], st.half1[:], self.root[:], ALU.subtract, ALU.mult)
        pool.drain()
        pool.wait_ge(self.copied, 2 * k + 2)
        pool.tensor_tensor(self.part[:], self.rows[:, P:self.W], self.weight[:].to_broadcast([P, RK]), ALU.mult)
        pool.tensor_tensor(self.part_k[:], self.square_k[:], self.weight[:], ALU.mult)
        pool.drain()
        pool.tensor_tensor(self.rows[:, 0:RK], self.rows[:, 0:RK], self.part[:], ALU.add)
        pool.tensor_tensor(self.pivot[:], self.gram_k[:], self.part_k[:], ALU.add)
        pool.drain()
        pool.tensor_tensor(self.inv[:], self.pivot[:], st.powers[:, 1:2], ALU.pow)
        pool.drain()
        pool.tensor_tensor(self.factor[:], self.below_k[:], self.inv[:], ALU.mult)
        pool.drain()
        pool.tensor_tensor(self.update[:], self.rows[:, 0:P], self.factor[:].to_broadcast([P, P]), ALU.mult)
        pool.drain()
        pool.tensor_tensor(el[:], el[:], self.update[:], ALU.add)
        pool.drain()




def is_last(g):
    return isinstance(g, int) and g == GROUPS - 1


class Jobs:

    def __init__(self, mem, name, banks, jobs, ahead=(), done_before=(), for_after=()):
        self.banks = banks
        n = len(banks)
        self.steady = {job: (i % n, i // n) for i, job in enumerate(jobs)}
        left = [job for job in jobs if job not in ahead or job in for_after]
        ahead = [job for job in ahead if job not in done_before]
        self.final = {job: (i % n, i // n) for i, job in enumerate(left)}
        self.first = {job: (i % n, i // n) for i, job in enumerate(ahead)}
        self.before = [len(range(b, len(ahead), n)) for b in range(n)]
        self.uses = [len(range(b, len(jobs), n)) for b in range(n)]
        self.full = [mem.sem(f"{name}_full{i}") for i in range(n)]
        self.free = [mem.sem(f"{name}_free{i}") for i in range(n)]

    def open(self, eng):
        for free in self.free:
            eng.sem_inc(free, 1)

    def at(self, g, job):
        if isinstance(g, int) and g < 0:
            return self.first[job]
        b, k = (self.final if is_last(g) else self.steady)[job]
        return b, g * self.uses[b] + k + self.before[b]

    def bank(self, g, job):
        return self.banks[self.at(g, job)[0]]

    def full_of(self, g, job):
        return self.full[self.at(g, job)[0]]

    def free_of(self, g, job):
        return self.free[self.at(g, job)[0]]

    def wait_free(self, eng, g, job):
        b, n = self.at(g, job)
        eng.wait_ge(self.free[b], n + 1)

    def wait_full(self, eng, g, job):
        b, n = self.at(g, job)
        eng.wait_ge(self.full[b], n + 1)

    def wait_taken(self, eng, g, job):
        b, n = self.at(g, job)
        eng.wait_ge(self.free[b], n + 2)


def for_groups(eng, body, first=0):
    for g in range(first):
        body(g)
    with eng.Fori(first, GROUPS - 1) as g:
        body(g)
    body(GROUPS - 1)


class Split:

    def __init__(self, m, name, tokens):
        self.both = m.sb(f"{name}_parts", [P, 2, 2, tokens], F32R)
        self.hi, self.lo = self.both[:, 0], self.both[:, 1]
        self.rest = m.sb(f"{name}_rest", [KR, tokens], F32R)

    def ones(self, eng, sem):
        eng.memset(self.rest[3 * CR:KR, :].bitcast(F32), 1.0).then_inc(sem, 1)


def product(pe, out, acts, tokens, weights, cols, weights_held):
    w_hi, w_lo, w_r = weights
    terms = [(acts.hi[:, k, tokens], w_hi[:, k, cols]) for k in range(2)]
    terms += [(acts.hi[:, k, tokens], w_lo[:, k, cols]) for k in range(2)]
    terms += [(acts.lo[:, k, tokens], w_hi[:, k, cols]) for k in range(2)]
    terms += [(acts.rest[:, tokens], w_r[:, cols])]
    for i, (a, w) in enumerate(terms):
        held, streamed = (w, a) if weights_held else (a, w)
        mm = pe.matmul(out, held, streamed, start=(i == 0), stop=(i == len(terms) - 1))
    return mm


ATTENTION, MLP = 0, 1


class Norm:

    def __init__(self, m, st):
        self.st = st
        self.acts = Split(m, "h", TG)
        self.h = m.sb("ln_h", [P, 3, TG])
        self.stats = m.sb("ln_stats", [P, GP, 6])
        self.mv = m.sb("ln_mean_var", [P, GP, 2])
        self.var = m.sb("ln_var_eps", [P, GP])
        self.rstd = m.sb("ln_rstd", [P, GP])
        self.xn = m.sb("ln_xn", [P, GP, CD])
        self.aggr, self.var_ready, self.rstd_ready = m.sem("ln_aggr_done"), m.sem("ln_var_ready"), m.sem("ln_rstd_ready")
        self.xn_ready, self.shifted = m.sem("ln_xn_ready"), m.sem("ln_shifted")
        self.hi_ready, self.lo_ready = m.sem("ln_hi_ready"), m.sem("ln_lo_ready")

    def use(self, jobs):
        self.jobs = jobs

    def count(self, of):
        return of[0] + GROUPS * of[1]

    def statistics(self, dve, of):
        x, g, n = self.st.x, of[0], self.count(of)
        for p in range(GP):
            dve.bn_stats(self.stats[:, p, :], x[:, bass.ds(g * GP + p, 1), :].rearrange("p q c -> p (q c)"))
        dve.drain()
        for p in range(GP):
            dve.bn_aggr(self.mv[:, p, :], self.stats[:, p, :]).then_inc(self.aggr, 1)
        dve.wait_ge(self.aggr, n * GP + GP)
        dve.tensor_scalar(self.var[:], self.mv[:, :, 1], EPS, None, ALU.add).then_inc(self.var_ready, 1)

    def root(self, pool, of):
        pool.wait_ge(self.var_ready, self.count(of) + 1)
        pool.tensor_tensor(self.rstd[:], self.var[:], self.st.minus_half[:], ALU.pow).then_inc(self.rstd_ready, 1)

    def normalize(self, dve, of):
        x, g = self.st.x, of[0]
        dve.wait_ge(self.rstd_ready, self.count(of) + 1)
        for p in range(GP):
            mean, rstd = self.mv[:, p, 0:1], self.rstd[:, p:p + 1]
            xg = x[:, bass.ds(g * GP + p, 1), :].rearrange("p q c -> p (q c)")
            dve.tensor_scalar(self.xn[:, p, 0:C], xg, mean, rstd, ALU.subtract, ALU.mult).then_inc(self.xn_ready, 1)
            dve.tensor_scalar(self.xn[:, p, C:CD].rearrange("p (r c) -> p r c", r=2),
                              x[:, bass.ds(g * GP + p, 1), 2 * P:C].to_broadcast([P, 2, CR]), mean, rstd,
                              ALU.subtract, ALU.mult).then_inc(self.xn_ready, 1)

    def transposes(self, pe, of, at):
        pe.wait_ge(self.xn_ready, (self.count(of) + 1) * 2 * GP)
        for t in range(3):
            rows = P if t < 2 else 3 * CR
            job = ("ln", t)
            self.jobs.wait_free(pe, at, job)
            for p in range(GP):
                mm = pe.transpose(self.jobs.bank(at, job)[0:rows, p * P:(p + 1) * P],
                                  self.xn[:, p, t * P:t * P + rows], self.st.ident[:])
            mm.then_inc(self.jobs.full_of(at, job), 1)

    def rows(self, t):
        return P if t < 2 else 3 * CR

    def by(self, n, of, t):
        return self.st.mod_t[0:self.rows(t), 2 * of[1] + n, t, bass.ds(of[0] * GB, GB)].unsqueeze(2).to_broadcast([self.rows(t), GB, L])

    def scale_up(self, dve, of, at):
        for t in range(3):
            job = ("ln", t)
            self.jobs.wait_full(dve, at, job)
            dve.tensor_tensor(self.h[0:self.rows(t), t, :].rearrange("p (b l) -> p b l", l=L),
                              self.jobs.bank(at, job)[0:self.rows(t), :].rearrange("p (b l) -> p b l", l=L),
                              self.by(1, of, t), ALU.mult).then_inc(self.jobs.free_of(at, job), 1)

    def shift_by(self, dve, of, at):
        for t in range(3):
            h = self.h[0:self.rows(t), t, :].rearrange("p (b l) -> p b l", l=L)
            self.jobs.wait_taken(dve, at, ("ln", t))
            dve.tensor_tensor(h, h, self.by(0, of, t), ALU.add).then_inc(self.shifted, 1)

    def high(self, act, of):
        for t in range(3):
            act.wait_ge(self.shifted, self.count(of) * 3 + t + 1)
            out = self.acts.hi[:, t, :] if t < 2 else self.acts.rest[0:3 * CR, :]
            act.copy(out, self.h[0:P if t < 2 else 3 * CR, t, :]).then_inc(self.hi_ready, 1)

    def low(self, dve, of):
        for t in range(3):
            dve.wait_ge(self.hi_ready, self.count(of) * 3 + t + 1)
            if t < 2:
                out, hi, h = self.acts.lo[:, t, :], self.acts.hi[:, t, :], self.h[:, t, :]
            else:
                r = slice(2 * CR, 3 * CR)
                out, hi, h = self.acts.rest[r, :], self.acts.rest[r, :], self.h[r, t, :]
            dve.tensor_tensor(out, h, hi.bitcast(F32), ALU.subtract).then_inc(self.lo_ready, 1)

    def wait_acts(self, eng, of):
        eng.wait_ge(self.lo_ready, 3 * (self.count(of) + 1))


def gate_loads(sp, nc, io, which, gate, loaded, used):
    src = io["gates"].rearrange("(q b) s c -> b s q c", b=2)
    with sp.Fori(0, GROUPS) as g:
        sp.wait_ge(used, g * GP + 1)
        for b in range(2):
            sp.dma_start(gate[L * b:L * (b + 1), :, :],
                         src[b, which, bass.ds(g * GP, GP), :].unsqueeze(0).to_broadcast([L, GP, C])
                         ).then_inc(loaded, 16)


def attention(nc, st, io, elim):
    with ExitStack() as ctx:
        m = Memory(nc, ctx)
        o_t = Split(m, "o_t", TG)
        banks = m.banks("att_ps", 5)
        scores = ctx.enter_context(nc.psum_tensor("scores", [P, 2, BANK], F32))
        elim.use(m.banks("elim_ps", 1)[0])
        T = H // 4

        q, k = (lambda t: [("q", t)]), (lambda t: [("k", t)])
        pt, ov = (lambda t: [("pt", t, 0), ("pt", t, 1)]), (lambda t: [("o", t, 0), ("o", t, 1)])
        ln, v = [("ln", t) for t in range(3)], [("v", p) for p in range(GP)]
        names = q(2) + pt(0) + k(2) + ov(0) + ln + q(3) + pt(1) + k(3) + ov(1)
        names += pt(2) + q(0) + ov(2) + k(0) + pt(3) + ov(3) + v
        names += [("ot", t) for t in range(3)] + q(1) + k(1) + [("proj", p) for p in range(GP)]
        jobs = Jobs(m, "att", banks, names, ln + q(0) + k(0) + v + q(1) + k(1), for_after=ln)

        q_diag, norm, acts = st.q_diag, st.norm, st.norm.acts
        va = m.sb("va", [P, GP, HP, 2, VW])
        norm.use(jobs)
        k_t = m.sb("k_t", [P, 2, TG])
        prob = m.sb("prob", [P, 2, 2, TG])
        row_max = m.sb("row_max", [P, 2, 2, GB])
        prob_t = m.sb("prob_t", [P, 2, TG])
        rsum = m.sb("rsum", [P, 2, GP, 2])
        o = m.sb("o", [P, GP, CD])
        gated = m.sb("gated", [P, 2, C])
        gate = m.sb("gate", [P, GP, C])

        begun, v_begun, gate_in = m.sem("att_begun"), m.sem("v_begun"), m.sem("gate_in")
        scored, max_done, less_max = m.sem("scored"), m.sem("max_done"), m.sem("less_max")
        exp_done, inverted, o_ready = m.sem("exp_done"), m.sem("inverted"), m.sem("o_ready")
        o_hi, o_lo, added = m.sem("o_hi"), m.sem("o_lo"), m.sem("added")

        def turn(g, t):
            return g * T + t

        def before(g, t):
            return g - 1 if t < 2 else g

        def rows_of(t):
            return P if t < 2 else 3 * CR

        def following(g):
            return (0, MLP) if is_last(g) else (g + 1, ATTENTION)

        def step_of(g, i):
            return g * ELIM_ATT + (i - 1 if is_last(g) and i > 2 else i)

        block = ctx.enter_context(nc.Block())

        @block.sync
        def _(sp):
            gate_loads(sp, nc, io, 0, gate, gate_in, added)

        @block.gpsimd
        def _(pool):
            acts.ones(pool, begun)
            o_t.ones(pool, begun)
            pool.drain()
            pool.memset(va[:], 0.0)
            pool.drain()
            for b in range(2):
                pool.memset(va[L * b:L * (b + 1), :, :, b, 2 * D].rearrange("p g q -> p (g q)"), 1.0).then_inc(v_begun, 1)
                pool.drain()

            def body(g):
                norm.root(pool, following(g))
                for i in range(ELIM_ATT):
                    if not (is_last(g) and i == 2):
                        elim.pool(pool, step_of(g, i))
            for_groups(pool, body)

        @block.scalar
        def _(act):
            def take_q(t, at):
                jobs.wait_full(act, at, ("q", t))
                for r in range(4):
                    rows = slice(DP * r, DP * (r + 1))
                    cp = act.copy(q_diag[rows, t % 2, r // 2, :, r % 2, :],
                                  jobs.bank(at, ("q", t))[rows, :].rearrange("p (s l) -> p s l", l=L))
                cp.then_inc(jobs.free_of(at, ("q", t)), 1)

            def take_v(at, p):
                job = ("v", p)
                jobs.wait_full(act, at, job)
                for b in range(2):
                    rows = slice(L * b, L * (b + 1))
                    cp = act.copy(va[rows, p, :, b, 0:2 * D],
                                  jobs.bank(at, job)[rows, 0:C].rearrange("p (i d) -> p i d", d=2 * D))
                cp.then_inc(jobs.free_of(at, job), 1)

            def exponential(g, t):
                n = turn(g, t)
                act.wait_ge(less_max, n + 2)
                act.activation(prob[:, t % 2], prob[:, t % 2], ACT.Exp, scale=SCALE).then_inc(exp_done, 1)

            def take_prob_t(g, t):
                for i in range(2):
                    job = ("pt", t, i)
                    jobs.wait_full(act, g, job)
                    act.copy(prob_t[:, i, :], jobs.bank(g, job)[:]).then_inc(jobs.free_of(g, job), 1)

            def repeat_rest(g):
                jobs.wait_taken(act, g, ("o", T - 1, 1))
                act.copy(o[:, :, C:CD].rearrange("p g (r c) -> p g r c", r=2),
                         o[:, :, 2 * P:C].unsqueeze(2).to_broadcast([P, GP, 2, CR])).then_inc(o_ready, 1)

            def o_high(g):
                for t in range(3):
                    jobs.wait_full(act, g, ("ot", t))
                    out = o_t.hi[:, t, :] if t < 2 else o_t.rest[0:3 * CR, :]
                    act.copy(out, jobs.bank(g, ("ot", t))[0:rows_of(t), :]).then_inc(o_hi, 1)

            norm.high(act, (0, ATTENTION))
            take_q(0, -1)
            act.wait_ge(v_begun, 2)
            for p in range(GP):
                take_v(-1, p)
            exponential(0, 0)
            take_q(1, -1)
            act.wait_ge(st.rotation_kept, 32)

            def body(g):
                ahead = not is_last(g)
                take_prob_t(g, 0)
                take_q(2, g)
                exponential(g, 1)
                elim.act(act, step_of(g, 0))
                take_prob_t(g, 1)
                take_q(3, g)
                exponential(g, 2)
                elim.act(act, step_of(g, 1))
                jobs.wait_full(act, g, ("k", 3))
                norm.high(act, following(g))
                take_prob_t(g, 2)
                exponential(g, 3)
                if ahead:
                    elim.act(act, step_of(g, 2))
                    take_q(0, g)
                take_prob_t(g, 3)
                elim.act(act, step_of(g, 3))
                if ahead:
                    take_v(g, 0)
                    exponential(g + 1, 0)
                    take_v(g, 1)
                repeat_rest(g)
                if ahead:
                    take_v(g, 2)
                    take_v(g, 3)
                o_high(g)
                if ahead:
                    take_q(1, g)
                elim.act(act, step_of(g, 4))
            for_groups(act, body)

        @block.vector
        def _(dve):
            jobs.open(dve)
            dve.sem_inc(less_max, 1)
            dve.sem_inc(added, 1)
            norm.scale_up(dve, (0, ATTENTION), -1)
            norm.shift_by(dve, (0, ATTENTION), -1)
            norm.low(dve, (0, ATTENTION))

            def softmax_max(g, t):
                n = turn(g, t)
                s = scores[:].rearrange("p i (s m) -> p i s m", m=L)
                dve.wait_ge(scored, n + 1)
                dve.tensor_reduce(row_max[:, t % 2], s, AX_X, ALU.max).then_inc(max_done, 1)
                dve.wait_ge(max_done, n + 1)
                dve.tensor_tensor(prob[:, t % 2].rearrange("p i (s m) -> p i s m", m=L), s,
                                  row_max[:, t % 2].unsqueeze(3).to_broadcast([P, 2, GB, L]), ALU.subtract
                                  ).then_inc(less_max, 1)

            def take_k(t, at):
                jobs.wait_full(dve, at, ("k", t))
                dve.tensor_copy(k_t[:, t % 2, :], jobs.bank(at, ("k", t))[:]).then_inc(jobs.free_of(at, ("k", t)), 1)

            def take_o(g, t):
                for i in range(2):
                    job = ("o", t, i)
                    jobs.wait_full(dve, g, job)
                    src = jobs.bank(g, job)[:, 0:GP * 2 * VW].rearrange("p (g b d) -> p g b d", b=2, d=VW)
                    dve.reciprocal(rsum[:, i], src[:, :, :, 2 * D]).then_inc(inverted, 1)
                    dve.wait_ge(inverted, turn(g, t) * 2 + i + 1)
                    for w in range(2):
                        rows = slice(L * w, L * (w + 1))
                        h = 4 * t + 2 * i + w
                        for b in range(2):
                            tt = dve.tensor_tensor(o[L * b:L * (b + 1), :, h * D:(h + 1) * D],
                                                   src[rows, :, b, w * D:(w + 1) * D],
                                                   rsum[rows, i, :, b:b + 1].to_broadcast([L, GP, D]), ALU.mult)
                    tt.then_inc(jobs.free_of(g, job), 1)

            def o_low(g):
                for t in range(3):
                    bank = jobs.bank(g, ("ot", t))
                    dve.wait_ge(o_hi, g * 3 + t + 1)
                    r = slice(0, P) if t < 2 else slice(2 * CR, 3 * CR)
                    out, hi = (o_t.lo[:, t, :], o_t.hi[:, t, :]) if t < 2 else (o_t.rest[r, :], o_t.rest[r, :])
                    dve.tensor_tensor(out, bank[r, :], hi.bitcast(F32), ALU.subtract
                                      ).then_inc(jobs.free_of(g, ("ot", t)), 1)

            def residual(g, p):
                n = g * GP + p
                job = ("proj", p)
                xg = st.x[:, bass.ds(n, 1), :].rearrange("p q c -> p (q c)")
                jobs.wait_full(dve, g, job)
                if p == 0:
                    dve.wait_ge(gate_in, 32 * (g + 1))
                dve.tensor_tensor(gated[:, p % 2, :], jobs.bank(g, job)[:, 0:C], gate[:, p, :], ALU.mult
                                  ).then_inc(jobs.free_of(g, job), 1)
                jobs.wait_taken(dve, g, job)
                dve.tensor_tensor(xg, xg, gated[:, p % 2, :], ALU.add).then_inc(added, 1)

            take_k(0, -1)
            softmax_max(0, 0)
            take_k(1, -1)

            def body(g):
                ahead = not is_last(g)
                norm.statistics(dve, following(g))
                softmax_max(g, 1)
                norm.normalize(dve, following(g))
                take_k(2, g)
                take_o(g, 0)
                norm.scale_up(dve, following(g), g)
                softmax_max(g, 2)
                norm.shift_by(dve, following(g), g)
                take_k(3, g)
                take_o(g, 1)
                norm.low(dve, following(g))
                softmax_max(g, 3)
                take_o(g, 2)
                if ahead:
                    take_k(0, g)
                    softmax_max(g + 1, 0)
                take_o(g, 3)
                o_low(g)
                if ahead:
                    take_k(1, g)
                for p in range(GP):
                    residual(g, p)
            for_groups(dve, body)

        @block.tensor
        def _(pe):
            def project_qk(job, at):
                jobs.wait_free(pe, at, job)
                c = ("qk".index(job[0]) * T + job[1]) * P
                product(pe, jobs.bank(at, job)[:], acts, slice(0, TG), (st.wqk_hi, st.wqk_lo, st.wqk_r),
                        slice(c, c + P), True).then_inc(jobs.full_of(at, job), 1)

            def project_v(g, at):
                for p in range(GP):
                    job = ("v", p)
                    jobs.wait_free(pe, at, job)
                    product(pe, jobs.bank(at, job)[:, 0:C], acts, slice(p * P, (p + 1) * P),
                            (st.wv_hi, st.wv_lo, st.wv_r), slice(0, C), False).then_inc(jobs.full_of(at, job), 1)

            def score(g, t, at):
                jobs.wait_taken(pe, at, ("q", t))
                jobs.wait_taken(pe, at, ("k", t))
                pe.wait_ge(less_max, turn(g, t) + 1)
                for i in range(2):
                    for s in range(GB):
                        tok = slice(s * L, (s + 1) * L)
                        mm = pe.matmul(scores[:, i, tok], q_diag[:, t % 2, i, s, :, :], k_t[:, t % 2, tok],
                                       start=True, stop=True)
                mm.then_inc(scored, 1)

            def transpose_prob(g, t):
                pe.wait_ge(exp_done, turn(g, t) + 1)
                for i in range(2):
                    job = ("pt", t, i)
                    jobs.wait_free(pe, g, job)
                    for p in range(GP):
                        mm = pe.transpose(jobs.bank(g, job)[:, p * P:(p + 1) * P],
                                          prob[:, t % 2, i, p * P:(p + 1) * P], st.ident[:])
                    mm.then_inc(jobs.full_of(g, job), 1)

            def weigh_v(g, t):
                if t == 0:
                    jobs.wait_taken(pe, g - 1, ("v", GP - 1))
                for i in range(2):
                    job = ("o", t, i)
                    jobs.wait_taken(pe, g, ("pt", t, i))
                    jobs.wait_free(pe, g, job)
                    for p in range(GP):
                        mm = pe.matmul(jobs.bank(g, job)[:, p * 2 * VW:(p + 1) * 2 * VW],
                                       prob_t[:, i, p * P:(p + 1) * P], va[:, p, 2 * t + i, :, :],
                                       start=True, stop=True)
                    mm.then_inc(jobs.full_of(g, job), 1)

            def transpose_o(g):
                pe.wait_ge(o_ready, g + 1)
                for t in range(3):
                    jobs.wait_free(pe, g, ("ot", t))
                    for p in range(GP):
                        mm = pe.transpose(jobs.bank(g, ("ot", t))[0:rows_of(t), p * P:(p + 1) * P],
                                          o[:, p, t * P:t * P + rows_of(t)], st.ident[:])
                    mm.then_inc(jobs.full_of(g, ("ot", t)), 1)

            def project(g):
                for t in range(3):
                    jobs.wait_taken(pe, g, ("ot", t))
                for p in range(GP):
                    job = ("proj", p)
                    jobs.wait_free(pe, g, job)
                    product(pe, jobs.bank(g, job)[:, 0:C], o_t, slice(p * P, (p + 1) * P),
                            (st.wp_hi, st.wp_lo, st.wp_r), slice(0, C), False).then_inc(jobs.full_of(g, job), 1)

            norm.transposes(pe, (0, ATTENTION), -1)
            pe.wait_ge(begun, 2)
            norm.wait_acts(pe, (0, ATTENTION))
            project_qk(("q", 0), -1)
            project_qk(("k", 0), -1)
            score(0, 0, -1)
            project_v(0, -1)
            project_qk(("q", 1), -1)
            project_qk(("k", 1), -1)

            def body(g):
                ahead = not is_last(g)
                score(g, 1, g - 1)
                project_qk(("q", 2), g)
                transpose_prob(g, 0)
                project_qk(("k", 2), g)
                elim.pe(pe, step_of(g, 0))
                weigh_v(g, 0)
                norm.transposes(pe, following(g), g)
                score(g, 2, g)
                project_qk(("q", 3), g)
                transpose_prob(g, 1)
                project_qk(("k", 3), g)
                elim.pe(pe, step_of(g, 1))
                weigh_v(g, 1)
                score(g, 3, g)
                transpose_prob(g, 2)
                if ahead:
                    norm.wait_acts(pe, (g + 1, ATTENTION))
                    project_qk(("q", 0), g)
                    elim.pe(pe, step_of(g, 2))
                weigh_v(g, 2)
                if ahead:
                    project_qk(("k", 0), g)
                transpose_prob(g, 3)
                if ahead:
                    score(g + 1, 0, g)
                elim.pe(pe, step_of(g, 3))
                weigh_v(g, 3)
                if ahead:
                    project_v(g + 1, g)
                transpose_o(g)
                if ahead:
                    project_qk(("q", 1), g)
                    project_qk(("k", 1), g)
                elim.pe(pe, step_of(g, 4))
                project(g)
            for_groups(pe, body, 1)


def mlp(nc, st, io, elim):
    with ExitStack() as ctx:
        m = Memory(nc, ctx)
        ln = [("ln", t) for t in range(3)]
        jobs = Jobs(m, "mlp", m.banks("mlp_ps", 7), [("fc1", f) for f in range(FT)] + ln + [("fc2", p) for p in range(GP)], ln, done_before=ln)
        elim.use(m.banks("elim2_ps", 1)[0])
        norm, acts = st.norm, st.norm.acts
        norm.use(jobs)
        NG = 3
        g32 = m.sb("g32", [P, NG, TG])
        g_hi, g_lo = m.sb("g_hi", [P, FT, TG], F32R), m.sb("g_lo", [P, FT, TG], F32R)
        gated = m.sb("gated2", [P, 2, C])
        gate = m.sb("gate2", [P, GP, C])
        gate_in, added = m.sem("gate2_in"), m.sem("added2")
        g_lo_done = m.sem("g_lo_done")

        def step_of(g, i):
            return ELIM_ATT * GROUPS - 1 + g * ELIM_MLP + i

        def places(g):
            return {1: 0, 6: 1} if is_last(g) else {1: 0}


        block = ctx.enter_context(nc.Block())

        @block.sync
        def _(sp):
            rotation_moves(sp, st.rotation[:], io, st.rotation_in, to_dram=False)
            gate_loads(sp, nc, io, 1, gate, gate_in, added)

        @block.gpsimd
        def _(pool):
            def body(g):
                for i in range(len(places(g)) + 2):
                    if i == 1 and not is_last(g):
                        norm.root(pool, (g + 1, MLP))
                    elim.pool(pool, step_of(g, i))
            for_groups(pool, body)

        @block.scalar
        def _(act):
            def body(g):
                for f in range(FT):
                    job = ("fc1", f)
                    bank = jobs.bank(g, job)
                    jobs.wait_full(act, g, job)
                    act.wait_ge(g_lo_done, g * FT + f + 1)
                    act.activation(g32[:, f % NG, :], bank[:], ACT.Gelu_apprx_tanh)
                    act.activation(g_hi[:, f, :], bank[:], ACT.Gelu_apprx_tanh
                                   ).then_inc(jobs.free_of(g, job), 1)
                    if f in places(g):
                        elim.act(act, step_of(g, places(g)[f]))
                elim.act(act, step_of(g, len(places(g))))
                if not is_last(g):
                    norm.high(act, (g + 1, MLP))
                elim.act(act, step_of(g, len(places(g)) + 1))
            for_groups(act, body)

        @block.vector
        def _(dve):
            jobs.open(dve)
            dve.sem_inc(added, 1)
            dve.sem_inc(g_lo_done, NG)

            def low(g, f):
                jobs.wait_taken(dve, g, ("fc1", f))
                dve.tensor_tensor(g_lo[:, f, :], g32[:, f % NG, :], g_hi[:, f, :].bitcast(F32), ALU.subtract
                                  ).then_inc(g_lo_done, 1)

            def residual(g, p):
                n = g * GP + p
                job = ("fc2", p)
                xg = st.x[:, bass.ds(n, 1), :].rearrange("p q c -> p (q c)")
                jobs.wait_full(dve, g, job)
                if p == 0:
                    dve.wait_ge(gate_in, 32 * (g + 1))
                dve.tensor_tensor(gated[:, p % 2, :], jobs.bank(g, job)[:, 0:C], gate[:, p, :], ALU.mult
                                  ).then_inc(jobs.free_of(g, job), 1)
                jobs.wait_taken(dve, g, job)
                dve.tensor_tensor(xg, xg, gated[:, p % 2, :], ALU.add).then_inc(added, 1)

            def body(g):
                ahead = not is_last(g)
                for f in range(FT):
                    low(g, f)
                    if f == 1 and ahead:
                        norm.statistics(dve, (g + 1, MLP))
                    if f == 5 and ahead:
                        norm.normalize(dve, (g + 1, MLP))
                if ahead:
                    norm.scale_up(dve, (g + 1, MLP), g)
                    norm.shift_by(dve, (g + 1, MLP), g)
                for p in range(GP):
                    if p == 1 and ahead:
                        norm.low(dve, (g + 1, MLP))
                    residual(g, p)
            for_groups(dve, body)

        @block.tensor
        def _(pe):
            def down(g, p):
                job, tok = ("fc2", p), slice(p * P, (p + 1) * P)
                jobs.wait_free(pe, g, job)
                if p == 0:
                    pe.wait_ge(g_lo_done, (g + 1) * FT + NG)
                out = jobs.bank(g, job)[:, 0:C]
                pe.matmul(out, st.ones2[:], st.b2[:], start=True, stop=False)
                for f in range(FT):
                    pe.matmul(out, g_hi[:, f, tok], st.w2_hi[:, f, :], start=False, stop=False)
                    pe.matmul(out, g_hi[:, f, tok], st.w2_lo[:, f, :], start=False, stop=False)
                    mm = pe.matmul(out, g_lo[:, f, tok], st.w2_hi[:, f, :], start=False, stop=(f == FT - 1))
                mm.then_inc(jobs.full_of(g, job), 1)

            def body(g):
                norm.wait_acts(pe, (g, MLP))
                for f in range(FT):
                    job = ("fc1", f)
                    jobs.wait_free(pe, g, job)
                    product(pe, jobs.bank(g, job)[:], acts, slice(0, TG), (st.w1_hi, st.w1_lo, st.w1_r),
                            slice(f * P, (f + 1) * P), True).then_inc(jobs.full_of(g, job), 1)
                    if f in places(g):
                        elim.pe(pe, step_of(g, places(g)[f]))
                if not is_last(g):
                    norm.transposes(pe, (g + 1, MLP), g)
                if not is_last(g):
                    elim.pe(pe, step_of(g, len(places(g))))
                for p in range(GP):
                    down(g, p)
                    if p == 0 and is_last(g):
                        elim.pe(pe, step_of(g, len(places(g))))
                    if p == 2:
                        elim.pe(pe, step_of(g, len(places(g)) + 1))
            for_groups(pe, body)


def rotate(nc, st, io):
    with ExitStack() as ctx:
        m = Memory(nc, ctx)
        xs, dz, out = [("x", t) for t in range(3)], [("dz", 0), ("dz", 1)], [("out", p) for p in range(GP)]
        ps = m.banks("rot_ps", 8)
        jobs = Jobs(m, "rot", ps, xs + dz + [("z",)] + out, xs + [("z",)])
        prod = m.sb("diag_prod", [P, RK])
        pivots = m.sb("pivots", [P, 1])
        sign = m.sb("sign", [RK, 1])
        scale = m.sb("scale", [RK, 1])
        t_scaled = m.sb("t_scaled", [RK, RK])
        t_tr = m.sb("t_tr", [RK, RK])
        u = m.sb("u", [P, 3, 2 * RK])
        u_t = m.sb("u_t", [RK, C])
        x_s = m.sb("x_s", [P, GP, C])
        e_s = m.sb("e_s", [P, GP, 2, RK])
        x_t = m.sb("x_t", [P, 3, TG])
        z_t = m.sb("z_t", [P, TG])
        dz_t = m.sb("dz_t", [RK, TG])
        copied, e_copied, done, stored = m.sem("x_copied"), m.sem("e_copied"), m.sem("rot_done"), m.sem("stored")
        basis_step, pivots_done = m.sem("basis_step"), m.sem("pivots_done")
        root_done, t_turned, u_done, u_copied = m.sem("root_done"), m.sem("t_turned"), m.sem("u_done"), m.sem("u_copied")
        block = ctx.enter_context(nc.Block())

        def rows_of(t):
            return P if t < 2 else CR

        @block.gpsimd
        def _(pool):
            pool.wait_ge(pivots_done, 1)
            pool.tensor_tensor(scale[:], pivots[0:RK, :], st.minus_half[0:RK, 0:1], ALU.pow).then_inc(root_done, 1)

        @block.sync
        def _(sp):
            dst = io["out"].rearrange("(q b) l c -> (b l) q c", b=2)
            with sp.Fori(0, GROUPS) as g:
                sp.wait_ge(done, g + 1)
                sp.dma_start(dst[:, bass.ds(g * GP, GP), :], st.x[:, bass.ds(g * GP, GP), :]).then_inc(stored, 16)
            sp.wait_ge(stored, 16 * GROUPS)

        @block.scalar
        def _(act):
            def stage_x(g):
                act.copy(x_s[:], st.x[:, bass.ds(g * GP, GP), :]).then_inc(copied, 1)

            def stage_e(g):
                act.copy(e_s[:], st.rotation[:, bass.ds(g * GP, GP), :].unsqueeze(2).to_broadcast([P, GP, 2, RK])
                         ).then_inc(e_copied, 1)

            def take_x(at):
                for t in (0, 2):
                    jobs.wait_full(act, at, ("x", t))
                    act.copy(x_t[0:rows_of(t), t, :], jobs.bank(at, ("x", t))[0:rows_of(t), :]
                             ).then_inc(jobs.free_of(at, ("x", t)), 1)

            stage_x(0)
            take_x(-1)
            act.wait_ge(st.rotation_in, 32)
            stage_e(0)

            def body(g):
                if not is_last(g):
                    stage_x(g + 1)
                    take_x(g)
                    jobs.wait_full(act, g, ("dz", 1))
                    stage_e(g + 1)
            for_groups(act, body)

        @block.vector
        def _(dve):
            def take_x(at):
                jobs.wait_full(dve, at, ("x", 1))
                dve.tensor_copy(x_t[:, 1, :], jobs.bank(at, ("x", 1))[:]).then_inc(jobs.free_of(at, ("x", 1)), 1)

            def take_z(at):
                jobs.wait_full(dve, at, ("z",))
                dve.tensor_copy(z_t[:], jobs.bank(at, ("z",))[:]).then_inc(jobs.free_of(at, ("z",)), 1)

            jobs.open(dve)
            dve.tensor_tensor(prod[:], st.elim[:, 0:RK], st.ident2[:], ALU.mult).then_inc(basis_step, 1)
            dve.wait_ge(basis_step, 1)
            dve.reduce_sum(pivots[:], prod[:], AX_X).then_inc(pivots_done, 1)
            dve.wait_ge(pivots_done, 1)
            dve.tensor_scalar(sign[:], pivots[RK:P, :], 0.0, -2.0, ALU.is_ge, ALU.mult).then_inc(basis_step, 1)
            dve.wait_ge(root_done, 1)
            dve.wait_ge(basis_step, 2)
            dve.tensor_scalar(scale[:], sign[:], 1.0, scale[:], ALU.add, ALU.mult).then_inc(basis_step, 1)
            dve.wait_ge(basis_step, 3)
            dve.tensor_scalar(t_scaled[:], st.elim[0:RK, RK:P], scale[:], None, ALU.mult).then_inc(basis_step, 1)
            take_x(-1)
            dve.wait_ge(t_turned, 1)
            dve.tensor_copy(t_tr[:], ps[7][0:RK, 0:RK]).then_inc(basis_step, 1)
            dve.wait_ge(u_done, 1)
            for t in range(3):
                dve.tensor_copy(u[0:rows_of(t), t, :].rearrange("p (w k) -> p w k", w=2),
                                ps[4 + t][0:rows_of(t), 0:RK].unsqueeze(1).to_broadcast([rows_of(t), 2, RK])
                                ).then_inc(u_copied, 1)
            dve.tensor_copy(u_t[:], ps[7][0:RK, 0:C]).then_inc(u_copied, 1)
            take_z(-1)

            def body(g):
                if not is_last(g):
                    take_x(g)
                for b in range(2):
                    jobs.wait_full(dve, g, ("dz", b))
                    dve.tensor_copy(dz_t[:].rearrange("k (q b l) -> k q b l", b=2, l=L)[:, :, b, :],
                                    jobs.bank(g, ("dz", b))[0:RK, 0:GP * L].rearrange("k (q l) -> k q l", l=L)
                                    ).then_inc(jobs.free_of(g, ("dz", b)), 1)
                if not is_last(g):
                    take_z(g)
                for p in range(GP):
                    job = ("out", p)
                    xg = st.x[:, bass.ds(g * GP + p, 1), :].rearrange("p q c -> p (q c)")
                    jobs.wait_full(dve, g, job)
                    dve.tensor_tensor(xg, xg, jobs.bank(g, job)[:, 0:C], ALU.add).then_inc(jobs.free_of(g, job), 1)
                jobs.wait_taken(dve, g, ("out", GP - 1))
                dve.sem_inc(done, 1)
            for_groups(dve, body)

        @block.tensor
        def _(pe):
            def transpose_x(g, at):
                pe.wait_ge(copied, g + 1)
                for t in range(3):
                    jobs.wait_free(pe, at, ("x", t))
                    for p in range(GP):
                        mm = pe.transpose(jobs.bank(at, ("x", t))[0:rows_of(t), p * P:(p + 1) * P],
                                          x_s[:, p, t * P:t * P + rows_of(t)], st.ident[:])
                    mm.then_inc(jobs.full_of(at, ("x", t)), 1)

            def into_subspace(at):
                jobs.wait_free(pe, at, ("z",))
                for t in range(3):
                    jobs.wait_taken(pe, at, ("x", t))
                    mm = pe.matmul(jobs.bank(at, ("z",))[:], u[0:rows_of(t), t, :], x_t[0:rows_of(t), t, :],
                                   start=(t == 0), stop=(t == 2))
                mm.then_inc(jobs.full_of(at, ("z",)), 1)

            def rotation(g):
                jobs.wait_taken(pe, g - 1, ("z",))
                pe.wait_ge(e_copied, g + 1)
                for b in range(2):
                    rows = slice(L * b, L * (b + 1))
                    jobs.wait_free(pe, g, ("dz", b))
                    for p in range(GP):
                        tok = slice(p * P + L * b, p * P + L * (b + 1))
                        n = 2 if p == 0 else 1
                        out = jobs.bank(g, ("dz", b))[0:n * RK, p * L:(p + 1) * L]
                        held = e_s[rows, p, 0:n, :]
                        mm = pe.matmul(out, held, z_t[rows, tok], start=True, stop=True)
                    mm.then_inc(jobs.full_of(g, ("dz", b)), 1)

            def out_of_subspace(g):
                for b in range(2):
                    jobs.wait_taken(pe, g, ("dz", b))
                for p in range(GP):
                    job = ("out", p)
                    jobs.wait_free(pe, g, job)
                    pe.matmul(jobs.bank(g, job)[:, 0:C], dz_t[:, p * P:(p + 1) * P], u_t[:], start=True, stop=True
                              ).then_inc(jobs.full_of(g, job), 1)

            transpose_x(0, -1)
            pe.wait_ge(basis_step, 4)
            pe.transpose(ps[7][0:RK, 0:RK], t_scaled[:], st.ident[0:RK, 0:RK]).then_inc(t_turned, 1)
            pe.wait_ge(basis_step, 5)
            for t in range(3):
                pe.matmul(ps[4 + t][0:rows_of(t), 0:RK], st.p_t[:, t * P:t * P + rows_of(t)], t_tr[:], start=True, stop=True)
            pe.matmul(ps[7][0:RK, 0:C], t_tr[:], st.p_t[:], start=True, stop=True).then_inc(u_done, 1)
            pe.wait_ge(u_copied, 4)
            into_subspace(-1)

            def body(g):
                if not is_last(g):
                    transpose_x(g + 1, g)
                rotation(g)
                if not is_last(g):
                    into_subspace(g)
                out_of_subspace(g)
            for_groups(pe, body, 1)


class State:
    pass


def state(nc, ctx):
    m, st = Memory(nc, ctx), State()
    st.x = m.sb("x", [P, PAIRS, C])
    st.ident = m.sb("ident", [P, P])
    st.ident2 = m.sb("ident2", [P, RK])
    st.below = m.sb("below", [P, RK])
    st.half1, st.half2 = m.sb("half1", [P, 1]), m.sb("half2", [P, 1])
    st.ones_top, st.ones_low = m.sb("ones_top", [P, P]), m.sb("ones_low", [P, P])
    st.elim = m.sb("elim", [P, P])
    st.p_t = m.sb("p_t", [RK, C])
    st.lowrow = m.sb("lowrow", [P, 2])
    st.sel2 = m.sb("sel2", [2, 2])
    st.ones = m.sb("ones", [P, 1])
    st.minus_half = m.sb("minus_half", [P, GP])
    st.powers = m.sb("powers", [P, 2])
    st.mod_t = m.sb("mod_t", [P, 4, 3, B])
    return st


def weight_state(nc, ctx, st):
    m = Memory(nc, ctx)
    st.wqk_hi, st.wqk_lo = m.sb("wqk_hi", [P, 2, 2 * H * DP], F32R), m.sb("wqk_lo", [P, 2, 2 * H * DP], F32R)
    st.wqk_r = m.sb("wqk_r", [KR, 2 * H * DP], F32R)
    st.wv_hi, st.wv_lo, st.wv_r = m.sb("wv_hi", [P, 2, C], F32R), m.sb("wv_lo", [P, 2, C], F32R), m.sb("wv_r", [KR, C], F32R)
    st.wp_hi, st.wp_lo, st.wp_r = m.sb("wp_hi", [P, 2, C], F32R), m.sb("wp_lo", [P, 2, C], F32R), m.sb("wp_r", [KR, C], F32R)
    st.w1_hi, st.w1_lo, st.w1_r = m.sb("w1_hi", [P, 2, FF], F32R), m.sb("w1_lo", [P, 2, FF], F32R), m.sb("w1_r", [KR, FF], F32R)
    st.w2_hi, st.w2_lo = m.sb("w2_hi", [P, FT, C], F32R), m.sb("w2_lo", [P, FT, C], F32R)
    st.b2, st.ones2 = m.sb("b2", [P, C], F32R), m.sb("ones2", [P, P], F32R)


def attention_state(nc, ctx, st):
    m = Memory(nc, ctx)
    st.q_diag = m.sb("q_diag", [P, 2, 2, GB, 2, L])
    st.rotation_kept = m.sem("rotation_kept")


def program(nc, io):
    io["gates"] = nc.dram_tensor("gates", (B, 2, C), F32, kind="Internal").ap()
    io["skew"] = nc.dram_tensor("skew_dram", (B, RK, RK), F32, kind="Internal").ap()
    with ExitStack() as ctx:
        st = state(nc, ctx)
        weight_state(nc, ctx, st)
        setup(nc, Memory(nc, ctx), st, io)
        with ExitStack() as inner:
            elim = Elimination(Memory(nc, inner), st)
            st.norm = Norm(Memory(nc, inner), st)
            with ExitStack() as att:
                attention_state(nc, att, st)
                rotations(nc, st, io)
                attention(nc, st, io, elim)
            st.rotation = Memory(nc, inner).sb("rotation", [P, PAIRS, RK])
            st.rotation_in = Memory(nc, inner).sem("rotation_in")
            mlp(nc, st, io, elim)
            rotate(nc, st, io)


_INS = ["x", "cond_1152", "L0_cond_W_qkv", "L0_cond_b_qkv", "L0_cond_W_proj", "L0_cond_b_proj", "L0_cond_W_fc1",
        "L0_cond_b_fc1", "L0_cond_W_fc2", "L0_cond_b_fc2", "L0_cond_W_ada", "L0_cond_b_ada", "L1_cond_P",
        "L1_cond_W", "L1_cond_b"]


def kernel(**inputs):
    import numpy as _np
    import concourse.bacc as _bacc
    from concourse import mybir as _mybir
    from concourse.bass_utils import run_bass_kernel_spmd as _run

    nc = _bacc.Bacc("TRN2", target_bir_lowering=False, num_devices=1)
    arrays, io = {}, {}
    for name in _INS:
        a = _np.ascontiguousarray(inputs[name])
        arrays[f"in_{name}_dram"] = a
        io[name] = nc.dram_tensor(f"in_{name}_dram", a.shape, _mybir.dt.from_np(a.dtype), kind="ExternalInput").ap()
    io["out"] = nc.dram_tensor("out_0_dram", (64, 64, 288), _mybir.dt.float32, kind="ExternalOutput").ap()
    program(nc, io)
    r = _run(nc, [arrays], core_ids=[0])
    return r.results[0]["out_0_dram"]
```
